# Optimizing a Trainium2 kernel written in Bass

```python
import numpy as np
import jax
import jax.numpy as jnp

def _softmax(x, axis=-1):
    return jax.nn.softmax(x, axis=axis)

def _gelu(x):
    return jax.nn.gelu(x, approximate=True)

def _silu(x):
    return jax.nn.silu(x)

def _sigmoid(x):
    return jax.nn.sigmoid(x)

def _layernorm(x, axis=-1, eps=1e-05):
    m = jnp.mean(x, axis=axis, keepdims=True)
    v = jnp.var(x, axis=axis, keepdims=True)
    return (x - m) / jnp.sqrt(v + eps)

def _scatter_add(tgt, idx, src, axis=0):
    return tgt.at[idx].add(src)

def _segment_sum(src, seg, n):
    return jax.ops.segment_sum(src, seg, n)
kernel_name = 'mk_hybrid_d1_jaxref_r8_c53c1b'

def setup_inputs(seed: int=0):
    np.random.seed(seed)
    _w = jnp.asarray

    def _L0_attn_a_setup():
        import jax, jax.numpy as jnp
        import numpy as np
        EMBED = 128
        HEADS = 16
        HEAD_DIM = EMBED // HEADS
        key = jax.random.key(seed)
        k1, k2, k3, k4, k5 = jax.random.split(key, 5)
        B, S = (2, 256)
        scale = 1.0 / np.sqrt(EMBED)
        return {'input_tensor': jax.random.normal(k1, (B, S, EMBED), dtype=jnp.float32), 'qkv_weight': jax.random.normal(k2, (3 * EMBED, EMBED), dtype=jnp.float32) * scale, 'qkv_bias': jax.random.normal(k3, (3 * EMBED,), dtype=jnp.float32) * 0.02, 'out_weight': jax.random.normal(k4, (EMBED, EMBED), dtype=jnp.float32) * scale, 'out_bias': jax.random.normal(k5, (EMBED,), dtype=jnp.float32) * 0.02}
    _L0_attn_a_in = _L0_attn_a_setup()

    def _L0_attn_b_setup():
        import jax, jax.numpy as jnp
        import numpy as np
        D = 128
        H = 16
        DH = D // H
        B, N = (4, 128)
        key = jax.random.key(seed)
        k0, k1, k2 = jax.random.split(key, 3)
        x = jax.random.normal(k0, (B, N, D), jnp.float32)
        Wkqv = jax.random.normal(k1, (H, D, 2 * D + DH), jnp.float32) * 0.02
        bkqv = jnp.zeros((H, 2 * D + DH), jnp.float32)
        Wp = jax.random.normal(k2, (D, D), jnp.float32) * 0.02
        bp = jnp.zeros((D,), jnp.float32)
        return {'x': x, 'Wkqv': Wkqv, 'bkqv': bkqv, 'Wp': Wp, 'bp': bp}
    _L0_attn_b_in = _L0_attn_b_setup()

    def _L0_ffn_setup():
        import jax, jax.numpy as jnp
        import numpy as np
        TOP_K = 2
        NUM_EXPERTS = 8
        B, T, H, F = (4, 256, 128, 512)
        key = jax.random.key(seed)
        ks = jax.random.split(key, 6)
        s_in = 1.0 / np.sqrt(H)
        s_ff = 1.0 / np.sqrt(F)
        return {'x': jax.random.normal(ks[0], (B, T, H), dtype=jnp.float32), 'router_w': jax.random.normal(ks[1], (NUM_EXPERTS, H), dtype=jnp.float32) * s_in, 'router_b': jax.random.normal(ks[2], (NUM_EXPERTS,), dtype=jnp.float32) * 0.01, 'gate_w': jax.random.normal(ks[3], (NUM_EXPERTS, F, H), dtype=jnp.float32) * s_in, 'up_w': jax.random.normal(ks[4], (NUM_EXPERTS, F, H), dtype=jnp.float32) * s_in, 'down_w': jax.random.normal(ks[5], (NUM_EXPERTS, H, F), dtype=jnp.float32) * s_ff}
    _L0_ffn_in = _L0_ffn_setup()
    _d = {'L0_attn_a_input_tensor': _L0_attn_a_in['input_tensor'], 'L0_attn_a_qkv_weight': _L0_attn_a_in['qkv_weight'], 'L0_attn_a_qkv_bias': _L0_attn_a_in['qkv_bias'], 'L0_attn_a_out_weight': _L0_attn_a_in['out_weight'], 'L0_attn_a_out_bias': _L0_attn_a_in['out_bias'], 'L0_attn_b_Wkqv': _L0_attn_b_in['Wkqv'], 'L0_attn_b_bkqv': _L0_attn_b_in['bkqv'], 'L0_attn_b_Wp': _L0_attn_b_in['Wp'], 'L0_attn_b_bp': _L0_attn_b_in['bp'], 'L0_ffn_router_w': _L0_ffn_in['router_w'], 'L0_ffn_router_b': _L0_ffn_in['router_b'], 'L0_ffn_gate_w': _L0_ffn_in['gate_w'], 'L0_ffn_up_w': _L0_ffn_in['up_w'], 'L0_ffn_down_w': _L0_ffn_in['down_w']}
    _x0 = _d['L0_attn_a_input_tensor']
    _d['L0_attn_a_input_tensor'] = jax.random.normal(jax.random.fold_in(jax.random.key(seed), 1), (8, 256, 128), dtype=_x0.dtype)
    del _x0
    return _d

def reference(L0_attn_a_input_tensor, L0_attn_a_qkv_weight, L0_attn_a_qkv_bias, L0_attn_a_out_weight, L0_attn_a_out_bias, L0_attn_b_Wkqv, L0_attn_b_bkqv, L0_attn_b_Wp, L0_attn_b_bp, L0_ffn_router_w, L0_ffn_router_b, L0_ffn_gate_w, L0_ffn_up_w, L0_ffn_down_w):

    def _L0_attn_a_ref(input_tensor, qkv_weight, qkv_bias, out_weight, out_bias):
        import jax, jax.numpy as jnp
        import numpy as np
        EMBED = 128
        HEADS = 16
        HEAD_DIM = EMBED // HEADS
        B, S, D = input_tensor.shape
        qkv = jnp.einsum('bsd,ed->bse', input_tensor, qkv_weight) + qkv_bias
        q, k, v = jnp.split(qkv, 3, axis=-1)

        def to_heads(t):
            return t.reshape(B, S, HEADS, HEAD_DIM).transpose(0, 2, 1, 3)
        q, k, v = (to_heads(q), to_heads(k), to_heads(v))
        scores = jnp.einsum('bhqd,bhkd->bhqk', q, k) / jnp.sqrt(jnp.float32(HEAD_DIM))
        probs = jax.nn.softmax(scores, axis=-1)
        attn = jnp.einsum('bhqk,bhkd->bhqd', probs, v)
        attn = attn.transpose(0, 2, 1, 3).reshape(B, S, D)
        out = jnp.einsum('bsd,ed->bse', attn, out_weight) + out_bias
        return out

    def _L0_attn_b_ref(x, Wkqv, bkqv, Wp, bp):
        import jax, jax.numpy as jnp
        import numpy as np
        D = 128
        H = 16
        DH = D // H
        B, N = (4, 128)
        Bm, Nm, Dm = x.shape
        y = jnp.einsum('bnd,hde->bhne', x, Wkqv) + bkqv[None, :, None, :]
        k = y[..., :Dm]
        q = y[..., Dm:2 * Dm]
        v = y[..., 2 * Dm:]
        A = jnp.einsum('bhnd,bhmd->bhnm', q, k) / jnp.sqrt(jnp.float32(Dm))
        mask = jnp.tril(jnp.ones((Nm, Nm), dtype=bool))
        A = jnp.where(mask[None, None], A, -jnp.inf)
        A = jax.nn.softmax(A, axis=-1)
        sa = jnp.einsum('bhnm,bhmd->bnhd', A, v).reshape(Bm, Nm, Dm)
        return sa @ Wp + bp

    def _L0_ffn_ref(x, router_w, router_b, gate_w, up_w, down_w):
        import jax, jax.numpy as jnp
        import numpy as np
        TOP_K = 2
        NUM_EXPERTS = 8
        B, T, H, F = (4, 256, 128, 512)
        logits = jnp.einsum('bth,eh->bte', x, router_w) + router_b
        topv, topi = jax.lax.top_k(logits, TOP_K)
        gates = jax.nn.softmax(topv, axis=-1)

        def body(acc, inputs):
            e, gw, uw, dw = inputs
            w = jnp.sum(gates * (topi == e), axis=-1)
            h = jax.nn.silu(jnp.einsum('bth,fh->btf', x, gw)) * jnp.einsum('bth,fh->btf', x, uw)
            y = jnp.einsum('btf,hf->bth', h, dw)
            return (acc + y * w[..., None], None)
        init = jnp.zeros_like(x)
        xs = (jnp.arange(NUM_EXPERTS), gate_w, up_w, down_w)
        out, _ = jax.lax.scan(body, init, xs)
        return out
    x = L0_attn_a_input_tensor
    x = x + _L0_attn_a_ref(_layernorm(x, axis=-1), L0_attn_a_qkv_weight, L0_attn_a_qkv_bias, L0_attn_a_out_weight, L0_attn_a_out_bias)
    x = x + _L0_ffn_ref(_layernorm(x, axis=-1), L0_ffn_router_w, L0_ffn_router_b, L0_ffn_gate_w, L0_ffn_up_w, L0_ffn_down_w)
    x = x + _L0_attn_b_ref(_layernorm(x, axis=-1), L0_attn_b_Wkqv, L0_attn_b_bkqv, L0_attn_b_Wp, L0_attn_b_bp)
    x = x + _L0_ffn_ref(_layernorm(x, axis=-1), L0_ffn_router_w, L0_ffn_router_b, L0_ffn_gate_w, L0_ffn_up_w, L0_ffn_down_w)
    return x

_drawn_inputs = setup_inputs


def setup_inputs(seed=0):
    import zlib

    import numpy as np

    out = dict(_drawn_inputs(seed))
    spreads = {'L0_attn_b_bkqv': (0.0, 0.1), 'L0_attn_b_bp': (0.0, 0.1)}
    factors = {}
    for name, (base, spread) in spreads.items():
        noise = np.random.default_rng([zlib.crc32(name.encode()), seed]).standard_normal(out[name].shape)
        drawn = base * np.exp(spread * noise) if base else spread * noise
        out[name] = jnp.asarray(drawn.astype(out[name].dtype))
    for name, factor in factors.items():
        out[name] = (out[name] * factor).astype(out[name].dtype)
    return out
```

```python
from contextlib import ExitStack

import concourse.bass as bass
from concourse import mybir

ALU = mybir.AluOpType
ACT = mybir.ActivationFunctionType
AX_X = mybir.AxisListType.X
F32 = mybir.dt.float32
F32R = mybir.dt.float32r
BF16 = mybir.dt.bfloat16
I32 = mybir.dt.int32
U32 = mybir.dt.uint32

P = 128
BATCH, SEQ, D = 8, 256, 128
TILES = BATCH * SEQ // P
CH = SEQ // P
HEADS, DH = 16, 8
GROUPS = 4
QUAD = 32
VCOLS = 16
EXPERTS, TOPK, FF = 8, 2, 512
FCH = FF // P
SLOT_TILES = TILES * TOPK + EXPERTS
LN_EPS = 1e-5
MASKED = -1.0e30

_WIDTHS = dict(ident=P, ones=P, head=HEADS, group=GROUPS, rank=EXPERTS, full=TILES,
               upto=EXPERTS * EXPERTS, tile_no=SLOT_TILES)
CONST, _at = {}, 0
for _name, _width in _WIDTHS.items():
    CONST[_name] = (_at, _at + _width)
    _at += _width
CONST_COLS = _at


def behind(eng, sem, value):
    if isinstance(value, int) and value <= 0:
        return
    eng.wait_ge(sem, value)


def layer_norm_stats(nc, sem, x_res, mean_var, stats, rstd, work):
    moments, std_in, std_out, rstd_done = sem("moments"), sem("std_in"), sem("std_out"), sem("rstd_done")
    stats_done = sem("stats_done")
    with nc.Block() as block:

        @block.vector
        def _(dve):
            if "vector_first" in work:
                work["vector_first"](dve)
            for t in range(TILES):
                dve.bn_stats(stats[:, t, :], x_res[:, t, :]).then_inc(stats_done, 1)
            dve.wait_ge(stats_done, TILES)
            for t in range(TILES):
                dve.bn_aggr(mean_var[:, t, :], stats[:, t, :]).then_inc(moments, 1)
            dve.wait_ge(moments, TILES)
            dve.tensor_scalar(rstd, mean_var[:, :, 1], LN_EPS, None, ALU.add).then_inc(std_in, 1)
            dve.wait_ge(std_out, 1)
            dve.reciprocal(rstd, rstd).then_inc(rstd_done, 1)
            if "vector" in work:
                work["vector"](dve)

        @block.scalar
        def _(act):
            if "scalar_first" in work:
                work["scalar_first"](act)
            act.wait_ge(std_in, 1)
            act.activation(rstd, rstd, ACT.Sqrt).then_inc(std_out, 1)
            if "scalar" in work:
                work["scalar"](act)

        for name in ("sync", "gpsimd", "tensor"):
            if name in work:
                {"sync": block.sync, "gpsimd": block.gpsimd, "tensor": block.tensor}[name](work[name])


def attention(nc, kept, causal, x_res, mean_var, rstd, stats, cst, ident, ident_bf, causal_bf, weights, split_w=None):
    scale = float((D if causal else DH) ** -0.5)
    UNITS = HEADS // 2 if causal else 4
    with ExitStack() as ctx:
        tag = "c" if causal else "a"

        def sb(name, shape, dt):
            return ctx.enter_context(nc.sbuf_tensor(f"{tag}_{name}", shape, dt))

        def sem(name):
            return kept.enter_context(nc.semaphore(f"{tag}_{name}"))

        WCOLS = HEADS * P if causal else 2 * GROUPS * 3 * QUAD
        w_hi = sb("w_hi", [P, WCOLS], F32R)
        w_lo = sb("w_lo", [P, WCOLS], F32R)
        V_COLS = P + HEADS if causal else P
        wv_hi, wv_lo = sb("wv_hi", [P, V_COLS], F32R), sb("wv_lo", [P, V_COLS], F32R)
        wv, wo = sb("wv", [P, P], F32), sb("wo", [P, P], F32)
        bv, bo = sb("bv", [P, P], F32), sb("bo", [P, P], F32)
        bias = sb("bias", [P, HEADS], F32)
        if causal:
            u_bias = sb("u_bias", [P, HEADS], F32)
        loaded, hi_made = sem("loaded"), sem("hi_made")

        def load(sp):
            for dst, name in ((wv, "wv"), (wo, "wo"), (bv, "bv"), (bo, "bo")):
                sp.dma_start(dst[:, :], weights[name]).then_inc(loaded, 16)

        if causal:
            with (nc.sbuf_tensor("c_wqT", [P, HEADS, P], F32) as wqT, nc.sbuf_tensor("c_wkT", [P, HEADS, P], F32) as wkT,
                  nc.sbuf_tensor("c_bq", [P, HEADS], F32) as bq, nc.sbuf_tensor("c_bk", [P, HEADS], F32) as bk,
                  nc.sbuf_tensor("c_bqk", [P, HEADS], F32) as bqk,
                  nc.psum_tensor("c_ps_m", [P, HEADS * P], F32) as ps_m, nc.psum_tensor("c_ps_c", [P, 512], F32) as ps_c):
                bqk_made, w_made = sem("bqk_made"), sem("w_made")

                def load_all(sp):
                    load(sp)
                    for dst, name in ((wqT[:, :, :], "wqT"), (wkT[:, :, :], "wkT"), (bq[:, :], "bq"), (bk[:, :], "bk")):
                        sp.dma_start(dst, weights[name]).then_inc(loaded, 16)

                def products(pe):
                    pe.wait_ge(loaded, 8 * 16)
                    for h in range(HEADS):
                        pe.matmul(ps_m[:, h * P:(h + 1) * P], wqT[:, h, :], wkT[:, h, :], start=True, stop=True)
                    for h in range(HEADS):
                        pe.matmul(ps_c[:, h:h + 1], wkT[:, h, :], bq[:, h:h + 1], start=True, stop=True)
                        pe.matmul(ps_c[:, HEADS + h:HEADS + h + 1], wqT[:, h, :], bk[:, h:h + 1], start=True, stop=True)
                    pe.wait_ge(bqk_made, 1)
                    pe.matmul(ps_c[:, 2 * HEADS:3 * HEADS], cst("ones"), bqk[:, :], start=True, stop=True).then_inc(w_made, 1)

                def bias_products(dve):
                    dve.wait_ge(loaded, 8 * 16)
                    dve.tensor_tensor(bqk[:, :], bq[:, :], bk[:, :], ALU.mult).then_inc(bqk_made, 1)

                def hi_parts(act):
                    act.wait_ge(w_made, 1)
                    act.copy(w_hi[:, :], ps_m[:, :])
                    act.copy(wv_hi[:, P:V_COLS], ps_c[:, HEADS:2 * HEADS])
                    act.copy(wv_hi[:, 0:P], wv[:, :]).then_inc(hi_made, 1)

                def lo_parts(dve):
                    dve.wait_ge(hi_made, 1)
                    dve.tensor_tensor(w_lo[:, :], ps_m[:, :], w_hi[:, :].bitcast(F32), ALU.subtract)
                    dve.tensor_tensor(wv_lo[:, P:V_COLS], ps_c[:, HEADS:2 * HEADS], wv_hi[:, P:V_COLS].bitcast(F32), ALU.subtract)
                    dve.tensor_tensor(wv_lo[:, 0:P], wv[:, :], wv_hi[:, 0:P].bitcast(F32), ALU.subtract)
                    dve.tensor_copy(bias[:, :], ps_c[:, 0:HEADS])
                    dve.tensor_copy(u_bias[:, :], ps_c[:, 2 * HEADS:3 * HEADS])

                layer_norm_stats(nc, sem, x_res, mean_var, stats, rstd[:, :], {
                    "sync": load_all, "tensor": products, "vector_first": bias_products, "vector": lo_parts,
                    "scalar": hi_parts})
        else:
            with nc.sbuf_tensor("a_wqk", [P, WCOLS], F32) as wqk:

                def load_all(sp):
                    load(sp)
                    sp.dma_start(wqk[:, :], weights["wqk"]).then_inc(loaded, 16)
                    sp.dma_start(bias[:, 0:2 * GROUPS], weights["bqk"]).then_inc(loaded, 16)
                    gate_w, up_w, big, (gate_in, up_in, down_in), down_w = split_w
                    for w, w_in in ((gate_w, gate_in), (up_w, up_in)):
                        sp.dma_start(w[1][:, :, :].rearrange("p e f -> p (e f)").bitcast(F32), w_in).then_inc(big, 16)
                    sp.dma_start(down_w[:, :, :], down_in).then_inc(big, 16)

                def hi_parts(act):
                    act.wait_ge(loaded, 6 * 16)
                    act.copy(w_hi[:, :], wqk[:, :])
                    act.copy(wv_hi[:, 0:P], wv[:, :]).then_inc(hi_made, 1)

                def lo_parts(dve):
                    dve.wait_ge(hi_made, 1)
                    dve.tensor_tensor(w_lo[:, :], wqk[:, :], w_hi[:, :].bitcast(F32), ALU.subtract)
                    dve.tensor_tensor(wv_lo[:, 0:P], wv[:, :], wv_hi[:, 0:P].bitcast(F32), ALU.subtract)

                layer_norm_stats(nc, sem, x_res, mean_var, stats, rstd[:, :], {
                    "sync": load_all, "vector": lo_parts, "scalar": hi_parts})

        TWO = range(2)
        xn = sb("xn", [P, CH, P], F32)
        x_hi = [sb(f"x_hi{p}", [P, SEQ], F32R) for p in TWO]
        x_lo = [sb(f"x_lo{p}", [P, SEQ], F32R) for p in TWO]
        v_st = [sb(f"v_st{p}", [P, CH, HEADS, VCOLS], F32) for p in TWO]
        row_max = [sb(f"row_max{p}", [P, HEADS, CH], F32) for p in TWO]
        shift = [sb(f"shift{p}", [P, HEADS, CH], F32) for p in TWO]
        o_all = [sb(f"o_all{p}", [P, GROUPS, SEQ], F32) for p in TWO]
        r_inv = sb("r_inv", [P, HEADS], F32)
        att = sb("att", [P, HEADS, DH], F32)
        att_t = sb("att_t", [P, P], F32)
        ST_COLS = SEQ + P if causal else 2 * SEQ
        probs = sb("probs", [P, 8, ST_COLS], F32)
        if causal:
            t_hi = [sb(f"t_hi{p}", [P, HEADS, SEQ], F32R) for p in TWO]
            t_lo = [sb(f"t_lo{p}", [P, HEADS, SEQ], F32R) for p in TWO]
            neg_max = sb("neg_max", [HEADS, SEQ], F32R)
            u_row = [sb(f"u_row{p}", [P, CH, HEADS], F32) for p in TWO]
            pick = sb("pick", [HEADS, HEADS], F32R)
            m_row = sb("m_row", [P, HEADS, CH], F32)
        else:
            q_st = [sb(f"q_st{p}", [P, GROUPS, SEQ], F32R) for p in TWO]
            k_all = sb("k_all", [P, GROUPS, SEQ], F32)
            k_st = [sb(f"k_st{p}", [P, HEADS, SEQ], F32R) for p in TWO]

        def bank(name, n=1):
            return ctx.enter_context(nc.psum_tensor(f"{tag}_{name}", [P, 512 * n], F32))

        ps_s = [bank(f"ps_s{i}") for i in TWO]
        ps_st = [bank(f"ps_st{i}") for i in TWO]
        ps_o = bank("ps_o")
        ps_x = bank("ps_x")
        ps_p = [bank(f"ps_p{i}") for i in TWO]

        consts_set = sem("consts_set")
        xn_ready, xt_done, xhi_ready, xlo_ready = sem("xn_ready"), sem("xt_done"), sem("xhi_ready"), sem("xlo_ready")
        v_done, v_ready, bias_added = sem("v_done"), sem("v_ready"), sem("bias_added")
        proj_done, proj_hi, proj_lo = sem("proj_done"), sem("proj_hi"), sem("proj_lo")
        s_done, max_done, shift_ready, shift_t_done, shift_set = (
            sem("s_done"), sem("max_done"), sem("shift_ready"), sem("shift_t_done"), sem("shift_set"))
        st_done, exp_done, o_done, o_kept = sem("st_done"), sem("exp_done"), sem("o_done"), sem("o_kept")
        ot_done, rinv_done, att_done, att_t_done, att_t_kept, out_done, res_done = (
            sem("ot_done"), sem("rinv_done"), sem("att_done"), sem("att_t_done"), sem("att_t_kept"),
            sem("out_done"), sem("res_done"))
        if causal:
            m_done, cut_begun, cut_done = sem("m_done"), sem("cut_begun"), sem("cut_done")
        else:
            k_spread, split_hi, split_lo = sem("k_spread"), sem("split_hi"), sem("split_lo")
        probs_ready = cut_done if causal else exp_done
        N_CONST = 6 if causal else 9

        SLOTS = 22
        UNIT_SLOT, SPREAD_SLOT, ST_SLOT, S_SLOT, AV_SLOT = 2, 3, 3, 6, 8
        END_SLOTS = {7: (0, 0), 9: (0, 1), 11: (0, 2), 13: (1, 0), 15: (1, 1), 17: (1, 2)}
        SPLIT_SLOTS = {10: 0, 16: 1}

        def pipeline(pieces, Fori):
            def step(i, parity, head, middle, tail):
                for s in range(SLOTS):
                    if head and s == 0:
                        pieces["norm"](i, parity)
                    if middle and s == 1:
                        pieces["shift"](i - 1, 1 - parity)
                    if head and s == 1:
                        pieces["v"](i, parity)
                    if head and 0 <= s - UNIT_SLOT < UNITS:
                        pieces["project"](i, parity, s - UNIT_SLOT)
                    if middle and 0 <= s - ST_SLOT < HEADS:
                        pieces["shifted"](i - 1, 1 - parity, s - ST_SLOT)
                    if head and not causal and 0 <= s - SPREAD_SLOT < HEADS // 2:
                        for h in range(2 * (s - SPREAD_SLOT), 2 * (s - SPREAD_SLOT) + 2):
                            pieces["spread_k"](i, parity, h)
                    if head and 0 <= s - S_SLOT < HEADS:
                        pieces["scores"](i, parity, s - S_SLOT)
                    if middle and s >= AV_SLOT and (s - AV_SLOT) % 4 == 0 and (s - AV_SLOT) // 4 < GROUPS:
                        pieces["values"](i - 1, 1 - parity, (s - AV_SLOT) // 4)
                    if tail and s in END_SLOTS:
                        pieces["end"](i - 2, parity, *END_SLOTS[s], i if head else None)
                    if head and not causal and s in SPLIT_SLOTS:
                        pieces["split"](i, SPLIT_SLOTS[s])

            step(0, 0, True, False, False)
            step(1, 1, True, True, False)
            with Fori(0, BATCH // 2 - 1) as pair:
                step(2 * pair + 2, 0, True, True, True)
                step(2 * pair + 3, 1, True, True, True)
            step(BATCH, 0, False, True, True)
            step(BATCH + 1, 1, False, False, True)

        def nothing(*_):
            pass

        with nc.Block() as block:

            @block.gpsimd
            def _(pool):
                for p in TWO:
                    pool.memset(v_st[p][:, :, :, DH:DH + 1], 1.0).then_inc(consts_set, 1)
                    pool.memset(v_st[p][:, :, :, DH + 1:VCOLS], 0.0).then_inc(consts_set, 1)

                def norm(b, p):
                    pool.wait_ge(xn_ready, b + 1)
                    for c in range(CH):
                        pool.tensor_tensor(x_res[:, b * CH + c, :], x_res[:, b * CH + c, :], bo[:, :],
                                           ALU.add).then_inc(bias_added, 1)

                def spread_k(b, p, h):
                    behind(pool, st_done, HEADS * (b - 1))
                    pool.wait_ge(proj_lo, b * UNITS + h // 8 + 1)
                    mask = cst("group")[0:3 * QUAD, h % 4:h % 4 + 1].to_broadcast([3 * QUAD, SEQ])
                    pool.tensor_tensor(k_st[p][0:3 * QUAD, h, :], k_all[0:3 * QUAD, h // 4, :], mask, ALU.mult
                                       ).then_inc(k_spread, 1)

                def split(i, n):
                    pool.wait_ge(split_hi, 2 * i + n + 1)
                    hi, lo = split_w[n]
                    pool.tensor_tensor(lo[:, i, :], lo[:, i, :].bitcast(F32), hi[:, i, :].bitcast(F32),
                                       ALU.subtract).then_inc(split_lo, 1)

                def shifted(b, p, h):
                    if causal:
                        pool.wait_ge(exp_done, HEADS * b + h + 1)
                        pool.sem_inc(cut_begun, 1)
                        slot, at = (h - h % 2) % 8, (0, SEQ)[h % 2]
                        diag = probs[:, slot:slot + 2, at:at + P]
                        pool.affine_select(out=diag, in_=diag, compare_op=ALU.is_ge, fill=0.0, base=0,
                                           pattern=[[0, 2], [1, P]], channel_multiplier=-1).then_inc(cut_done, 1)

                pipeline(dict(norm=norm, v=nothing, project=nothing, spread_k=spread_k, scores=nothing, split=split,
                              shifted=shifted, values=nothing, end=nothing, shift=nothing), pool.Fori)

            @block.scalar
            def _(act):
                def norm(b, p):
                    act.wait_ge(xt_done, b + 1)
                    behind(act, st_done, HEADS * (b - 1))
                    act.copy(x_hi[p][:, :], ps_p[1][:, 0:SEQ]).then_inc(xhi_ready, 1)

                def project(b, p, u):
                    act.wait_ge(proj_done, b * UNITS + u + 1)
                    if not causal and u < 2:
                        behind(act, k_spread, HEADS * b)
                    for r in range(2):
                        src = ps_p[u % 2][:, r * SEQ:(r + 1) * SEQ]
                        if causal:
                            h = 2 * u + r
                            dst, n, col = t_hi[p][:, h, :], P, h
                        elif u < 2:
                            dst, n, col = k_all[0:3 * QUAD, 2 * u + r, :].bitcast(F32R), 3 * QUAD, GROUPS + 2 * u + r
                        else:
                            dst, n, col = q_st[p][0:3 * QUAD, 2 * (u - 2) + r, :], 3 * QUAD, 2 * (u - 2) + r
                        last = act.activation(dst, src[0:n, :], ACT.Identity, bias=bias[0:n, col:col + 1])
                    last.then_inc(proj_hi, 1)

                def shifted(b, p, h):
                    n = HEADS * b + h
                    act.wait_ge(st_done, n + 1)
                    behind(act, o_done, GROUPS * b + h // 4 - 1)
                    if causal:
                        slot, width = (h - h % 2) % 8, (SEQ, P)[h % 2]
                        at = (0, SEQ)[h % 2]
                        act.activation(probs[:, slot:slot + 2, at:at + width],
                                       ps_st[h % 2][:, 0:2 * width].rearrange("p (n q) -> p n q", q=width),
                                       ACT.Exp, scale=scale).then_inc(exp_done, 1)
                    else:
                        act.activation(probs[:, h % 8, :], ps_st[h % 2][:, 0:ST_COLS], ACT.Exp, scale=scale
                                       ).then_inc(exp_done, 1)

                def shift_(b, p):
                    if not causal:
                        act.wait_ge(shift_set, 2 * b + 1)
                        for g in range(2, GROUPS):
                            last = act.copy(q_st[p][3 * QUAD:3 * QUAD + HEADS, g, :], ps_o[0:HEADS, 0:SEQ])
                        last.then_inc(shift_set, 1)

                def split(i, n):
                    hi, lo = split_w[n]
                    act.wait_ge(split_w[2], 3 * 16)
                    act.copy(hi[:, i, :], lo[:, i, :].bitcast(F32)).then_inc(split_hi, 1)

                def values(b, p, g):
                    act.wait_ge(o_done, GROUPS * b + g + 1)
                    act.copy(o_all[p][:, g, :], ps_o[:, 0:SEQ]).then_inc(o_kept, 1)

                def end(b, p, c, part, _):
                    if part == 1:
                        act.wait_ge(att_t_done, CH * b + c + 1)
                        act.copy(att_t[:, :], ps_x[:, 0:P]).then_inc(att_t_kept, 1)

                pipeline(dict(norm=norm, v=nothing, project=project, spread_k=nothing, scores=nothing, split=split,
                              shifted=shifted, values=values, end=end, shift=shift_), act.Fori)

            @block.vector
            def _(dve):
                dve.memset(ps_o[:, :], 0.0).then_inc(consts_set, 1)
                if causal:
                    dve.tensor_copy(pick[:, :], ident[0:HEADS, 0:HEADS]).then_inc(consts_set, 1)
                else:
                    for p in TWO:
                        dve.memset(q_st[p][3 * QUAD:P, :, :].bitcast(F32), 0.0).then_inc(consts_set, 1)
                        dve.tensor_copy(k_st[p][3 * QUAD:P, :, :],
                                        cst("head")[3 * QUAD:P, :].unsqueeze(2).to_broadcast([QUAD, HEADS, SEQ])
                                        ).then_inc(consts_set, 1)

                def norm(b, p):
                    behind(dve, xt_done, b)
                    for c in range(CH):
                        t = b * CH + c
                        mean = mean_var[:, t:t + 1, 0] if isinstance(t, int) else mean_var[:, bass.ds(t, 1), 0]
                        scl = rstd[:, t:t + 1] if isinstance(t, int) else rstd[:, bass.ds(t, 1)]
                        last = dve.tensor_scalar(xn[:, c, :], x_res[:, t, :], mean, scl, ALU.subtract, ALU.mult)
                    last.then_inc(xn_ready, 1)
                    dve.wait_ge(xhi_ready, b + 1)
                    dve.tensor_tensor(x_lo[p][:, :], ps_p[1][:, 0:SEQ], x_hi[p][:, :].bitcast(F32),
                                      ALU.subtract).then_inc(xlo_ready, 1)

                def v(b, p):
                    dve.wait_ge(v_done, b + 1)
                    for c in range(CH):
                        last = dve.tensor_tensor(v_st[p][:, c, :, 0:DH],
                                                 ps_x[:, c * V_COLS:c * V_COLS + P].rearrange("p (h d) -> p h d", d=DH),
                                                 bv[:, :].rearrange("p (h d) -> p h d", d=DH), ALU.add)
                    if causal:
                        for c in range(CH):
                            at = c * V_COLS + P
                            last = dve.tensor_tensor(u_row[p][:, c, :], ps_x[:, at:at + HEADS], u_bias[:, :], ALU.add)
                    last.then_inc(v_ready, 1)

                def project(b, p, u):
                    dve.wait_ge(proj_hi, b * UNITS + u + 1)
                    for r in range(2):
                        src = ps_p[u % 2][:, r * SEQ:(r + 1) * SEQ]
                        if causal:
                            h = 2 * u + r
                            hi, lo, a, z, col = t_hi[p][:, h, :], t_lo[p][:, h, :], 0, P, h
                        elif u < 2:
                            a, z, col = 2 * QUAD, 3 * QUAD, GROUPS + 2 * u + r
                            hi = k_all[a:z, 2 * u + r, :].bitcast(F32R)
                            lo = hi
                        else:
                            a, z, col = QUAD, 2 * QUAD, 2 * (u - 2) + r
                            hi = q_st[p][a:z, 2 * (u - 2) + r, :]
                            lo = hi
                        last = dve.scalar_tensor_tensor(out=lo, in0=src[a:z, :], scalar=bias[a:z, col:col + 1],
                                                        in1=hi.bitcast(F32), op0=ALU.add, op1=ALU.subtract)
                    last.then_inc(proj_lo, 1)

                def scores(b, p, h):
                    dve.wait_ge(s_done, HEADS * b + h + 1)
                    if causal:
                        dve.tensor_reduce(row_max[p][:, h, 0:1], ps_s[h % 2][:, 0:P], AX_X, ALU.max)
                        dve.tensor_reduce(row_max[p][:, h, 1:2], ps_s[h % 2][:, P:P + SEQ], AX_X,
                                          ALU.max).then_inc(max_done, 1)
                    else:
                        dve.tensor_reduce(row_max[p][:, h, :], ps_s[h % 2][:, :].rearrange("p (c k) -> p c k", k=SEQ),
                                          AX_X, ALU.max).then_inc(max_done, 1)

                def shift_(b, p):
                    dve.wait_ge(max_done, HEADS * (b + 1))
                    if causal:
                        u = u_row[p][:, :, :].rearrange("p c h -> p h c")
                        dve.tensor_tensor(m_row[:, :, :], row_max[p][:, :, :], u, ALU.add).then_inc(m_done, 1)
                        dve.wait_ge(m_done, b + 1)
                        dve.tensor_tensor(shift[p][:, :, :], u, m_row[:, :, :], ALU.subtract).then_inc(shift_ready, 1)
                    else:
                        dve.tensor_scalar(shift[p][:, :, :], row_max[p][:, :, :], -1.0, None,
                                          ALU.mult).then_inc(shift_ready, 1)
                    dve.wait_ge(shift_t_done, b + 1)
                    if causal:
                        behind(dve, st_done, HEADS * b)
                        dve.tensor_copy(neg_max[:, :], ps_o[0:HEADS, 0:SEQ]).then_inc(shift_set, 1)
                    else:
                        for g in range(2):
                            last = dve.tensor_copy(q_st[p][3 * QUAD:3 * QUAD + HEADS, g, :], ps_o[0:HEADS, 0:SEQ])
                        last.then_inc(shift_set, 1)

                def end(b, p, c, part, _):
                    n = CH * b + c
                    if part == 0:
                        dve.wait_ge(ot_done, n + 1)
                        o = ps_x[:, :].rearrange("p (h r) -> p h r", r=QUAD)
                        dve.reciprocal(r_inv[:, :], o[:, :, DH]).then_inc(rinv_done, 1)
                        dve.wait_ge(rinv_done, n + 1)
                        dve.tensor_tensor(att[:, :, :], o[:, :, 0:DH],
                                          r_inv[:, :].unsqueeze(2).to_broadcast([P, HEADS, DH]), ALU.mult
                                          ).then_inc(att_done, 1)
                    if part == 2:
                        dve.wait_ge(out_done, n + 1)
                        dve.wait_ge(bias_added, n + 1)
                        dve.tensor_tensor(x_res[:, n, :], ps_x[:, 0:P], x_res[:, n, :], ALU.add).then_inc(res_done, 1)

                pipeline(dict(norm=norm, v=v, project=project, spread_k=nothing, scores=scores, split=nothing,
                              shifted=nothing, values=nothing, end=end, shift=shift_), dve.Fori)

            @block.tensor
            def _(pe):
                pe.wait_ge(consts_set, N_CONST)

                def three(out, hi_l, lo_l, hi_r, lo_r, first=True, last=True):
                    pe.matmul(out, hi_l, hi_r, start=first, stop=False)
                    pe.matmul(out, hi_l, lo_r, start=False, stop=False)
                    return pe.matmul(out, lo_l, hi_r, start=False, stop=last)

                def norm(b, p):
                    pe.wait_ge(xn_ready, b + 1)
                    behind(pe, proj_lo, UNITS * b)
                    for c in range(CH):
                        last = pe.transpose(ps_p[1][:, c * P:(c + 1) * P], xn[:, c, :], ident)
                    last.then_inc(xt_done, 1)

                def v(b, p):
                    pe.wait_ge(xlo_ready, b + 1)
                    for c in range(CH):
                        cols = slice(c * P, (c + 1) * P)
                        last = three(ps_x[:, c * V_COLS:(c + 1) * V_COLS], x_hi[p][:, cols], x_lo[p][:, cols],
                                     wv_hi[:, :], wv_lo[:, :])
                    last.then_inc(v_done, 1)

                def project(b, p, u):
                    behind(pe, proj_lo, b * UNITS + u - 1)
                    for r in range(2):
                        if causal:
                            cols, n = slice((2 * u + r) * P, (2 * u + r + 1) * P), P
                        else:
                            g = (GROUPS + 2 * u + r) if u < 2 else 2 * (u - 2) + r
                            cols, n = slice(g * 3 * QUAD, (g + 1) * 3 * QUAD), 3 * QUAD
                        last = three(ps_p[u % 2][0:n, r * SEQ:(r + 1) * SEQ], w_hi[:, cols], w_lo[:, cols],
                                     x_hi[p][:, :], x_lo[p][:, :])
                    last.then_inc(proj_done, 1)

                def scores(b, p, h):
                    behind(pe, max_done, HEADS * b + h - 1)
                    out = ps_s[h % 2]
                    if causal:
                        pe.wait_ge(proj_lo, b * UNITS + h // 2 + 1)
                        pe.matmul(out[:, 0:P], t_hi[p][:, h, 0:P], x_hi[p][:, 0:P], start=True, stop=False)
                        pe.matmul(out[:, 0:P], ident_bf, causal_bf, start=False, stop=True)
                        pe.matmul(out[:, P:P + SEQ], t_hi[p][:, h, P:SEQ], x_hi[p][:, :], start=True, stop=False)
                        last = pe.matmul(out[:, SEQ:SEQ + P], ident_bf, causal_bf, start=False, stop=True)
                    else:
                        pe.wait_ge(proj_lo, b * UNITS + 2 + h // 8 + 1)
                        pe.wait_ge(k_spread, HEADS * b + h + 1)
                        for c in range(CH):
                            last = pe.matmul(out[:, c * SEQ:(c + 1) * SEQ],
                                             q_st[p][0:3 * QUAD, h // 4, c * P:(c + 1) * P], k_st[p][0:3 * QUAD, h, :],
                                             start=True, stop=True)
                    last.then_inc(s_done, 1)

                def shift_(b, p):
                    pe.wait_ge(shift_ready, b + 1)
                    behind(pe, o_kept, GROUPS * b)
                    for c in range(CH):
                        last = pe.transpose(ps_o[0:HEADS, c * P:(c + 1) * P], shift[p][:, :, c], ident)
                    last.then_inc(shift_t_done, 1)

                def shifted(b, p, h):
                    n = HEADS * b + h
                    if h == 0:
                        pe.wait_ge(shift_set, b + 1 if causal else 2 * b + 2)
                    behind(pe, exp_done, n - 1)
                    out = ps_st[h % 2]
                    if causal:
                        keys = slice(P * (h % 2), P * (h % 2) + P)
                        pair, width = h - h % 2, (SEQ, P)[h % 2]
                        q = slice(SEQ - width, SEQ)
                        both = out[:, 0:2 * width].rearrange("p (n q) -> p n q", q=width)
                        three(both, x_hi[p][:, keys], x_lo[p][:, keys], t_hi[p][:, pair:pair + 2, q],
                              t_lo[p][:, pair:pair + 2, q], last=False)
                        for n in range(2):
                            one = pair + n
                            last = pe.matmul(both[:, n, :], pick[:, one:one + 1].to_broadcast([HEADS, P]),
                                             neg_max[:, q], start=False, stop=(n == 1))
                    else:
                        for c in range(CH):
                            last = pe.matmul(out[:, c * SEQ:(c + 1) * SEQ], k_st[p][:, h, c * P:(c + 1) * P],
                                             q_st[p][:, h // 4, :], start=True, stop=True)
                    last.then_inc(st_done, 1)

                def values(b, p, g):
                    n = GROUPS * b + g
                    pe.wait_ge(probs_ready, 4 * (n + 1))
                    pe.wait_ge(v_ready, b + 1)
                    behind(pe, o_kept, n)
                    for c in range(CH):
                        for k in range(4):
                            pr = probs[:, 4 * (g % 2) + k, :]
                            rows = slice(k * QUAD, k * QUAD + VCOLS)
                            if causal and c == 1:
                                out, pr = ps_o[rows, P:SEQ], pr[:, SEQ:SEQ + P]
                            else:
                                out, pr = ps_o[rows, 0:SEQ], pr[:, c * SEQ:(c + 1) * SEQ]
                            last = pe.matmul(out, v_st[p][:, c, 4 * g + k, :], pr, start=(c == 0), stop=(c == CH - 1))
                    last.then_inc(o_done, 1)

                def end(b, p, c, part, i):
                    n = CH * b + c
                    if part == 0:
                        pe.wait_ge(o_kept, GROUPS * (b + 1))
                        if c == 1:
                            pe.wait_ge(res_done, n)
                        elif i is not None:
                            pe.wait_ge(v_ready, i + 1)
                        else:
                            behind(pe, res_done, n)
                        for g in range(GROUPS):
                            last = pe.transpose(ps_x[:, g * P:(g + 1) * P], o_all[p][:, g, c * P:(c + 1) * P], ident)
                        last.then_inc(ot_done, 1)
                    elif part == 1:
                        pe.wait_ge(att_done, n + 1)
                        pe.transpose(ps_x[:, 0:P], att[:, :, :].rearrange("p h d -> p (h d)"), ident).then_inc(att_t_done, 1)
                    else:
                        pe.wait_ge(att_t_kept, n + 1)
                        pe.matmul(ps_x[:, 0:P], att_t[:, :], wo[:, :], start=True, stop=True).then_inc(out_done, 1)

                pipeline(dict(norm=norm, v=v, project=project, spread_k=nothing, scores=scores, split=nothing,
                              shifted=shifted, values=values, end=end, shift=shift_), pe.Fori)


def experts(nc, kept, layer, x_res, mean_var, rstd, stats, cst, ident, ones_bf, below_bf, gate_w, up_w, down_w, router_w,
            router_b, slots_dram, y_dram, slots_zeroed):
    with ExitStack() as ctx:
        def sb(name, shape, dt):
            return ctx.enter_context(nc.sbuf_tensor(f"m{layer}_{name}", shape, dt))

        def sem(name):
            return kept.enter_context(nc.semaphore(f"m{layer}_{name}"))

        layer_norm_stats(nc, sem, x_res, mean_var, stats, rstd[:, :], {})

        gates = sb("gates", [P, TOPK, TILES], F32)
        slot_u = sb("slot_u", [P, TOPK, TILES], U32)
        tile_expert = sb("tile_expert", [P, SLOT_TILES], I32)
        shape = [P, TILES, EXPERTS]

        with ExitStack() as rctx:
            def rb(name, shape, dt):
                return rctx.enter_context(nc.sbuf_tensor(f"m{layer}_{name}", shape, dt))

            xn = rb("xn", [P, TILES, P], F32)
            xt = rb("xt", [P, TILES, P], F32)
            logits = rb("logits", shape, F32)
            left = rb("left", shape, F32)
            chosen = rb("chosen", [P, TOPK] + shape[1:], F32)
            both = rb("both", shape, BF16)
            key = rb("key", shape, F32)
            top = rb("top", [P, TOPK, TILES], F32)
            rank = rb("rank", [P, TOPK, TILES], F32)
            drop = rb("drop", [P, TILES], F32)
            ex = rb("ex", [P, TILES], F32)
            den = rb("den", [P, TILES], F32)
            total = rb("total", [P, EXPERTS], F32)
            over = rb("over", [P, EXPERTS, TILES], F32)
            n_tiles = rb("n_tiles", [P, EXPERTS], F32)
            upto = rb("upto", [P, EXPERTS, EXPERTS], F32)
            end_tile = rb("end_tile", [P, EXPERTS], F32)
            first_slot = rb("first_slot", [P, EXPERTS], F32)
            place = rb("place", shape, F32)
            placed = rb("placed", [P, TOPK] + shape[1:], F32)
            slot_f = rb("slot_f", [P, TOPK, TILES], F32)
            past = rb("past", [P, SLOT_TILES, EXPERTS], F32)
            te_f = rb("te_f", [P, SLOT_TILES], F32)
            ps_t = [rctx.enter_context(nc.psum_tensor(f"m{layer}_ps_t{i}", [P, 512], F32)) for i in range(4)]
            ps_l = rctx.enter_context(nc.psum_tensor(f"m{layer}_ps_l", [P, 512], F32))
            ps_n = rctx.enter_context(nc.psum_tensor(f"m{layer}_ps_n", [P, 512], F32))
            ps_c = rctx.enter_context(nc.psum_tensor(f"m{layer}_ps_c", [P, 512], F32))
            xn_ready, xt_done, xt_kept, logits_done = sem("xn_ready"), sem("xt_done"), sem("xt_kept"), sem("logits_done")
            link, gap_ready, ex_done = sem("link"), sem("gap_ready"), sem("ex_done")
            both_ready, counted, slots_ready, sent = sem("both_ready"), sem("counted"), sem("slots_ready"), sem("sent")
            TPB = 4

            with nc.Block() as block:

                @block.vector
                def _(dve):
                    done = [0]

                    def then(instruction):
                        done[0] += 1
                        instruction.then_inc(link, 1)
                        dve.wait_ge(link, done[0])

                    with dve.Fori(0, TILES) as t:
                        dve.tensor_scalar(xn[:, t, :], x_res[:, t, :], mean_var[:, bass.ds(t, 1), 0],
                                          rstd[:, bass.ds(t, 1)], ALU.subtract, ALU.mult).then_inc(xn_ready, 1)
                    dve.wait_ge(logits_done, 1)
                    wide = lambda a: a.unsqueeze(2).to_broadcast(shape)
                    rb_wide = router_b[:, :].unsqueeze(1).to_broadcast(shape)
                    rank_wide = cst("rank").unsqueeze(1).to_broadcast(shape)
                    then(dve.tensor_tensor(logits[:, :, :], ps_l[:, 0:TILES * EXPERTS].rearrange("p (t e) -> p t e", e=EXPERTS),
                                           rb_wide, ALU.add))
                    src = logits
                    for k in range(TOPK):
                        then(dve.tensor_reduce(top[:, k, :], src[:, :, :], AX_X, ALU.max))
                        then(dve.tensor_tensor(key[:, :, :], src[:, :, :], wide(top[:, k, :]), ALU.is_equal))
                        then(dve.tensor_tensor(key[:, :, :], key[:, :, :], rank_wide, ALU.mult))
                        then(dve.tensor_reduce(rank[:, k, :], key[:, :, :], AX_X, ALU.max))
                        then(dve.tensor_tensor(chosen[:, k, :, :], rank_wide, wide(rank[:, k, :]), ALU.is_equal))
                        if k == 0:
                            then(dve.scalar_tensor_tensor(out=left[:, :, :].rearrange("p t e -> p (t e)"),
                                                          in0=chosen[:, 0, :, :].rearrange("p t e -> p (t e)"),
                                                          scalar=-3.0e38, in1=logits[:, :, :].rearrange("p t e -> p (t e)"),
                                                          op0=ALU.mult, op1=ALU.add))
                            src = left
                    dve.tensor_tensor(both[:, :, :], chosen[:, 0, :, :], chosen[:, 1, :, :], ALU.add).then_inc(both_ready, 1)
                    dve.tensor_tensor(drop[:, :], top[:, 1, :], top[:, 0, :], ALU.subtract).then_inc(gap_ready, 1)
                    dve.wait_ge(ex_done, 1)
                    then(dve.tensor_scalar(den[:, :], ex[:, :], 1.0, None, ALU.add))
                    then(dve.reciprocal(gates[:, 0, :], den[:, :]))
                    then(dve.tensor_tensor(gates[:, 1, :], gates[:, 0, :], ex[:, :], ALU.mult))
                    dve.wait_ge(counted, 1)
                    then(dve.tensor_copy(total[:, :], ps_c[:, 0:EXPERTS]))
                    then(dve.tensor_tensor(over[:, :, :], total[:, :].unsqueeze(2).to_broadcast([P, EXPERTS, TILES]),
                                           cst("full").unsqueeze(1).to_broadcast([P, EXPERTS, TILES]), ALU.is_gt))
                    then(dve.tensor_reduce(n_tiles[:, :], over[:, :, :], AX_X, ALU.add))
                    then(dve.tensor_tensor(upto[:, :, :], n_tiles[:, :].unsqueeze(1).to_broadcast([P, EXPERTS, EXPERTS]),
                                           cst("upto").rearrange("p (a b) -> p a b", b=EXPERTS), ALU.mult))
                    then(dve.tensor_reduce(end_tile[:, :], upto[:, :, :], AX_X, ALU.add))
                    then(dve.tensor_tensor(first_slot[:, :], end_tile[:, :], n_tiles[:, :], ALU.subtract))
                    then(dve.tensor_scalar(first_slot[:, :], first_slot[:, :], float(P), None, ALU.mult))
                    then(dve.tensor_tensor(place[:, :, :], ps_n[:, 0:TILES * EXPERTS].rearrange("p (t e) -> p t e", e=EXPERTS),
                                           first_slot[:, :].unsqueeze(1).to_broadcast(shape), ALU.add))
                    for k in range(TOPK):
                        then(dve.tensor_tensor(placed[:, k, :, :], chosen[:, k, :, :], place[:, :, :], ALU.mult))
                        then(dve.tensor_reduce(slot_f[:, k, :], placed[:, k, :, :], AX_X, ALU.add))
                    dve.tensor_copy(slot_u[:, :, :], slot_f[:, :, :]).then_inc(slots_ready, 1)
                    then(dve.tensor_tensor(past[:, :, :], cst("tile_no").unsqueeze(2).to_broadcast([P, SLOT_TILES, EXPERTS]),
                                           end_tile[:, :].unsqueeze(1).to_broadcast([P, SLOT_TILES, EXPERTS]), ALU.is_ge))
                    then(dve.tensor_reduce(te_f[:, :], past[:, :, :], AX_X, ALU.add))
                    then(dve.tensor_scalar(te_f[:, :], te_f[:, :], float(EXPERTS - 1), None, ALU.min))
                    then(dve.tensor_copy(tile_expert[:, :], te_f[:, :]))

                @block.scalar
                def _(act):
                    for q in range(TILES // TPB):
                        act.wait_ge(xt_done, q + 1)
                        act.copy(xt[:, q * TPB:(q + 1) * TPB, :], ps_t[q][:, :].rearrange("p (t k) -> p t k", k=P)
                                 ).then_inc(xt_kept, 1)
                    act.wait_ge(gap_ready, 1)
                    act.activation(ex[:, :], drop[:, :], ACT.Exp).then_inc(ex_done, 1)

                @block.tensor
                def _(pe):
                    for q in range(TILES // TPB):
                        pe.wait_ge(xn_ready, (q + 1) * TPB)
                        for t in range(TPB):
                            last = pe.transpose(ps_t[q][:, t * P:(t + 1) * P], xn[:, q * TPB + t, :], ident)
                        last.then_inc(xt_done, 1)
                    for t in range(TILES):
                        if t % TPB == 0:
                            pe.wait_ge(xt_kept, t // TPB + 1)
                        last = pe.matmul(ps_l[:, t * EXPERTS:(t + 1) * EXPERTS], xt[:, t, :], router_w[:, :],
                                         start=True, stop=True)
                    last.then_inc(logits_done, 1)
                    pe.wait_ge(both_ready, 1)
                    before = ps_n[:, 0:TILES * EXPERTS].rearrange("p (t e) -> p t e", e=EXPERTS)
                    pe.matmul(before, below_bf, both[:, :, :], start=True, stop=False)
                    for t in range(TILES - 1):
                        n = TILES - 1 - t
                        pe.matmul(before[:, t + 1:TILES, :], ones_bf, both[:, t:t + 1, :].to_broadcast([P, n, EXPERTS]),
                                  start=False, stop=(t == TILES - 2))
                    for t in range(TILES):
                        last = pe.matmul(ps_c[:, 0:EXPERTS], ones_bf, both[:, t, :], start=(t == 0), stop=(t == TILES - 1))
                    last.then_inc(counted, 1)

                @block.gpsimd
                def _(pool):
                    if slots_zeroed is not None:
                        pool.wait_ge(slots_zeroed, 16)
                    pool.wait_ge(slots_ready, 1)
                    for t in range(TILES):
                        for k in range(TOPK):
                            pool.indirect_dma_start(
                                out=slots_dram[:, :], out_offset=bass.IndirectOffsetOnAxis(ap=slot_u[:, k, t:t + 1], axis=0),
                                in_=xn[:, t, :], in_offset=None).then_inc(sent, 16)
                    pool.wait_ge(sent, 16 * TILES * TOPK)

        with ExitStack() as ectx:
            def eb(name, shape, dt):
                return ectx.enter_context(nc.sbuf_tensor(f"m{layer}_{name}", shape, dt))

            TWO = range(2)
            xs = [eb(f"xs{p}", [P, P], F32) for p in TWO]
            xs_hi = [eb(f"xs_hi{p}", [P, P], F32R) for p in TWO]
            xs_lo = [eb(f"xs_lo{p}", [P, P], F32R) for p in TWO]
            act_g = [eb(f"act_g{p}", [P, FF], F32) for p in TWO]
            hid = [eb(f"hid{p}", [P, FF], F32) for p in TWO]
            hid_t = [eb(f"hid_t{p}", [P, FCH, P], F32) for p in TWO]
            ys = [eb(f"ys{p}", [P, P], F32) for p in TWO]
            ps = [ectx.enter_context(nc.psum_tensor(f"m{layer}_ps{i}", [P, 512], F32)) for i in range(8)]
            ps_g, ps_u, ps_h, ps_x, ps_y = ps[0:2], ps[2:4], ps[4:6], ps[6], ps[7]
            in_landed = [sem(f"in_landed{p}") for p in TWO]
            out_landed = [sem(f"out_landed{p}") for p in TWO]
            t_done, hi_ready, lo_ready, gu_done, silu_done = (
                sem("t_done"), sem("hi_ready"), sem("lo_ready"), sem("gu_done"), sem("silu_done"))
            hid_ready, ht_done, ht_kept, y_done, y_kept = (
                sem("hid_ready"), sem("ht_done"), sem("ht_kept"), sem("y_done"), sem("y_kept"))

            with nc.Block() as block:

                @block.sync
                def _(sp):
                    def load(pair):
                        for p in TWO:
                            t = 2 * pair + p
                            behind(sp, t_done, t - 1)
                            sp.dma_start(xs[p][:, :], slots_dram[bass.ds(t * P, P), :]).then_inc(in_landed[p], 16)

                    load(0)
                    with sp.Fori(1, SLOT_TILES // 2) as pair:
                        load(pair)

                @block.tensor
                def _(pe):
                    def first(t, pair, p):
                        pe.wait_ge(in_landed[p], 16 * pair + 16)
                        behind(pe, lo_ready, t)
                        pe.transpose(ps_x[:, 0:P], xs[p][:, :], ident).then_inc(t_done, 1)
                        e = pe.value_load(tile_expert[0:1, bass.ds(t, 1)], min_val=0, max_val=EXPERTS - 1)
                        pe.wait_ge(lo_ready, t + 1)
                        behind(pe, hid_ready, t - 1)
                        for out, w in ((ps_g[p], gate_w), (ps_u[p], up_w)):
                            pe.matmul(out[:, :], xs_hi[p][:, :], w[0][:, e, :], start=True, stop=False)
                            pe.matmul(out[:, :], xs_hi[p][:, :], w[1][:, e, :], start=False, stop=False)
                            last = pe.matmul(out[:, :], xs_lo[p][:, :], w[0][:, e, :], start=False, stop=True)
                        last.then_inc(gu_done, 1)

                    def second(t, p):
                        pe.wait_ge(hid_ready, t + 1)
                        for f in range(FCH):
                            last = pe.transpose(ps_h[p][:, f * P:(f + 1) * P], hid[p][:, f * P:(f + 1) * P], ident)
                        last.then_inc(ht_done, 1)

                    def third(t, p):
                        e = pe.value_load(tile_expert[0:1, bass.ds(t, 1)], min_val=0, max_val=EXPERTS - 1)
                        pe.wait_ge(ht_kept, t + 1)
                        behind(pe, y_kept, t)
                        for f in range(FCH):
                            last = pe.matmul(ps_y[:, 0:P], hid_t[p][:, f, :], down_w[:, e, f * P:(f + 1) * P],
                                             start=(f == 0), stop=(f == FCH - 1))
                        last.then_inc(y_done, 1)

                    first(0, 0, 0)
                    first(1, 0, 1)
                    second(0, 0)
                    third(0, 0)
                    with pe.Fori(1, SLOT_TILES // 2) as pair:
                        for p in TWO:
                            t = 2 * pair + p
                            first(t, pair, p)
                            second(t - 1, 1 - p)
                            third(t - 1, 1 - p)
                    second(SLOT_TILES - 1, 1)
                    third(SLOT_TILES - 1, 1)

                @block.scalar
                def _(act):
                    def front(t, p):
                        act.wait_ge(t_done, t + 1)
                        behind(act, gu_done, t - 1)
                        act.copy(xs_hi[p][:, :], ps_x[:, 0:P]).then_inc(hi_ready, 1)

                    def middle(t, p):
                        act.wait_ge(gu_done, t + 1)
                        act.activation(act_g[p][:, :], ps_g[p][:, :], ACT.Silu).then_inc(silu_done, 1)

                    def back(t, p):
                        act.wait_ge(ht_done, t + 1)
                        act.copy(hid_t[p][:, :, :], ps_h[p][:, :].rearrange("p (f k) -> p f k", k=P)).then_inc(ht_kept, 1)

                    front(0, 0)
                    front(1, 1)
                    middle(0, 0)
                    back(0, 0)
                    with act.Fori(1, SLOT_TILES // 2) as pair:
                        for p in TWO:
                            t = 2 * pair + p
                            front(t, p)
                            middle(t - 1, 1 - p)
                            back(t - 1, 1 - p)
                    middle(SLOT_TILES - 1, 1)
                    back(SLOT_TILES - 1, 1)

                @block.vector
                def _(dve):
                    def front(t, p):
                        dve.wait_ge(hi_ready, t + 1)
                        dve.tensor_tensor(xs_lo[p][:, :], ps_x[:, 0:P], xs_hi[p][:, :].bitcast(F32),
                                          ALU.subtract).then_inc(lo_ready, 1)

                    def middle(t, p):
                        dve.wait_ge(silu_done, t + 1)
                        dve.tensor_tensor(hid[p][:, :], ps_u[p][:, :], act_g[p][:, :], ALU.mult).then_inc(hid_ready, 1)

                    def back(t, pair, p):
                        dve.wait_ge(y_done, t + 1)
                        behind(dve, out_landed[p], 16 * pair)
                        dve.tensor_copy(ys[p][:, :], ps_y[:, 0:P]).then_inc(y_kept, 1)

                    def both_tiles(pair):
                        for p in TWO:
                            t = 2 * pair + p
                            front(t, p)
                            middle(t - 1, 1 - p)
                            back(t - 1, pair if p else pair - 1, 1 - p)

                    front(0, 0)
                    front(1, 1)
                    middle(0, 0)
                    back(0, 0, 0)
                    both_tiles(1)
                    with dve.Fori(2, SLOT_TILES // 2) as pair:
                        both_tiles(pair)
                    middle(SLOT_TILES - 1, 1)
                    back(SLOT_TILES - 1, SLOT_TILES // 2 - 1, 1)

                @block.gpsimd
                def _(pool):
                    with pool.Fori(0, SLOT_TILES // 2) as pair:
                        for p in TWO:
                            t = 2 * pair + p
                            pool.wait_ge(y_kept, t + 1)
                            pool.dma_start(y_dram[bass.ds(t * P, P), :], ys[p][:, :]).then_inc(out_landed[p], 16)
                    for p in TWO:
                        pool.wait_ge(out_landed[p], 16 * (SLOT_TILES // 2))

        with ExitStack() as cctx:
            y = cctx.enter_context(nc.sbuf_tensor(f"m{layer}_y", [P, TOPK, TILES, P], F32))
            got = [sem(f"got{t}") for t in range(TILES // 4)]
            first_added, second_added = sem("first_added"), sem("second_added")
            with nc.Block() as block:

                @block.gpsimd
                def _(pool):
                    for t in range(TILES):
                        for k in range(TOPK):
                            pool.indirect_dma_start(
                                out=y[:, k, t, :], out_offset=None, in_=y_dram[:, :],
                                in_offset=bass.IndirectOffsetOnAxis(ap=slot_u[:, k, t:t + 1], axis=0)).then_inc(got[t // 4], 16)

                @block.vector
                def _(dve):
                    for t in range(TILES):
                        if t % 4 == 0:
                            dve.wait_ge(got[t // 4], 16 * TOPK * 4)
                        dve.scalar_tensor_tensor(out=x_res[:, t, :], in0=y[:, 0, t, :], scalar=gates[:, 0, t:t + 1],
                                                 in1=x_res[:, t, :], op0=ALU.mult, op1=ALU.add).then_inc(first_added, 1)
                    for t in range(TILES):
                        dve.wait_ge(first_added, t + 1)
                        dve.scalar_tensor_tensor(out=x_res[:, t, :], in0=y[:, 1, t, :], scalar=gates[:, 1, t:t + 1],
                                                 in1=x_res[:, t, :], op0=ALU.mult, op1=ALU.add).then_inc(second_added, 1)


def hybrid_kernel(nc, ins, out):
    with ExitStack() as ctx:
        def sb(name, shape, dt):
            return ctx.enter_context(nc.sbuf_tensor(name, shape, dt))

        def sem(name):
            return ctx.enter_context(nc.semaphore(name))

        x_res = sb("x_res", [P, TILES, P], F32)
        consts = sb("consts", [P, CONST_COLS], F32)
        mean_var = sb("mean_var", [P, TILES, 2], F32)
        stats = sb("stats", [P, TILES, 6], F32)
        rstd = sb("rstd", [P, TILES], F32)
        ones_bf, below_bf, ident_bf, causal_bf = (sb(n, [P, P], BF16) for n in ("ones_bf", "below_bf", "ident_bf", "causal_bf"))
        gate_w = [sb(f"gate_{n}", [P, EXPERTS, FF], F32R) for n in ("hi", "lo")]
        up_w = [sb(f"up_{n}", [P, EXPERTS, FF], F32R) for n in ("hi", "lo")]
        down_w = sb("down_w", [P, EXPERTS, FF], F32)
        router_w = sb("router_w", [P, EXPERTS], F32)
        router_b = sb("router_b", [P, EXPERTS], F32)
        slots_dram = nc.dram_tensor("slots_dram", (SLOT_TILES * P, D), F32, kind="Internal").ap()
        y_dram = nc.dram_tensor("y_dram", (SLOT_TILES * P, D), F32, kind="Internal").ap()
        slots_zeroed = sem("slots_zeroed")

        def cst(name):
            return consts[:, CONST[name][0]:CONST[name][1]]

        ident = cst("ident")

        small, big, zeros_set, cast = sem("small"), sem("big"), sem("zeros_set"), sem("cast")
        with (nc.sbuf_tensor("zeros", [P, SLOT_TILES * P], F32) as zeros, nc.sbuf_tensor("to_cast", [P, 2, P], F32) as to_cast):
            with nc.Block() as block:

                @block.sync
                def _(sp):
                    sp.dma_start(consts[:, :], ins["consts"]).then_inc(small, 16)
                    sp.dma_start(to_cast[:, :, :], ins["cast"]).then_inc(small, 16)
                    sp.dma_start(x_res[:, :, :], ins["x"].rearrange("(t p) d -> p t d", p=P)).then_inc(small, 16)
                    sp.dma_start(router_w[:, :], ins["router_w"]).then_inc(small, 16)
                    sp.dma_start(router_b[:, :], ins["router_b"]).then_inc(small, 16)
                    sp.wait_ge(zeros_set, 1)
                    sp.dma_start(slots_dram.rearrange("(p a) d -> p (a d)", p=P), zeros[:, :]).then_inc(slots_zeroed, 16)
                    sp.wait_ge(small, 5 * 16)
                    sp.wait_ge(slots_zeroed, 16)

                @block.gpsimd
                def _(pool):
                    pool.memset(zeros[:, :], 0.0).then_inc(zeros_set, 1)

                @block.vector
                def _(dve):
                    dve.wait_ge(small, 5 * 16)
                    for dst, src in ((ones_bf, cst("ones")), (ident_bf, ident), (below_bf, to_cast[:, 0, :]), (causal_bf, to_cast[:, 1, :])):
                        dve.tensor_copy(dst[:, :], src).then_inc(cast, 1)

        moe = (x_res, mean_var, rstd, stats, cst, ident, ones_bf[:, :], below_bf[:, :], gate_w, up_w, down_w, router_w,
               router_b, slots_dram, y_dram)
        attn = (x_res, mean_var, rstd, stats, cst, ident, ident_bf[:, :], causal_bf[:, :])
        attention(nc, ctx, False, *attn, {k[2:]: v for k, v in ins.items() if k.startswith("a_")},
                  (gate_w, up_w, big, (ins["gate_w"], ins["up_w"], ins["down_w"]), down_w))
        experts(nc, ctx, 0, *moe, slots_zeroed)
        attention(nc, ctx, True, *attn, {k[2:]: v for k, v in ins.items() if k.startswith("c_")})
        experts(nc, ctx, 1, *moe, None)

        stored = sem("stored")
        with nc.Block() as block:

            @block.sync
            def _(sp):
                sp.dma_start(out.rearrange("(t p) d -> p t d", p=P), x_res[:, :, :]).then_inc(stored, 16)
                sp.wait_ge(stored, 16)


def constants():
    import numpy as np
    c = np.zeros((P, CONST_COLS), np.float32)

    def put(name, value):
        c[:, CONST[name][0]:CONST[name][1]] = value

    i = np.arange(P)
    put("ident", np.eye(P))
    put("ones", 1.0)
    put("head", i[:, None] - 3 * QUAD == np.arange(HEADS)[None, :])
    put("group", (i[:, None] % QUAD) // DH == np.arange(GROUPS)[None, :])
    put("rank", EXPERTS - np.arange(EXPERTS))
    put("full", P * np.arange(TILES))
    e = np.arange(EXPERTS)
    put("upto", (e[None, :] <= e[:, None]).astype(np.float32).reshape(1, -1))
    put("tile_no", np.arange(SLOT_TILES))
    below = i[:, None] < i[None, :]
    causal = np.where(i[None, :] <= i[:, None], 0.0, MASKED)
    return c, np.stack([below, causal], 1).astype(np.float32)


def kernel(**inputs):
    import numpy as np
    import concourse.bacc as bacc
    from concourse.bass_utils import run_bass_kernel_spmd

    a = {k: np.asarray(v) for k, v in inputs.items()}
    wide = lambda v: np.ascontiguousarray(np.broadcast_to(v[None, :], (P, v.shape[0])))
    qkv, qkv_b = a["L0_attn_a_qkv_weight"], a["L0_attn_a_qkv_bias"]

    def groups(w):
        w = w.reshape(GROUPS, 1, QUAD, -1)
        return np.broadcast_to(w, (GROUPS, 3, QUAD, w.shape[-1])).reshape(GROUPS * 3 * QUAD, -1)

    bqk = np.zeros((P, 2 * GROUPS), np.float32)
    bqk[0:3 * QUAD] = np.concatenate([groups(qkv_b[0:D, None]), groups(qkv_b[D:2 * D, None])]).reshape(2 * GROUPS, 3 * QUAD).T
    kqv, kqv_b = a["L0_attn_b_Wkqv"], a["L0_attn_b_bkqv"]
    consts, cast = constants()
    arrays = {
        "consts": consts, "cast": cast,
        "x": a["L0_attn_a_input_tensor"].reshape(TILES * P, D),
        "router_w": a["L0_ffn_router_w"].T,
        "router_b": wide(a["L0_ffn_router_b"]),
        "gate_w": a["L0_ffn_gate_w"].transpose(2, 0, 1).reshape(P, -1),
        "up_w": a["L0_ffn_up_w"].transpose(2, 0, 1).reshape(P, -1),
        "down_w": a["L0_ffn_down_w"].transpose(2, 0, 1).reshape(FCH, P, EXPERTS, P).transpose(1, 2, 0, 3).reshape(P, EXPERTS, FF),
        "a_wqk": np.concatenate([groups(qkv[0:D]), groups(qkv[D:2 * D])]).T,
        "a_bqk": bqk,
        "a_wv": qkv[2 * D:].T, "a_bv": wide(qkv_b[2 * D:]),
        "a_wo": a["L0_attn_a_out_weight"].T, "a_bo": wide(a["L0_attn_a_out_bias"]),
        "c_wkT": kqv[:, :, 0:D].transpose(2, 0, 1), "c_wqT": kqv[:, :, D:2 * D].transpose(2, 0, 1),
        "c_bk": kqv_b[:, 0:D].T, "c_bq": kqv_b[:, D:2 * D].T,
        "c_wv": kqv[:, :, 2 * D:].transpose(1, 0, 2).reshape(D, HEADS * DH), "c_bv": wide(kqv_b[:, 2 * D:].reshape(-1)),
        "c_wo": a["L0_attn_b_Wp"], "c_bo": wide(a["L0_attn_b_bp"]),
    }
    nc = bacc.Bacc("TRN2", target_bir_lowering=False, num_devices=1)
    arrays = {k: np.ascontiguousarray(v) for k, v in arrays.items()}
    ins = {k: nc.dram_tensor(f"in_{k}", v.shape, mybir.dt.from_np(v.dtype), kind="ExternalInput").ap()
           for k, v in arrays.items()}
    out = nc.dram_tensor("out_x", (TILES * P, D), F32, kind="ExternalOutput").ap()
    hybrid_kernel(nc, ins, out)
    r = run_bass_kernel_spmd(nc, [{f"in_{k}": v for k, v in arrays.items()}], core_ids=[0])
    return np.asarray(r.results[0]["out_x"]).reshape(BATCH, SEQ, D)
```

```python
from contextlib import ExitStack

import concourse.bass as bass
from concourse import mybir

ALU = mybir.AluOpType
ACT = mybir.ActivationFunctionType
AX_X = mybir.AxisListType.X
F32 = mybir.dt.float32
F32R = mybir.dt.float32r
BF16 = mybir.dt.bfloat16
I32 = mybir.dt.int32
U32 = mybir.dt.uint32

P = 128
BATCH, SEQ, D = 8, 256, 128
TOKENS = BATCH * SEQ
TILES = TOKENS // P
CH = SEQ // P
HEADS, DH = 16, 8
GROUPS = 4
QUAD = 32
VCOLS = 16
EXPERTS, TOPK, FF = 8, 2, 512
FCH = FF // P
SLOT_TILES = TILES * TOPK + EXPERTS
RING = 4
SMALL_LOADS = 4
LN_EPS = 1e-5
MASKED = -1.0e30

def columns(widths):
    at, where = 0, {}
    for name, width in widths.items():
        where[name] = (at, at + width)
        at += width
    return where, at


CONST, CONST_COLS = columns(dict(ident=P, ones=P, head=HEADS, group=GROUPS))
MOE_CONST, MOE_COLS = columns(dict(rank=EXPERTS, full=TILES, upto=EXPERTS * EXPERTS, tile_no=SLOT_TILES, row_no=P,
                                   part_no=1, digit=SLOT_TILES, pair_no=TOPK * TILES, pad_row=SLOT_TILES))


PLAIN_AT = {'step': 57, 'center': 2, 'norm': 8, 'low': 9, 'project': [10, 12, 15, 21], 'v': 18, 'shift': 76, 'keep_shift': 77, 'spread_k': [13, 2], 'scores': [25, 30, 33, 35, 38, 40, 43, 45, 49, 52, 55, 58, 61, 64, 67, 70], 'shifted': [79, 82, 85, 88, 89, 92, 95, 100, 101, 104, 107, 110, 113, 116, 122, 125], 'values': [94, 100, 104, 110, 118, 119, 128, 131], 'end': [135, 141, 147, 153, 159, 168], 'split': [38, 55]}
CAUSAL_AT = {'step': 62, 'center': 0, 'norm': 4, 'low': 12, 'project': [13, 16, 19, 22, 23, 26, 32, 35], 'v': 15, 'shift': 73, 'keep_shift': 75, 'scores': [22, 25, 28, 31, 34, 37, 40, 45, 46, 49, 52, 53, 58, 59, 62, 65], 'shifted': [76, 79, 82, 85, 88, 91, 95, 98, 101, 104, 107, 110, 114, 116, 119, 122], 'values': [93, 94, 104, 106, 116, 117, 128, 129], 'end': [142, 151, 157, 163, 169, 175]}

def behind(eng, sem, value):
    if isinstance(value, int) and value <= 0:
        return
    eng.wait_ge(sem, value)


def layer_norm_stats(nc, sem, x_res, mean_var, stats, rstd, work, sums_ready=True):
    moments, std_in, std_out = sem("moments"), sem("std_in"), sem("std_out")
    with nc.Block() as block:

        @block.vector
        def _(dve):
            if "vector_first" in work:
                work["vector_first"](dve)
            if not sums_ready:
                for t in range(TILES):
                    dve.bn_stats(stats[:, t, :], x_res[:, t, :]).then_inc(moments, 1)
                dve.wait_ge(moments, TILES)
            for t in range(TILES):
                dve.bn_aggr(mean_var[:, t, :], stats[:, t, :]).then_inc(moments, 1)
            dve.wait_ge(moments, TILES if sums_ready else 2 * TILES)
            dve.tensor_scalar(rstd, mean_var[:, :, 1], LN_EPS, None, ALU.add).then_inc(std_in, 1)
            dve.wait_ge(std_out, 1)
            dve.reciprocal(rstd, rstd)
            if "vector" in work:
                work["vector"](dve)

        @block.scalar
        def _(act):
            if "scalar_first" in work:
                work["scalar_first"](act)
            act.wait_ge(std_in, 1)
            act.activation(rstd, rstd, ACT.Sqrt).then_inc(std_out, 1)
            if "scalar" in work:
                work["scalar"](act)

        for name in ("sync", "gpsimd", "tensor"):
            if name in work:
                {"sync": block.sync, "gpsimd": block.gpsimd, "tensor": block.tensor}[name](work[name])


def attention(nc, kept, causal, x_res, mean_var, rstd, stats, cst, ident, ident_bf, causal_bf, weights, split_w=None,
              later_loads=None, ready=None, first=None):
    scale = float((D if causal else DH) ** -0.5)
    UNITS = HEADS // 2 if causal else 4
    with ExitStack() as ctx:
        tag = "c" if causal else "a"

        def sb(name, shape, dt):
            return ctx.enter_context(nc.sbuf_tensor(f"{tag}_{name}", shape, dt))

        def sem(name):
            return kept.enter_context(nc.semaphore(f"{tag}_{name}"))

        WCOLS = HEADS * P if causal else 2 * GROUPS * 3 * QUAD
        V_COLS = P + HEADS if causal else P
        if causal:
            w_hi, w_lo, wv_hi, wv_lo, wo, bv, bo, bias, u_bias = (
                ready.w_hi, ready.w_lo, ready.wv_hi, ready.wv_lo, ready.wo, ready.bv, ready.bo, ready.bias, ready.u_bias)
            layer_norm_stats(nc, sem, x_res, mean_var, stats, rstd[:, :], {})
        else:
            w_hi, w_lo = sb("w_hi", [P, WCOLS], F32R), sb("w_lo", [P, WCOLS], F32R)
            wv_hi, wv_lo = sb("wv_hi", [P, V_COLS], F32R), sb("wv_lo", [P, V_COLS], F32R)
            wv, wo = sb("wv", [P, P], F32), sb("wo", [P, P], F32)
            bv, bo = sb("bv", [P, P], F32), sb("bo", [P, P], F32)
            bias = sb("bias", [P, HEADS], F32)
            q_st = [sb(f"q_st{p}", [P, GROUPS, SEQ], F32R) for p in range(2)]
            k_st = [sb(f"k_st{p}", [P, HEADS, SEQ], F32R) for p in range(2)]
            loaded, hi_made = sem("loaded"), sem("hi_made")
            with nc.sbuf_tensor("a_wqk", [P, WCOLS], F32) as wqk, nc.sbuf_tensor("to_cast", [P, 2, P], F32) as to_cast:
                first_loads, casts, consts_in = first

                def fixed_rows(pool):
                    for p in range(2):
                        pool.memset(q_st[p][3 * QUAD:P, :, :].bitcast(F32), 0.0)

                def load_all(sp):
                    first_loads(sp, to_cast)
                    for dst, name in ((wv, "wv"), (wo, "wo"), (bv, "bv"), (bo, "bo")):
                        sp.dma_start(dst[:, :], weights[name]).then_inc(loaded, 16)
                    sp.dma_start(wqk[:, :], weights["wqk"]).then_inc(loaded, 16)
                    sp.dma_start(bias[:, 0:2 * GROUPS], weights["bqk"]).then_inc(loaded, 16)
                    gate_w, up_w, big, (gate_in, up_in, down_in), down_w = split_w
                    for w, w_in in ((gate_w, gate_in), (up_w, up_in)):
                        sp.dma_start(w[1][:, :, :].rearrange("p e f -> p (e f)").bitcast(F32), w_in).then_inc(big, 16)
                    sp.dma_start(down_w[:, :, :], down_in).then_inc(big, 16)

                def hi_parts(act):
                    act.wait_ge(consts_in, 16)
                    for p in range(2):
                        act.copy(k_st[p][3 * QUAD:P, :, :],
                                 cst("head")[3 * QUAD:P, :].unsqueeze(2).to_broadcast([QUAD, HEADS, SEQ]))
                    act.wait_ge(loaded, 6 * 16)
                    act.copy(w_hi[:, :], wqk[:, :])
                    act.copy(wv_hi[:, 0:P], wv[:, :]).then_inc(hi_made, 1)

                def lo_parts(dve):
                    dve.wait_ge(hi_made, 1)
                    dve.tensor_tensor(w_lo[:, :], wqk[:, :], w_hi[:, :].bitcast(F32), ALU.subtract)
                    dve.tensor_tensor(wv_lo[:, 0:P], wv[:, :], wv_hi[:, 0:P].bitcast(F32), ALU.subtract)

                layer_norm_stats(nc, sem, x_res, mean_var, stats, rstd[:, :], {
                    "sync": load_all, "vector_first": lambda dve: casts(dve, to_cast), "vector": lo_parts,
                    "scalar_first": hi_parts, "gpsimd": fixed_rows}, sums_ready=False)

        TWO = range(2)
        xn = sb("xn", [P, CH, P], F32)
        x_hi = [sb(f"x_hi{p}", [P, SEQ], F32R) for p in TWO]
        x_lo = [sb(f"x_lo{p}", [P, SEQ], F32R) for p in TWO]
        v_st = ready.v_st if causal else [sb(f"v_st{p}", [P, CH, HEADS, VCOLS], F32) for p in TWO]
        row_max = [sb(f"row_max{p}", [P, HEADS, CH], F32) for p in TWO]
        shift = [sb(f"shift{p}", [P, HEADS, CH], F32) for p in TWO]
        o_all = [ready.o_all0, ready.o_all1] if causal else [sb(f"o_all{p}", [P, GROUPS, SEQ], F32) for p in TWO]
        r_inv = sb("r_inv", [P, HEADS], F32)
        att = sb("att", [P, HEADS, DH], F32)
        att_t = sb("att_t", [P, P], F32)
        ST_COLS = SEQ + P if causal else 2 * SEQ
        probs = ready.probs if causal else sb("probs", [P, 8, ST_COLS], F32)
        if causal:
            t_hi = [sb(f"t_hi{p}", [P, HEADS, SEQ], F32R) for p in TWO]
            t_lo = [sb(f"t_lo{p}", [P, HEADS, SEQ], F32R) for p in TWO]
            neg_max = sb("neg_max", [HEADS, SEQ], F32R)
            u_row = [sb(f"u_row{p}", [P, CH, HEADS], F32) for p in TWO]
            pick = sb("pick", [HEADS, HEADS], F32R)
            m_row = sb("m_row", [P, HEADS, CH], F32)
        else:
            k_all = sb("k_all", [P, GROUPS, SEQ], F32)

        def bank(name, n=1):
            return ctx.enter_context(nc.psum_tensor(f"{tag}_{name}", [P, 512 * n], F32))

        ps_s = [bank(f"ps_s{i}") for i in TWO]
        ps_st = [bank(f"ps_st{i}") for i in TWO]
        ps_o = bank("ps_o")
        ps_x = bank("ps_x")
        ps_p = [bank(f"ps_p{i}") for i in TWO]

        consts_set = sem("consts_set")
        xn_ready, xt_done, xhi_ready, xlo_ready = sem("xn_ready"), sem("xt_done"), sem("xhi_ready"), sem("xlo_ready")
        v_done, v_ready, bias_added = sem("v_done"), sem("v_ready"), sem("bias_added")
        proj_done, proj_hi, proj_lo = sem("proj_done"), sem("proj_hi"), sem("proj_lo")
        s_done, max_done, shift_ready, shift_t_done, shift_set = (
            sem("s_done"), sem("max_done"), sem("shift_ready"), sem("shift_t_done"), sem("shift_set"))
        st_done, exp_done, o_done, o_kept = sem("st_done"), sem("exp_done"), sem("o_done"), sem("o_kept")
        ot_done, rinv_done, att_done, att_t_done, att_t_kept, out_done, res_done = (
            sem("ot_done"), sem("rinv_done"), sem("att_done"), sem("att_t_done"), sem("att_t_kept"),
            sem("out_done"), sem("res_done"))
        if causal:
            m_done, cut_begun, cut_done = sem("m_done"), sem("cut_begun"), sem("cut_done")
        else:
            k_spread, split_hi, split_lo = sem("k_spread"), sem("split_hi"), sem("split_lo")
        probs_ready = cut_done if causal else exp_done
        N_CONST = 6 if causal else 5

        if causal:
            AT = CAUSAL_AT
        else:
            AT = PLAIN_AT
        STEP = AT["step"]

        def pipeline(pieces, Fori):
            def at_time(b, p, at, newest):
                for name in ("center", "norm", "low", "v", "shift", "keep_shift"):
                    if at == AT[name]:
                        pieces[name](b, p)
                for n in range(UNITS):
                    if at == AT["project"][n]:
                        pieces["project"](b, p, n)
                for h in range(HEADS):
                    if not causal and at == AT["spread_k"][0] + h * AT["spread_k"][1]:
                        pieces["spread_k"](b, p, h)
                    if at == AT["shifted"][h]:
                        pieces["shifted"](b, p, h)
                    if at == AT["scores"][h]:
                        pieces["scores"](b, p, h)
                for n in range(GROUPS * CH):
                    if at == AT["values"][n]:
                        pieces["values"](b, p, n // CH, n % CH)
                for n in range(3 * CH):
                    if at == AT["end"][n]:
                        pieces["end"](b, p, n // 3, n % 3, newest)
                if not causal and at in AT["split"]:
                    pieces["split"](b, AT["split"].index(at))

            def step(i, parity, head, middle, tail):
                newest = i if head else None
                for s in range(STEP):
                    if tail:
                        at_time(i - 2, parity, 2 * STEP + s, newest)
                    if middle:
                        at_time(i - 1, 1 - parity, STEP + s, newest)
                    if head:
                        at_time(i, parity, s, newest)

            step(0, 0, True, False, False)
            step(1, 1, True, True, False)
            with Fori(0, BATCH // 2 - 1) as pair:
                step(2 * pair + 2, 0, True, True, True)
                step(2 * pair + 3, 1, True, True, True)
            step(BATCH, 0, False, True, True)
            step(BATCH + 1, 1, False, False, True)

        def nothing(*_):
            pass

        with nc.Block() as block:

            if later_loads is not None:
                block.sync(later_loads)

            @block.gpsimd
            def _(pool):
                for p in TWO:
                    pool.memset(v_st[p][:, :, :, DH:DH + 1], 1.0).then_inc(consts_set, 1)
                    pool.memset(v_st[p][:, :, :, DH + 1:VCOLS], 0.0).then_inc(consts_set, 1)

                def center(b, p):
                    pool.wait_ge(xn_ready, b + 1)
                    for c in range(CH):
                        pool.tensor_tensor(x_res[:, b * CH + c, :], x_res[:, b * CH + c, :], bo[:, :],
                                           ALU.add).then_inc(bias_added, 1)

                def spread_k(b, p, h):
                    if not isinstance(b, int) or b >= 2:
                        pool.wait_ge(st_done, HEADS * (b - 2) + h + 1)
                    pool.wait_ge(proj_lo, b * UNITS + h // 8 + 1)
                    mask = cst("group")[0:3 * QUAD, h % 4:h % 4 + 1].to_broadcast([3 * QUAD, SEQ])
                    pool.tensor_tensor(k_st[p][0:3 * QUAD, h, :], k_all[0:3 * QUAD, h // 4, :], mask, ALU.mult
                                       ).then_inc(k_spread, 1)

                def split(i, n):
                    pool.wait_ge(split_hi, 2 * i + n + 1)
                    hi, lo = split_w[n]
                    pool.tensor_tensor(lo[:, i, :], lo[:, i, :].bitcast(F32), hi[:, i, :].bitcast(F32),
                                       ALU.subtract).then_inc(split_lo, 1)

                def shifted(b, p, h):
                    if causal:
                        pool.wait_ge(exp_done, HEADS * b + h + 1)
                        pool.sem_inc(cut_begun, 1)
                        slot, at = (h - h % 2) % 8, (0, SEQ)[h % 2]
                        diag = probs[:, slot:slot + 2, at:at + P]
                        pool.affine_select(out=diag, in_=diag, compare_op=ALU.is_ge, fill=0.0, base=0,
                                           pattern=[[0, 2], [1, P]], channel_multiplier=-1).then_inc(cut_done, 1)

                pipeline(dict(center=center, norm=nothing, low=nothing, v=nothing, project=nothing, spread_k=spread_k,
                              scores=nothing, split=split, shifted=shifted, values=nothing, end=nothing,
                              shift=nothing, keep_shift=nothing), pool.Fori)

            @block.scalar
            def _(act):
                def norm(b, p):
                    act.wait_ge(xt_done, b + 1)
                    if causal:
                        behind(act, st_done, HEADS * (b - 1))
                    act.copy(x_hi[p][:, :], ps_p[1][:, 0:SEQ]).then_inc(xhi_ready, 1)

                def project(b, p, u):
                    act.wait_ge(proj_done, b * UNITS + u + 1)
                    if not causal and u < 2:
                        behind(act, k_spread, HEADS * b)
                    for r in range(2):
                        src = ps_p[u % 2][:, r * SEQ:(r + 1) * SEQ]
                        if causal:
                            h = 2 * u + r
                            dst, n, col = t_hi[p][:, h, :], P, h
                        elif u < 2:
                            dst, n, col = k_all[0:3 * QUAD, 2 * u + r, :].bitcast(F32R), 3 * QUAD, GROUPS + 2 * u + r
                        else:
                            dst, n, col = q_st[p][0:3 * QUAD, 2 * (u - 2) + r, :], 3 * QUAD, 2 * (u - 2) + r
                        last = act.activation(dst, src[0:n, :], ACT.Identity, bias=bias[0:n, col:col + 1])
                    last.then_inc(proj_hi, 1)

                def shifted(b, p, h):
                    n = HEADS * b + h
                    act.wait_ge(st_done, n + 1)
                    behind(act, o_done, GROUPS * b + h // 4 - 1)
                    if causal:
                        slot, width = (h - h % 2) % 8, (SEQ, P)[h % 2]
                        at = (0, SEQ)[h % 2]
                        act.activation(probs[:, slot:slot + 2, at:at + width],
                                       ps_st[h % 2][:, 0:2 * width].rearrange("p (n q) -> p n q", q=width),
                                       ACT.Exp, scale=scale).then_inc(exp_done, 1)
                    else:
                        act.activation(probs[:, h % 8, :], ps_st[h % 2][:, 0:ST_COLS], ACT.Exp, scale=scale
                                       ).then_inc(exp_done, 1)

                def keep_shift(b, p):
                    if not causal:
                        act.wait_ge(shift_set, 2 * b + 1)
                        for g in range(2, GROUPS):
                            last = act.copy(q_st[p][3 * QUAD:3 * QUAD + HEADS, g, :], ps_o[0:HEADS, 0:SEQ])
                        last.then_inc(shift_set, 1)

                def split(i, n):
                    hi, lo = split_w[n]
                    act.wait_ge(split_w[2], 3 * 16)
                    act.copy(hi[:, i, :], lo[:, i, :].bitcast(F32)).then_inc(split_hi, 1)

                def values(b, p, g, c):
                    if c < CH - 1:
                        return
                    act.wait_ge(o_done, GROUPS * b + g + 1)
                    act.copy(o_all[p][:, g, :], ps_o[:, 0:SEQ]).then_inc(o_kept, 1)

                def end(b, p, c, part, _):
                    if part == 1:
                        act.wait_ge(att_t_done, CH * b + c + 1)
                        act.copy(att_t[:, :], ps_x[:, 0:P]).then_inc(att_t_kept, 1)

                pipeline(dict(center=nothing, norm=norm, low=nothing, v=nothing, project=project, spread_k=nothing,
                              scores=nothing, split=split, shifted=shifted, values=values, end=end,
                              shift=nothing, keep_shift=keep_shift), act.Fori)

            @block.vector
            def _(dve):
                dve.memset(ps_o[:, :], 0.0).then_inc(consts_set, 1)
                if causal:
                    dve.tensor_copy(pick[:, :], ident[0:HEADS, 0:HEADS]).then_inc(consts_set, 1)

                def center(b, p):
                    behind(dve, xt_done, b)
                    for c in range(CH):
                        t = b * CH + c
                        mean = mean_var[:, t:t + 1, 0] if isinstance(t, int) else mean_var[:, bass.ds(t, 1), 0]
                        scl = rstd[:, t:t + 1] if isinstance(t, int) else rstd[:, bass.ds(t, 1)]
                        last = dve.tensor_scalar(xn[:, c, :], x_res[:, t, :], mean, scl, ALU.subtract, ALU.mult)
                    last.then_inc(xn_ready, 1)

                def low(b, p):
                    dve.wait_ge(xhi_ready, b + 1)
                    dve.tensor_tensor(x_lo[p][:, :], ps_p[1][:, 0:SEQ], x_hi[p][:, :].bitcast(F32),
                                      ALU.subtract).then_inc(xlo_ready, 1)

                def v(b, p):
                    dve.wait_ge(v_done, b + 1)
                    for c in range(CH):
                        last = dve.tensor_tensor(v_st[p][:, c, :, 0:DH],
                                                 ps_x[:, c * V_COLS:c * V_COLS + P].rearrange("p (h d) -> p h d", d=DH),
                                                 bv[:, :].rearrange("p (h d) -> p h d", d=DH), ALU.add)
                    if causal:
                        for c in range(CH):
                            at = c * V_COLS + P
                            last = dve.tensor_tensor(u_row[p][:, c, :], ps_x[:, at:at + HEADS], u_bias[:, :], ALU.add)
                    last.then_inc(v_ready, 1)

                def project(b, p, u):
                    dve.wait_ge(proj_hi, b * UNITS + u + 1)
                    for r in range(2):
                        src = ps_p[u % 2][:, r * SEQ:(r + 1) * SEQ]
                        if causal:
                            h = 2 * u + r
                            hi, lo, a, z, col = t_hi[p][:, h, :], t_lo[p][:, h, :], 0, P, h
                        elif u < 2:
                            a, z, col = 2 * QUAD, 3 * QUAD, GROUPS + 2 * u + r
                            hi = k_all[a:z, 2 * u + r, :].bitcast(F32R)
                            lo = hi
                        else:
                            a, z, col = QUAD, 2 * QUAD, 2 * (u - 2) + r
                            hi = q_st[p][a:z, 2 * (u - 2) + r, :]
                            lo = hi
                        last = dve.scalar_tensor_tensor(out=lo, in0=src[a:z, :], scalar=bias[a:z, col:col + 1],
                                                        in1=hi.bitcast(F32), op0=ALU.add, op1=ALU.subtract)
                    last.then_inc(proj_lo, 1)

                def scores(b, p, h):
                    dve.wait_ge(s_done, HEADS * b + h + 1)
                    if causal:
                        dve.tensor_reduce(row_max[p][:, h, 0:1], ps_s[h % 2][:, 0:P], AX_X, ALU.max)
                        dve.tensor_reduce(row_max[p][:, h, 1:2], ps_s[h % 2][:, P:P + SEQ], AX_X,
                                          ALU.max).then_inc(max_done, 1)
                    else:
                        dve.tensor_reduce(row_max[p][:, h, :], ps_s[h % 2][:, :].rearrange("p (c k) -> p c k", k=SEQ),
                                          AX_X, ALU.max).then_inc(max_done, 1)

                def shift_(b, p):
                    dve.wait_ge(max_done, HEADS * (b + 1))
                    if causal:
                        u = u_row[p][:, :, :].rearrange("p c h -> p h c")
                        dve.tensor_tensor(m_row[:, :, :], row_max[p][:, :, :], u, ALU.add).then_inc(m_done, 1)
                        dve.wait_ge(m_done, b + 1)
                        dve.tensor_tensor(shift[p][:, :, :], u, m_row[:, :, :], ALU.subtract).then_inc(shift_ready, 1)
                    else:
                        dve.tensor_scalar(shift[p][:, :, :], row_max[p][:, :, :], -1.0, None,
                                          ALU.mult).then_inc(shift_ready, 1)

                def keep_shift(b, p):
                    dve.wait_ge(shift_t_done, b + 1)
                    if causal:
                        behind(dve, st_done, HEADS * b)
                        dve.tensor_copy(neg_max[:, :], ps_o[0:HEADS, 0:SEQ]).then_inc(shift_set, 1)
                    else:
                        for g in range(2):
                            last = dve.tensor_copy(q_st[p][3 * QUAD:3 * QUAD + HEADS, g, :], ps_o[0:HEADS, 0:SEQ])
                        last.then_inc(shift_set, 1)

                def end(b, p, c, part, _):
                    n = CH * b + c
                    if part == 0:
                        dve.wait_ge(ot_done, n + 1)
                        o = ps_x[:, :].rearrange("p (h r) -> p h r", r=QUAD)
                        dve.reciprocal(r_inv[:, :], o[:, :, DH]).then_inc(rinv_done, 1)
                        dve.wait_ge(rinv_done, n + 1)
                        dve.tensor_tensor(att[:, :, :], o[:, :, 0:DH],
                                          r_inv[:, :].unsqueeze(2).to_broadcast([P, HEADS, DH]), ALU.mult
                                          ).then_inc(att_done, 1)
                    if part == 2:
                        dve.wait_ge(out_done, n + 1)
                        dve.wait_ge(bias_added, n + 1)
                        dve.tensor_tensor(x_res[:, n, :], ps_x[:, 0:P], x_res[:, n, :], ALU.add).then_inc(res_done, 1)
                        dve.wait_ge(res_done, n + 1)
                        dve.bn_stats(stats[:, n, :], x_res[:, n, :])

                pipeline(dict(center=center, norm=nothing, low=low, v=v, project=project, spread_k=nothing,
                              scores=scores, split=nothing, shifted=nothing, values=nothing, end=end,
                              shift=shift_, keep_shift=keep_shift), dve.Fori)

            @block.tensor
            def _(pe):
                pe.wait_ge(consts_set, N_CONST)

                def three(out, hi_l, lo_l, hi_r, lo_r, first=True, last=True):
                    pe.matmul(out, hi_l, hi_r, start=first, stop=False)
                    pe.matmul(out, hi_l, lo_r, start=False, stop=False)
                    return pe.matmul(out, lo_l, hi_r, start=False, stop=last)

                def norm(b, p):
                    pe.wait_ge(xn_ready, b + 1)
                    behind(pe, proj_lo, UNITS * b)
                    for c in range(CH):
                        last = pe.transpose(ps_p[1][:, c * P:(c + 1) * P], xn[:, c, :], ident)
                    last.then_inc(xt_done, 1)

                def v(b, p):
                    pe.wait_ge(xlo_ready, b + 1)
                    for c in range(CH):
                        cols = slice(c * P, (c + 1) * P)
                        last = three(ps_x[:, c * V_COLS:(c + 1) * V_COLS], x_hi[p][:, cols], x_lo[p][:, cols],
                                     wv_hi[:, :], wv_lo[:, :])
                    last.then_inc(v_done, 1)

                def project(b, p, u):
                    behind(pe, proj_lo, b * UNITS + u - 1)
                    if u == 0:
                        pe.wait_ge(xlo_ready, b + 1)
                    for r in range(2):
                        if causal:
                            cols, n = slice((2 * u + r) * P, (2 * u + r + 1) * P), P
                        else:
                            g = (GROUPS + 2 * u + r) if u < 2 else 2 * (u - 2) + r
                            cols, n = slice(g * 3 * QUAD, (g + 1) * 3 * QUAD), 3 * QUAD
                        last = three(ps_p[u % 2][0:n, r * SEQ:(r + 1) * SEQ], w_hi[:, cols], w_lo[:, cols],
                                     x_hi[p][:, :], x_lo[p][:, :])
                    last.then_inc(proj_done, 1)

                def scores(b, p, h):
                    behind(pe, max_done, HEADS * b + h - 1)
                    out = ps_s[h % 2]
                    if causal:
                        pe.wait_ge(proj_lo, b * UNITS + h // 2 + 1)
                        pe.matmul(out[:, 0:P], t_hi[p][:, h, 0:P], x_hi[p][:, 0:P], start=True, stop=False)
                        pe.matmul(out[:, 0:P], ident_bf, causal_bf, start=False, stop=True)
                        pe.matmul(out[:, P:P + SEQ], t_hi[p][:, h, P:SEQ], x_hi[p][:, :], start=True, stop=False)
                        last = pe.matmul(out[:, SEQ:SEQ + P], ident_bf, causal_bf, start=False, stop=True)
                    else:
                        pe.wait_ge(proj_lo, b * UNITS + 2 + h // 8 + 1)
                        pe.wait_ge(k_spread, HEADS * b + h + 1)
                        for c in range(CH):
                            last = pe.matmul(out[:, c * SEQ:(c + 1) * SEQ],
                                             q_st[p][0:3 * QUAD, h // 4, c * P:(c + 1) * P], k_st[p][0:3 * QUAD, h, :],
                                             start=True, stop=True)
                    last.then_inc(s_done, 1)

                def shift_(b, p):
                    pe.wait_ge(shift_ready, b + 1)
                    behind(pe, o_kept, GROUPS * b)
                    for c in range(CH):
                        last = pe.transpose(ps_o[0:HEADS, c * P:(c + 1) * P], shift[p][:, :, c], ident)
                    last.then_inc(shift_t_done, 1)

                def shifted(b, p, h):
                    n = HEADS * b + h
                    if h == 0:
                        pe.wait_ge(shift_set, b + 1 if causal else 2 * b + 2)
                    behind(pe, exp_done, n - 1)
                    out = ps_st[h % 2]
                    if causal:
                        keys = slice(P * (h % 2), P * (h % 2) + P)
                        pair, width = h - h % 2, (SEQ, P)[h % 2]
                        q = slice(SEQ - width, SEQ)
                        both = out[:, 0:2 * width].rearrange("p (n q) -> p n q", q=width)
                        three(both, x_hi[p][:, keys], x_lo[p][:, keys], t_hi[p][:, pair:pair + 2, q],
                              t_lo[p][:, pair:pair + 2, q], last=False)
                        for n in range(2):
                            one = pair + n
                            last = pe.matmul(both[:, n, :], pick[:, one:one + 1].to_broadcast([HEADS, P]),
                                             neg_max[:, q], start=False, stop=(n == 1))
                    else:
                        for c in range(CH):
                            last = pe.matmul(out[:, c * SEQ:(c + 1) * SEQ], k_st[p][:, h, c * P:(c + 1) * P],
                                             q_st[p][:, h // 4, :], start=True, stop=True)
                    last.then_inc(st_done, 1)

                def values(b, p, g, c):
                    n = GROUPS * b + g
                    if c == 0:
                        pe.wait_ge(probs_ready, 4 * (n + 1))
                        pe.wait_ge(v_ready, b + 1)
                        behind(pe, o_kept, n)
                    for k in range(4):
                        pr = probs[:, 4 * (g % 2) + k, :]
                        rows = slice(k * QUAD, k * QUAD + VCOLS)
                        if causal and c == 1:
                            out, pr = ps_o[rows, P:SEQ], pr[:, SEQ:SEQ + P]
                        else:
                            out, pr = ps_o[rows, 0:SEQ], pr[:, c * SEQ:(c + 1) * SEQ]
                        last = pe.matmul(out, v_st[p][:, c, 4 * g + k, :], pr, start=(c == 0), stop=(c == CH - 1))
                    if c == CH - 1:
                        last.then_inc(o_done, 1)

                def end(b, p, c, part, i):
                    n = CH * b + c
                    if part == 0:
                        pe.wait_ge(o_kept, GROUPS * (b + 1))
                        if c == 1:
                            pe.wait_ge(res_done, n)
                        elif i is not None:
                            pe.wait_ge(v_ready, i + 1)
                        else:
                            behind(pe, res_done, n)
                        for g in range(GROUPS):
                            last = pe.transpose(ps_x[:, g * P:(g + 1) * P], o_all[p][:, g, c * P:(c + 1) * P], ident)
                        last.then_inc(ot_done, 1)
                    elif part == 1:
                        pe.wait_ge(att_done, n + 1)
                        pe.transpose(ps_x[:, 0:P], att[:, :, :].rearrange("p h d -> p (h d)"), ident).then_inc(att_t_done, 1)
                    else:
                        pe.wait_ge(att_t_kept, n + 1)
                        pe.matmul(ps_x[:, 0:P], att_t[:, :], wo[:, :], start=True, stop=True).then_inc(out_done, 1)

                pipeline(dict(center=nothing, norm=norm, low=nothing, v=v, project=project, spread_k=nothing,
                              scores=scores, split=nothing, shifted=shifted, values=values, end=end,
                              shift=shift_, keep_shift=nothing), pe.Fori)


class CausalWeights:

    def __init__(self, nc, ctx, kept, weights):
        self.nc, self.ctx, self.weights = nc, ctx, weights
        self.probs = self.sb("probs", [P, 8, SEQ + P], F32)
        self.o_all0 = self.sb("o_all0", [P, GROUPS, SEQ], F32)
        flat = self.probs[:, :, :].rearrange("p a b -> p (a b)")
        HALF = HEADS // 2
        self.wqT = flat[:, 0:HEADS * P].rearrange("p (h k) -> p h k", k=P)
        self.wkT = [flat[:, HEADS * P:(HEADS + HALF) * P].rearrange("p (h k) -> p h k", k=P),
                    self.o_all0[:, :, :].rearrange("p g (h k) -> p (g h) k", k=P)]
        self.wv, self.wo, self.bv, self.bo = (self.sb(n, [P, P], F32) for n in ("wv", "wo", "bv", "bo"))
        self.bq, self.bk, self.bqk = (self.sb(n, [P, HEADS], F32) for n in ("bq", "bk", "bqk"))
        self.loaded, self.bqk_made, self.m_made, self.m_kept, self.w_made, self.hi_made = (
            kept.enter_context(nc.semaphore(f"cw_{n}")) for n in ("loaded", "bqk_made", "m_made", "m_kept", "w_made", "hi_made"))

    def sb(self, name, shape, dt):
        return self.ctx.enter_context(self.nc.sbuf_tensor(f"cw_{name}", shape, dt))

    def load(self, sp):
        half = HEADS // 2
        for n in range(2):
            sp.dma_start(self.wkT[n], self.weights["wkT"][:, n * half:(n + 1) * half, :]).then_inc(self.loaded, 16)
        for dst, name in ((self.wqT, "wqT"), (self.bq[:, :], "bq"), (self.bk[:, :], "bk"),
                          (self.wv[:, :], "wv"), (self.wo[:, :], "wo"), (self.bv[:, :], "bv"), (self.bo[:, :], "bo")):
            sp.dma_start(dst, self.weights[name]).then_inc(self.loaded, 16)

    def make_room(self):
        self.w_hi, self.w_lo = (self.sb(n, [P, HEADS * P], F32R) for n in ("w_hi", "w_lo"))
        self.wv_hi, self.wv_lo = (self.sb(n, [P, P + HEADS], F32R) for n in ("wv_hi", "wv_lo"))
        self.bias, self.u_bias = (self.sb(n, [P, HEADS], F32) for n in ("bias", "u_bias"))
        self.o_all1 = self.sb("o_all1", [P, GROUPS, SEQ], F32)
        self.v_st = [self.sb(f"v_st{p}", [P, CH, HEADS, VCOLS], F32) for p in range(2)]
        self.m = [self.o_all1[:, 0:2, :].rearrange("p a b -> p (a b)"), self.o_all1[:, 2:4, :].rearrange("p a b -> p (a b)"),
                  self.v_st[0][:, :, :, :].rearrange("p c h v -> p (c h v)"), self.v_st[1][:, :, :, :].rearrange("p c h v -> p (c h v)")]

    def key_weights(self, h):
        return self.wkT[h // (HEADS // 2)][:, h % (HEADS // 2), :]

    def products(self, pe, q, bank):
        if q == 0:
            pe.wait_ge(self.loaded, 9 * 16)
        behind(pe, self.m_kept, q - 1)
        for n in range(4):
            last = pe.matmul(bank[:, n * P:(n + 1) * P], self.wqT[:, 4 * q + n, :], self.key_weights(4 * q + n),
                             start=True, stop=True)
        last.then_inc(self.m_made, 1)

    def keep(self, act, q, bank):
        cols = slice(q * 4 * P, (q + 1) * 4 * P)
        act.wait_ge(self.m_made, q + 1)
        act.copy(self.w_hi[:, cols], bank[:, :])
        act.copy(self.m[q], bank[:, :]).then_inc(self.m_kept, 1)

    def low(self, pool):
        pool.wait_ge(self.loaded, 9 * 16)
        pool.tensor_tensor(self.bqk[:, :], self.bq[:, :], self.bk[:, :], ALU.mult).then_inc(self.bqk_made, 1)
        for q in range(HEADS // 4):
            cols = slice(q * 4 * P, (q + 1) * 4 * P)
            pool.wait_ge(self.m_kept, q + 1)
            pool.tensor_tensor(self.w_lo[:, cols], self.m[q], self.w_hi[:, cols].bitcast(F32), ALU.subtract)

    def key_biases(self, pe, bank):
        for h in range(HEADS):
            pe.matmul(bank[:, h:h + 1], self.key_weights(h), self.bq[:, h:h + 1], start=True, stop=True)

    def row_biases(self, pe, bank, ones):
        for h in range(HEADS):
            pe.matmul(bank[:, HEADS + h:HEADS + h + 1], self.wqT[:, h, :], self.bk[:, h:h + 1], start=True, stop=True)
        pe.wait_ge(self.bqk_made, 1)
        pe.matmul(bank[:, 2 * HEADS:3 * HEADS], ones, self.bqk[:, :], start=True, stop=True).then_inc(self.w_made, 1)

    def keep_biases(self, act, bank):
        act.copy(self.wv_hi[:, 0:P], self.wv[:, :])
        act.wait_ge(self.w_made, 1)
        act.copy(self.bias[:, :], bank[:, 0:HEADS])
        act.copy(self.u_bias[:, :], bank[:, 2 * HEADS:3 * HEADS])
        act.copy(self.wv_hi[:, P:P + HEADS], bank[:, HEADS:2 * HEADS]).then_inc(self.hi_made, 1)

    def low_biases(self, dve, bank):
        dve.wait_ge(self.hi_made, 1)
        dve.tensor_tensor(self.wv_lo[:, P:P + HEADS], bank[:, HEADS:2 * HEADS], self.wv_hi[:, P:P + HEADS].bitcast(F32),
                          ALU.subtract)
        dve.tensor_tensor(self.wv_lo[:, 0:P], self.wv[:, :], self.wv_hi[:, 0:P].bitcast(F32), ALU.subtract)


def experts(nc, kept, layer, x_res, mean_var, rstd, stats, cst, ident, ones_bf, below_bf, gate_w, up_w, down_w, router_w,
            router_b, moe_consts, xn_dram, y_dram, rings, beside=None, last_layer=False):
    with ExitStack() as ctx:
        def sb(name, shape, dt):
            return ctx.enter_context(nc.sbuf_tensor(f"m{layer}_{name}", shape, dt))

        def sem(name):
            return kept.enter_context(nc.semaphore(f"m{layer}_{name}"))

        tables = sb("tables", [P, MOE_COLS], F32)
        tables_in = sem("tables_in")

        def load_tables(sp):
            sp.dma_start(tables[:, :], moe_consts).then_inc(tables_in, 16)
            sp.wait_ge(tables_in, 16)

        layer_norm_stats(nc, sem, x_res, mean_var, stats, rstd[:, :], {"sync": load_tables})

        def table(name):
            return tables[:, MOE_CONST[name][0]:MOE_CONST[name][1]]

        gates = sb("gates", [P, TOPK, TILES], F32)
        turn_experts = sb("turn_experts", [P, SLOT_TILES // RING], I32)
        src_row = sb("src_row", [P, SLOT_TILES], U32)
        dst_row = sb("dst_row", [P, SLOT_TILES], U32)
        xs = [sb(f"xs{j}", [P, P], F32) for j in range(RING)]
        in_landed, out_landed, got, first_added, second_added = rings
        BEFORE = 16 * layer * (SLOT_TILES // RING)
        shape = [P, TILES, EXPERTS]

        def gather(pool, t):
            pool.indirect_dma_start(out=xs[t % RING][:, :], out_offset=None, in_=xn_dram[:, :],
                                    in_offset=bass.IndirectOffsetOnAxis(ap=src_row[:, t:t + 1], axis=0)
                                    ).then_inc(in_landed[t % RING], 16)

        with ExitStack() as rctx:
            def rb(name, shape, dt):
                return rctx.enter_context(nc.sbuf_tensor(f"m{layer}_{name}", shape, dt))

            PAIRS = TOPK * TILES
            xn = rb("xn", [P, TILES, P], F32)
            xt = rb("xt", [P, TILES, P], F32)
            logits = rb("logits", shape, F32)
            left = rb("left", shape, F32)
            chosen = rb("chosen", [P, TOPK] + shape[1:], F32)
            both = rb("both", shape, BF16)
            key = rb("key", shape, F32)
            top = rb("top", [P, TOPK, TILES], F32)
            rank = rb("rank", [P, TOPK, TILES], F32)
            drop = rb("drop", [P, TILES], F32)
            ex = rb("ex", [P, TILES], F32)
            den = rb("den", [P, TILES], F32)
            over = rb("over", [P, EXPERTS, TILES], F32)
            n_tiles = rb("n_tiles", [P, EXPERTS], F32)
            upto = rb("upto", [P, EXPERTS, EXPERTS], F32)
            end_tile = rb("end_tile", [P, EXPERTS], F32)
            first_slot = rb("first_slot", [P, EXPERTS], F32)
            place = rb("place", shape, F32)
            placed = rb("placed", [P, TOPK] + shape[1:], F32)
            slot_f = rb("slot_f", [P, PAIRS], F32)
            slot_i = rb("slot_i", [P, PAIRS], I32)
            in_tile_i = rb("in_tile_i", [P, PAIRS], I32)
            tile_i = rb("tile_i", [P, PAIRS], I32)
            in_tile = rb("in_tile", [P, PAIRS], F32)
            tile_of = rb("tile_of", [P, PAIRS], F32)
            row_is = rb("row_is", [P, PAIRS, P], BF16)
            tile_is = rb("tile_is", [P, PAIRS, SLOT_TILES], F32)
            named = rb("named", [P, PAIRS, 2, SLOT_TILES], BF16)
            found = rb("found", [P, SLOT_TILES], F32)
            second = rb("second", [P, SLOT_TILES], F32)
            padding = rb("padding", [P, SLOT_TILES], F32)
            token = rb("token", [P, SLOT_TILES], F32)
            past = rb("past", [P, SLOT_TILES, EXPERTS], F32)
            tile_expert = rb("tile_expert", [P, 1 + SLOT_TILES], F32)
            digits = rb("digits", [P, SLOT_TILES // RING, RING], F32)
            word = rb("word", [P, SLOT_TILES // RING], F32)
            ps_t = [rctx.enter_context(nc.psum_tensor(f"m{layer}_ps_t{i}", [P, 512], F32)) for i in range(2)]
            ps_m = [rctx.enter_context(nc.psum_tensor(f"m{layer}_ps_m{i}", [P, 512], F32)) for i in range(2)]
            ps_l = rctx.enter_context(nc.psum_tensor(f"m{layer}_ps_l", [P, 512], F32))
            ps_n = rctx.enter_context(nc.psum_tensor(f"m{layer}_ps_n", [P, 512], F32))
            ps_c = rctx.enter_context(nc.psum_tensor(f"m{layer}_ps_c", [P, 512], F32))
            ps_w = rctx.enter_context(nc.psum_tensor(f"m{layer}_ps_w", [P, 512], F32))
            xn_ready, xt_done, xt_kept, logits_done = sem("xn_ready"), sem("xt_done"), sem("xt_kept"), sem("logits_done")
            link, gap_ready, ex_done = sem("link"), sem("gap_ready"), sem("ex_done")
            both_ready, counted, xn_written = sem("both_ready"), sem("counted"), sem("xn_written")
            tiles_known, row_known, named_lo, named_hi, found_done, rows_ready = (
                sem("tiles_known"), sem("row_known"), sem("named_lo"), sem("named_hi"), sem("found_done"), sem("rows_ready"))
            TPB = 4

            with nc.Block() as block:

                @block.sync
                def _(sp):
                    for q in range(TILES // TPB):
                        sp.wait_ge(xn_ready, (q + 1) * TPB)
                        sp.dma_start(xn_dram[q * TPB * P:(q + 1) * TPB * P, :].rearrange("(t p) d -> p t d", p=P),
                                     xn[:, q * TPB:(q + 1) * TPB, :]).then_inc(xn_written, 16)

                @block.vector
                def _(dve):
                    done = [0]

                    def then(instruction):
                        done[0] += 1
                        instruction.then_inc(link, 1)
                        dve.wait_ge(link, done[0])

                    for t in range(TILES):
                        dve.tensor_scalar(xn[:, t, :], x_res[:, t, :], mean_var[:, t, 0:1], rstd[:, t:t + 1],
                                          ALU.subtract, ALU.mult).then_inc(xn_ready, 1)
                    dve.wait_ge(logits_done, 1)
                    wide = lambda a: a.unsqueeze(2).to_broadcast(shape)
                    rb_wide = router_b[:, :].unsqueeze(1).to_broadcast(shape)
                    rank_wide = table("rank").unsqueeze(1).to_broadcast(shape)
                    then(dve.tensor_tensor(logits[:, :, :], ps_l[:, 0:TILES * EXPERTS].rearrange("p (t e) -> p t e", e=EXPERTS),
                                           rb_wide, ALU.add))
                    src = logits
                    for k in range(TOPK):
                        then(dve.tensor_reduce(top[:, k, :], src[:, :, :], AX_X, ALU.max))
                        then(dve.tensor_tensor(key[:, :, :], src[:, :, :], wide(top[:, k, :]), ALU.is_equal))
                        then(dve.tensor_tensor(key[:, :, :], key[:, :, :], rank_wide, ALU.mult))
                        then(dve.tensor_reduce(rank[:, k, :], key[:, :, :], AX_X, ALU.max))
                        then(dve.tensor_tensor(chosen[:, k, :, :], rank_wide, wide(rank[:, k, :]), ALU.is_equal))
                        if k == 0:
                            then(dve.scalar_tensor_tensor(out=left[:, :, :].rearrange("p t e -> p (t e)"),
                                                          in0=chosen[:, 0, :, :].rearrange("p t e -> p (t e)"),
                                                          scalar=-3.0e38, in1=logits[:, :, :].rearrange("p t e -> p (t e)"),
                                                          op0=ALU.mult, op1=ALU.add))
                            src = left
                    dve.tensor_tensor(both[:, :, :], chosen[:, 0, :, :], chosen[:, 1, :, :], ALU.add).then_inc(both_ready, 1)
                    dve.tensor_tensor(drop[:, :], top[:, 1, :], top[:, 0, :], ALU.subtract).then_inc(gap_ready, 1)
                    dve.wait_ge(counted, 1)
                    then(dve.tensor_tensor(over[:, :, :], ps_c[:, 0:EXPERTS].unsqueeze(2).to_broadcast([P, EXPERTS, TILES]),
                                           table("full").unsqueeze(1).to_broadcast([P, EXPERTS, TILES]), ALU.is_gt))
                    then(dve.tensor_reduce(n_tiles[:, :], over[:, :, :], AX_X, ALU.add))
                    then(dve.tensor_tensor(upto[:, :, :], n_tiles[:, :].unsqueeze(1).to_broadcast([P, EXPERTS, EXPERTS]),
                                           table("upto").rearrange("p (a b) -> p a b", b=EXPERTS), ALU.mult))
                    then(dve.tensor_reduce(end_tile[:, :], upto[:, :, :], AX_X, ALU.add))
                    then(dve.tensor_tensor(first_slot[:, :], end_tile[:, :], n_tiles[:, :], ALU.subtract))
                    then(dve.tensor_scalar(first_slot[:, :], first_slot[:, :], float(P), None, ALU.mult))
                    dve.wait_ge(counted, 2)
                    then(dve.tensor_tensor(place[:, :, :], ps_n[:, 0:TILES * EXPERTS].rearrange("p (t e) -> p t e", e=EXPERTS),
                                           first_slot[:, :].unsqueeze(1).to_broadcast(shape), ALU.add))
                    then(dve.tensor_tensor(placed[:, :, :, :], chosen[:, :, :, :],
                                           place[:, :, :].unsqueeze(1).to_broadcast([P, TOPK] + shape[1:]), ALU.mult))
                    then(dve.tensor_reduce(slot_f[:, :], placed[:, :, :, :].rearrange("p k t e -> p (k t) e"), AX_X, ALU.add))
                    then(dve.tensor_copy(slot_i[:, :], slot_f[:, :]))
                    then(dve.tensor_scalar(tile_i[:, :], slot_i[:, :], P.bit_length() - 1, None, ALU.arith_shift_right))
                    then(dve.tensor_scalar(in_tile_i[:, :], slot_i[:, :], P - 1, None, ALU.bitwise_and))
                    then(dve.tensor_copy(tile_of[:, :], tile_i[:, :]))
                    then(dve.tensor_copy(in_tile[:, :], in_tile_i[:, :]))
                    dve.tensor_tensor(tile_is[:, :, :], tile_of[:, :].unsqueeze(2).to_broadcast([P, PAIRS, SLOT_TILES]),
                                      table("tile_no").unsqueeze(1).to_broadcast([P, PAIRS, SLOT_TILES]), ALU.is_equal
                                      ).then_inc(tiles_known, 1)
                    for k in range(TOPK):
                        half = slice(k * TILES, (k + 1) * TILES)
                        dve.tensor_tensor(row_is[:, half, :], in_tile[:, half].unsqueeze(2).to_broadcast([P, TILES, P]),
                                          table("row_no").unsqueeze(1).to_broadcast([P, TILES, P]), ALU.is_equal
                                          ).then_inc(row_known, 1)
                    then(dve.tensor_tensor(past[:, :, :], table("tile_no").unsqueeze(2).to_broadcast([P, SLOT_TILES, EXPERTS]),
                                           end_tile[:, :].unsqueeze(1).to_broadcast([P, SLOT_TILES, EXPERTS]), ALU.is_ge))
                    dve.memset(tile_expert[:, 0:1], 0.0)
                    then(dve.tensor_reduce(tile_expert[:, 1:], past[:, :, :], AX_X, ALU.add))
                    then(dve.tensor_scalar(tile_expert[:, :], tile_expert[:, :], float(EXPERTS - 1), None, ALU.min))
                    then(dve.tensor_tensor(digits[:, :, :], tile_expert[:, 1:].rearrange("p (q n) -> p q n", n=RING),
                                           table("digit").rearrange("p (q n) -> p q n", n=RING), ALU.mult))
                    then(dve.tensor_reduce(word[:, :], digits[:, :, :], AX_X, ALU.add))
                    then(dve.tensor_tensor(turn_experts[:, :], word[:, :], tile_expert[:, 0:SLOT_TILES:RING], ALU.add))
                    dve.wait_ge(found_done, 1)
                    hi, lo = ps_w[:, SLOT_TILES:2 * SLOT_TILES], found
                    then(dve.tensor_copy(found[:, :], ps_w[:, 0:SLOT_TILES]))
                    then(dve.scalar_tensor_tensor(out=found[:, :], in0=hi, scalar=float(P), in1=lo[:, :], op0=ALU.mult, op1=ALU.add))
                    dve.tensor_scalar(second[:, :], found[:, :], float(P + TOKENS), float(TOKENS), ALU.is_ge, ALU.mult)
                    then(dve.tensor_scalar(token[:, :], found[:, :], float(P), 0.0, ALU.subtract, ALU.max))
                    dve.tensor_tensor(src_row[:, :], token[:, :], second[:, :], ALU.subtract).then_inc(rows_ready, 1)
                    then(dve.scalar_tensor_tensor(out=padding[:, :], in0=found[:, :], scalar=0.0, in1=table("pad_row"),
                                                  op0=ALU.is_equal, op1=ALU.mult))
                    then(dve.scalar_tensor_tensor(out=dst_row[:, :], in0=found[:, :], scalar=float(P), in1=padding[:, :],
                                                  op0=ALU.subtract, op1=ALU.add))
                    dve.wait_ge(ex_done, 1)
                    then(dve.tensor_scalar(den[:, :], ex[:, :], 1.0, None, ALU.add))
                    then(dve.reciprocal(gates[:, 0, :], den[:, :]))
                    then(dve.tensor_tensor(gates[:, 1, :], gates[:, 0, :], ex[:, :], ALU.mult))
                    if beside is not None:
                        beside.low_biases(dve, ps_l)

                @block.scalar
                def _(act):
                    if beside is not None:
                        beside.keep(act, 0, ps_m[0])
                        beside.keep(act, 1, ps_m[1])
                    for q in range(TILES // TPB):
                        act.wait_ge(xt_done, q + 1)
                        act.copy(xt[:, q * TPB:(q + 1) * TPB, :], ps_t[q % 2][:, :].rearrange("p (t k) -> p t k", k=P)
                                 ).then_inc(xt_kept, 1)
                    if beside is not None:
                        beside.keep(act, 2, ps_m[0])
                        beside.keep(act, 3, ps_m[1])
                    act.wait_ge(gap_ready, 1)
                    act.activation(ex[:, :], drop[:, :], ACT.Exp).then_inc(ex_done, 1)
                    act.wait_ge(tiles_known, 1)
                    act.activation(named[:, :, 0, :], tile_is[:, :, :], ACT.Copy, scale=table("part_no")).then_inc(named_lo, 1)
                    if beside is not None:
                        beside.keep_biases(act, ps_l)

                @block.tensor
                def _(pe):
                    if beside is not None:
                        beside.products(pe, 0, ps_m[0])
                        beside.products(pe, 1, ps_m[1])
                    for q in range(TILES // TPB):
                        pe.wait_ge(xn_ready, (q + 1) * TPB)
                        behind(pe, xt_kept, q - 1)
                        for t in range(TPB):
                            last = pe.transpose(ps_t[q % 2][:, t * P:(t + 1) * P], xn[:, q * TPB + t, :], ident)
                        last.then_inc(xt_done, 1)
                    for t in range(TILES):
                        if t % TPB == 0:
                            pe.wait_ge(xt_kept, t // TPB + 1)
                        last = pe.matmul(ps_l[:, t * EXPERTS:(t + 1) * EXPERTS], xt[:, t, :], router_w[:, :],
                                         start=True, stop=True)
                    last.then_inc(logits_done, 1)
                    if beside is not None:
                        beside.products(pe, 2, ps_m[0])
                        beside.products(pe, 3, ps_m[1])
                    pe.wait_ge(both_ready, 1)
                    for t in range(TILES):
                        last = pe.matmul(ps_c[:, 0:EXPERTS], ones_bf, both[:, t, :], start=(t == 0), stop=(t == TILES - 1))
                    last.then_inc(counted, 1)
                    before = ps_n[:, 0:TILES * EXPERTS].rearrange("p (t e) -> p t e", e=EXPERTS)
                    pe.matmul(before, below_bf, both[:, :, :], start=True, stop=False)
                    for t in range(TILES - 1):
                        n = TILES - 1 - t
                        last = pe.matmul(before[:, t + 1:TILES, :], ones_bf, both[:, t:t + 1, :].to_broadcast([P, n, EXPERTS]),
                                         start=False, stop=(t == TILES - 2))
                    last.then_inc(counted, 1)
                    if beside is not None:
                        beside.key_biases(pe, ps_l)
                    pe.wait_ge(named_lo, 1)
                    pe.wait_ge(named_hi, 1)
                    for j in range(PAIRS):
                        if j % TILES == 0:
                            pe.wait_ge(row_known, j // TILES + 1)
                        last = pe.matmul(ps_w[:, 0:2 * SLOT_TILES], row_is[:, j, :],
                                         named[:, j, :, :].rearrange("p n a -> p (n a)"),
                                         start=(j == 0), stop=(j == PAIRS - 1))
                    last.then_inc(found_done, 1)
                    if beside is not None:
                        beside.row_biases(pe, ps_l, cst("ones"))

                @block.gpsimd
                def _(pool):
                    if beside is not None:
                        beside.low(pool)
                    pool.wait_ge(tiles_known, 1)
                    pool.tensor_tensor(named[:, :, 1, :], tile_is[:, :, :],
                                       table("pair_no").unsqueeze(2).to_broadcast([P, PAIRS, SLOT_TILES]), ALU.mult
                                       ).then_inc(named_hi, 1)
                    pool.wait_ge(xn_written, 16 * (TILES // TPB))
                    pool.wait_ge(rows_ready, 1)
                    for t in range(RING):
                        gather(pool, t)

        with ExitStack() as ectx:
            def eb(name, shape, dt):
                return ectx.enter_context(nc.sbuf_tensor(f"m{layer}_{name}", shape, dt))

            TWO = range(2)
            HALF = FF // 2
            xs_hi = [eb(f"xs_hi{p}", [P, P], F32R) for p in TWO]
            xs_lo = [eb(f"xs_lo{p}", [P, P], F32R) for p in TWO]
            act_g = [eb(f"act_g{p}", [P, FF], F32) for p in TWO]
            hid = [eb(f"hid{p}", [P, FF], F32) for p in TWO]
            hid_t = [eb(f"hid_t{p}", [P, FF], F32) for p in TWO]
            ys = [eb(f"ys{j}", [P, P], F32) for j in range(RING)]
            y = eb("y", [P, TOPK, TILES, P], F32)
            ps = [ectx.enter_context(nc.psum_tensor(f"m{layer}_ps{i}", [P, 512], F32)) for i in range(8)]
            ps_g, ps_u, ps_h, ps_x, ps_y = ps[0:2], ps[2:4], ps[4:6], ps[6], ps[7]
            t_done, hi_ready, lo_ready, gate_done, up_done, silu_done = (
                sem("t_done"), sem("hi_ready"), sem("lo_ready"), sem("gate_done"), sem("up_done"), sem("silu_done"))
            hid_ready, ht_done, front_kept, back_kept, y_done, y_kept = (
                sem("hid_ready"), sem("ht_done"), sem("front_kept"), sem("back_kept"), sem("y_done"), sem("y_kept"))
            QUADS = SLOT_TILES // RING

            def quads(step, Fori):
                for j in range(RING):
                    step(0, j)
                with Fori(1, QUADS - 1) as quad:
                    for j in range(RING):
                        step(quad, j)
                for j in range(RING):
                    step(QUADS - 1, j)

            with nc.Block() as block:

                @block.tensor
                def _(pe):
                    expert = {}

                    def load_experts(quad, first):
                        word = pe.value_load(turn_experts[0:1, bass.ds(quad, 1)], min_val=0, max_val=EXPERTS ** (RING + 1) - 1)
                        for n in range(0 if first else -1, RING):
                            expert[n] = (word >> (3 * (n + 1))) & (EXPERTS - 1)

                    def turn(t, quad, j):
                        pe.wait_ge(in_landed[j % RING], BEFORE + 16 * (quad + j // RING) + 16)
                        pe.transpose(ps_x[:, 0:P], xs[j % RING][:, :], ident).then_inc(t_done, 1)

                    def product(out, p, w, e):
                        pe.matmul(out[:, :], xs_hi[p][:, :], w[0][:, e, :], start=True, stop=False)
                        pe.matmul(out[:, :], xs_hi[p][:, :], w[1][:, e, :], start=False, stop=False)
                        return pe.matmul(out[:, :], xs_lo[p][:, :], w[0][:, e, :], start=False, stop=True)

                    def back(t, p):
                        for f in range(FCH):
                            last = pe.transpose(ps_h[f // 2][:, (f % 2) * P:(f % 2 + 1) * P], hid[p][:, f * P:(f + 1) * P], ident)
                        last.then_inc(ht_done, 1)

                    def down(t, p, e):
                        pe.wait_ge(front_kept, t + 1)
                        pe.wait_ge(back_kept, t + 1)
                        behind(pe, y_kept, t)
                        for f in range(FCH):
                            last = pe.matmul(ps_y[:, 0:P], hid_t[p][:, f * P:(f + 1) * P],
                                             down_w[:, e, f * P:(f + 1) * P], start=(f == 0), stop=(f == FCH - 1))
                        last.then_inc(y_done, 1)

                    def step(quad, j):
                        t, p = RING * quad + j, j % 2
                        first = isinstance(t, int) and t == 0
                        final = isinstance(t, int) and t == SLOT_TILES - 1
                        if j == 0:
                            load_experts(quad, first)
                        pe.wait_ge(lo_ready, t + 1)
                        product(ps_g[p], p, gate_w, expert[j]).then_inc(gate_done, 1)
                        if not first:
                            pe.wait_ge(hid_ready, t)
                            back(t - 1, 1 - p)
                        if not final:
                            turn(t + 1, quad, j + 1)
                        product(ps_u[p], p, up_w, expert[j]).then_inc(up_done, 1)
                        if not first:
                            down(t - 1, 1 - p, expert[j - 1])

                    turn(0, 0, 0)
                    quads(step, pe.Fori)
                    pe.wait_ge(hid_ready, SLOT_TILES)
                    back(SLOT_TILES - 1, 1)
                    down(SLOT_TILES - 1, 1, expert[RING - 1])

                @block.scalar
                def _(act):
                    def high(t, p):
                        act.wait_ge(t_done, t + 1)
                        act.copy(xs_hi[p][:, :], ps_x[:, 0:P]).then_inc(hi_ready, 1)

                    def front(t, p):
                        act.wait_ge(ht_done, t + 1)
                        act.copy(hid_t[p][:, 0:HALF], ps_h[0][:, 0:HALF]).then_inc(front_kept, 1)

                    def step(quad, j):
                        t, p = RING * quad + j, j % 2
                        act.wait_ge(gate_done, t + 1)
                        act.activation(act_g[p][:, :], ps_g[p][:, :], ACT.Silu).then_inc(silu_done, 1)
                        if not (isinstance(t, int) and t == 0):
                            front(t - 1, 1 - p)
                        if not (isinstance(t, int) and t == SLOT_TILES - 1):
                            high(t + 1, 1 - p)

                    high(0, 0)
                    quads(step, act.Fori)
                    front(SLOT_TILES - 1, 1)

                @block.vector
                def _(dve):
                    def low(t, p):
                        dve.wait_ge(hi_ready, t + 1)
                        dve.tensor_tensor(xs_lo[p][:, :], ps_x[:, 0:P], xs_hi[p][:, :].bitcast(F32),
                                          ALU.subtract).then_inc(lo_ready, 1)

                    def rest(t, p):
                        dve.wait_ge(ht_done, t + 1)
                        dve.tensor_copy(hid_t[p][:, HALF:FF], ps_h[1][:, 0:HALF]).then_inc(back_kept, 1)

                    def keep(quad, j, t):
                        dve.wait_ge(y_done, t + 1)
                        if not (isinstance(quad, int) and quad == 0):
                            dve.wait_ge(out_landed[j], BEFORE + 16 * quad)
                        dve.tensor_copy(ys[(j - 1) % RING][:, :], ps_y[:, 0:P]).then_inc(y_kept, 1)

                    def step(quad, j):
                        t, p = RING * quad + j, j % 2
                        first = isinstance(t, int) and t == 0
                        if not first:
                            rest(t - 1, 1 - p)
                        if not (isinstance(t, int) and t == SLOT_TILES - 1):
                            low(t + 1, 1 - p)
                        dve.wait_ge(silu_done, t + 1)
                        dve.wait_ge(up_done, t + 1)
                        dve.tensor_tensor(hid[p][:, :], ps_u[p][:, :], act_g[p][:, :], ALU.mult).then_inc(hid_ready, 1)
                        if not first:
                            keep(quad, j, t - 1)

                    low(0, 0)
                    quads(step, dve.Fori)
                    rest(SLOT_TILES - 1, 1)
                    keep(QUADS, 0, SLOT_TILES - 1)
                    for t in range(TILES):
                        if t % 4 == 0:
                            dve.wait_ge(got[t // 4], 16 * TOPK * (layer + 1))
                        dve.scalar_tensor_tensor(out=x_res[:, t, :], in0=y[:, 0, t, :], scalar=gates[:, 0, t:t + 1],
                                                 in1=x_res[:, t, :], op0=ALU.mult, op1=ALU.add).then_inc(first_added, 1)
                        if t % 4 == 3:
                            for u in range(t - 3, t + 1):
                                dve.wait_ge(first_added, layer * TILES + u + 1)
                                dve.scalar_tensor_tensor(out=x_res[:, u, :], in0=y[:, 1, u, :], scalar=gates[:, 1, u:u + 1],
                                                         in1=x_res[:, u, :], op0=ALU.mult, op1=ALU.add).then_inc(second_added, 1)
                            for u in range(t - 3, t + 1):
                                if not last_layer:
                                    dve.wait_ge(second_added, layer * TILES + u + 1)
                                    dve.bn_stats(stats[:, u, :], x_res[:, u, :])

                @block.gpsimd
                def _(pool):
                    for t in range(SLOT_TILES + 2):
                        if t + RING < SLOT_TILES:
                            pool.wait_ge(t_done, t + 1)
                            gather(pool, t + RING)
                        if t >= 2:
                            pool.wait_ge(y_kept, t - 1)
                            pool.indirect_dma_start(
                                out=y_dram[:, :], out_offset=bass.IndirectOffsetOnAxis(ap=dst_row[:, t - 2:t - 1], axis=0),
                                in_=ys[(t - 2) % RING][:, :], in_offset=None).then_inc(out_landed[(t - 2) % RING], 16)

                @block.sync
                def _(sp):
                    for j in range(RING):
                        sp.wait_ge(out_landed[j], BEFORE + 16 * QUADS)
                    for q in range(TILES // 4):
                        for k in range(TOPK):
                            rows = y_dram[k * TOKENS + q * 4 * P:k * TOKENS + (q + 1) * 4 * P, :]
                            sp.dma_start(y[:, k, q * 4:(q + 1) * 4, :], rows.rearrange("(t p) d -> p t d", p=P)
                                         ).then_inc(got[q], 16)


def hybrid_kernel(nc, ins, out):
    with ExitStack() as ctx:
        def sb(name, shape, dt):
            return ctx.enter_context(nc.sbuf_tensor(name, shape, dt))

        def sem(name):
            return ctx.enter_context(nc.semaphore(name))

        x_res = sb("x_res", [P, TILES, P], F32)
        consts = sb("consts", [P, CONST_COLS], F32)
        mean_var = sb("mean_var", [P, TILES, 2], F32)
        stats = sb("stats", [P, TILES, 6], F32)
        rstd = sb("rstd", [P, TILES], F32)
        ones_bf, below_bf, ident_bf, causal_bf = (sb(n, [P, P], BF16) for n in ("ones_bf", "below_bf", "ident_bf", "causal_bf"))
        gate_w = [sb(f"gate_{n}", [P, EXPERTS, FF], F32R) for n in ("hi", "lo")]
        up_w = [sb(f"up_{n}", [P, EXPERTS, FF], F32R) for n in ("hi", "lo")]
        down_w = sb("down_w", [P, EXPERTS, FF], F32)
        router_w = sb("router_w", [P, EXPERTS], F32)
        router_b = sb("router_b", [P, EXPERTS], F32)
        xn_dram = nc.dram_tensor("xn_dram", (TOKENS, D), F32, kind="Internal").ap()
        y_dram = nc.dram_tensor("y_dram", (TOPK * TOKENS + SLOT_TILES * P, D), F32, kind="Internal").ap()

        def cst(name):
            return consts[:, CONST[name][0]:CONST[name][1]]

        ident = cst("ident")

        small, big, consts_in = sem("small"), sem("big"), sem("consts_in")

        def first_loads(sp, to_cast):
            sp.dma_start(consts[:, :], ins["consts"]).then_inc(consts_in, 16)
            for dst, src in ((x_res[:, :, :], ins["x"].rearrange("(t p) d -> p t d", p=P)),
                             (to_cast[:, :, :], ins["cast"]), (router_w[:, :], ins["router_w"]),
                             (router_b[:, :], ins["router_b"])):
                sp.dma_start(dst, src).then_inc(small, 16)

        def casts(dve, to_cast):
            dve.wait_ge(consts_in, 16)
            dve.wait_ge(small, SMALL_LOADS * 16)
            for dst, src in ((ones_bf, cst("ones")), (ident_bf, ident), (below_bf, to_cast[:, 0, :]), (causal_bf, to_cast[:, 1, :])):
                dve.tensor_copy(dst[:, :], src)

        rings = ([sem(f"in_landed{j}") for j in range(RING)], [sem(f"out_landed{j}") for j in range(RING)],
                 [sem(f"got{q}") for q in range(TILES // 4)], sem("first_added"), sem("second_added"))
        moe = (x_res, mean_var, rstd, stats, cst, ident, ones_bf[:, :], below_bf[:, :], gate_w, up_w, down_w, router_w,
               router_b, ins["moe_consts"], xn_dram, y_dram, rings)
        attn = (x_res, mean_var, rstd, stats, cst, ident, ident_bf[:, :], causal_bf[:, :])
        with ExitStack() as causal_ctx:
            ready = CausalWeights(nc, causal_ctx, ctx, {k[2:]: v for k, v in ins.items() if k.startswith("c_")})
            attention(nc, ctx, False, *attn, {k[2:]: v for k, v in ins.items() if k.startswith("a_")},
                      (gate_w, up_w, big, (ins["gate_w"], ins["up_w"], ins["down_w"]), down_w), ready.load,
                      first=(first_loads, casts, consts_in))
            ready.make_room()
            experts(nc, ctx, 0, *moe, ready)
            attention(nc, ctx, True, *attn, None, ready=ready)
        experts(nc, ctx, 1, *moe, last_layer=True)

        stored = sem("stored")
        with nc.Block() as block:

            @block.sync
            def _(sp):
                sp.dma_start(out.rearrange("(t p) d -> p t d", p=P), x_res[:, :, :]).then_inc(stored, 16)
                sp.wait_ge(stored, 16)


def constants():
    import numpy as np
    c, m = np.zeros((P, CONST_COLS), np.float32), np.zeros((P, MOE_COLS), np.float32)

    def put(array, where, name, value):
        array[:, where[name][0]:where[name][1]] = value

    i = np.arange(P)
    put(c, CONST, "ident", np.eye(P))
    put(c, CONST, "ones", 1.0)
    put(c, CONST, "head", i[:, None] - 3 * QUAD == np.arange(HEADS)[None, :])
    put(c, CONST, "group", (i[:, None] % QUAD) // DH == np.arange(GROUPS)[None, :])
    put(m, MOE_CONST, "rank", EXPERTS - np.arange(EXPERTS))
    put(m, MOE_CONST, "full", P * np.arange(TILES))
    e = np.arange(EXPERTS)
    put(m, MOE_CONST, "upto", (e[None, :] <= e[:, None]).astype(np.float32).reshape(1, -1))
    put(m, MOE_CONST, "tile_no", np.arange(SLOT_TILES))
    put(m, MOE_CONST, "row_no", i)
    put(m, MOE_CONST, "digit", np.tile(EXPERTS ** (1 + np.arange(RING)), SLOT_TILES // RING))
    put(m, MOE_CONST, "part_no", i[:, None])
    put(m, MOE_CONST, "pair_no", 1 + np.arange(TOPK * TILES))
    put(m, MOE_CONST, "pad_row", P + TOPK * TOKENS + P * np.arange(SLOT_TILES)[None, :] + i[:, None])
    below = i[:, None] < i[None, :]
    causal = np.where(i[None, :] <= i[:, None], 0.0, MASKED)
    return c, m, np.stack([below, causal], 1).astype(np.float32)


def kernel(**inputs):
    import numpy as np
    import concourse.bacc as bacc
    from concourse.bass_utils import run_bass_kernel_spmd

    a = {k: np.asarray(v) for k, v in inputs.items()}
    wide = lambda v: np.ascontiguousarray(np.broadcast_to(v[None, :], (P, v.shape[0])))
    qkv, qkv_b = a["L0_attn_a_qkv_weight"], a["L0_attn_a_qkv_bias"]

    def groups(w):
        w = w.reshape(GROUPS, 1, QUAD, -1)
        return np.broadcast_to(w, (GROUPS, 3, QUAD, w.shape[-1])).reshape(GROUPS * 3 * QUAD, -1)

    bqk = np.zeros((P, 2 * GROUPS), np.float32)
    bqk[0:3 * QUAD] = np.concatenate([groups(qkv_b[0:D, None]), groups(qkv_b[D:2 * D, None])]).reshape(2 * GROUPS, 3 * QUAD).T
    kqv, kqv_b = a["L0_attn_b_Wkqv"], a["L0_attn_b_bkqv"]
    consts, moe_consts, cast = constants()
    arrays = {
        "consts": consts, "cast": cast, "moe_consts": moe_consts,
        "x": a["L0_attn_a_input_tensor"].reshape(TILES * P, D),
        "router_w": a["L0_ffn_router_w"].T,
        "router_b": wide(a["L0_ffn_router_b"]),
        "gate_w": a["L0_ffn_gate_w"].transpose(2, 0, 1).reshape(P, -1),
        "up_w": a["L0_ffn_up_w"].transpose(2, 0, 1).reshape(P, -1),
        "down_w": a["L0_ffn_down_w"].transpose(2, 0, 1).reshape(FCH, P, EXPERTS, P).transpose(1, 2, 0, 3).reshape(P, EXPERTS, FF),
        "a_wqk": np.concatenate([groups(qkv[0:D]), groups(qkv[D:2 * D])]).T,
        "a_bqk": bqk,
        "a_wv": qkv[2 * D:].T, "a_bv": wide(qkv_b[2 * D:]),
        "a_wo": a["L0_attn_a_out_weight"].T, "a_bo": wide(a["L0_attn_a_out_bias"]),
        "c_wkT": kqv[:, :, 0:D].transpose(2, 0, 1), "c_wqT": kqv[:, :, D:2 * D].transpose(2, 0, 1),
        "c_bk": kqv_b[:, 0:D].T, "c_bq": kqv_b[:, D:2 * D].T,
        "c_wv": kqv[:, :, 2 * D:].transpose(1, 0, 2).reshape(D, HEADS * DH), "c_bv": wide(kqv_b[:, 2 * D:].reshape(-1)),
        "c_wo": a["L0_attn_b_Wp"], "c_bo": wide(a["L0_attn_b_bp"]),
    }
    nc = bacc.Bacc("TRN2", target_bir_lowering=False, num_devices=1)
    arrays = {k: np.ascontiguousarray(v) for k, v in arrays.items()}
    ins = {k: nc.dram_tensor(f"in_{k}", v.shape, mybir.dt.from_np(v.dtype), kind="ExternalInput").ap()
           for k, v in arrays.items()}
    out = nc.dram_tensor("out_x", (TILES * P, D), F32, kind="ExternalOutput").ap()
    hybrid_kernel(nc, ins, out)
    r = run_bass_kernel_spmd(nc, [{f"in_{k}": v for k, v in arrays.items()}], core_ids=[0])
    return np.asarray(r.results[0]["out_x"]).reshape(BATCH, SEQ, D)
```

```python
from contextlib import ExitStack

import concourse.bass as bass
from concourse import mybir

ALU = mybir.AluOpType
ACT = mybir.ActivationFunctionType
AX_X = mybir.AxisListType.X
F32 = mybir.dt.float32
F32R = mybir.dt.float32r
BF16 = mybir.dt.bfloat16
I32 = mybir.dt.int32
U32 = mybir.dt.uint32

P = 128
BATCH, SEQ, D = 8, 256, 128
TOKENS = BATCH * SEQ
TILES = TOKENS // P
CH = SEQ // P
HEADS, DH = 16, 8
GROUPS = 4
QUAD = 32
VCOLS = 16
EXPERTS, TOPK, FF = 8, 2, 512
FCH = FF // P
SLOT_TILES = TILES * TOPK + EXPERTS
RING = 4
TURN = 2 * RING
SMALL_LOADS = 4
LN_EPS = 1e-5
MASKED = -1.0e30


def columns(widths):
    at, where = 0, {}
    for name, width in widths.items():
        where[name] = (at, at + width)
        at += width
    return where, at


CONST, CONST_COLS = columns(dict(ident=P, ones=P, head=HEADS, group=GROUPS))
MOE_CONST, MOE_COLS = columns(dict(rank=EXPERTS, full=TILES, upto=EXPERTS * EXPERTS, tile_no=SLOT_TILES, row_no=P,
                                   part_no=1, digit=SLOT_TILES, pair_no=TOPK * TILES, pad_row=SLOT_TILES))


PLAIN_AT = dict(
    step=57,
    center=1,
    norm=7,
    low=9,
    project=[10, 12, 15, 21],
    v=18,
    shift=76,
    keep_shift=77,
    spread_k=[13, 2],
    scores=[25, 30, 33, 35, 38, 40, 43, 45, 49, 52, 55, 58, 61, 64, 67, 70],
    shifted=[79, 82, 85, 88, 89, 92, 95, 100, 101, 104, 107, 108, 111, 114, 119, 123],
    values=[94, 100, 104, 110, 114, 119, 128, 131],
    end=[135, 141, 146, 153, 159, 165],
    split=[38, 55])
CAUSAL_AT = dict(
    step=62,
    center=0,
    norm=6,
    low=8,
    project=[16, 19, 22, 25, 26, 29, 32, 35],
    v=13,
    shift=73,
    keep_shift=75,
    scores=[21, 24, 27, 29, 33, 36, 39, 44, 45, 48, 51, 53, 58, 59, 63, 65],
    shifted=[76, 79, 82, 85, 88, 91, 95, 98, 101, 104, 107, 110, 114, 116, 119, 122],
    values=[98, 99, 109, 110, 121, 122, 133, 134],
    end=[143, 150, 156, 162, 168, 177])


def behind(eng, sem, value):
    if isinstance(value, int) and value <= 0:
        return
    eng.wait_ge(sem, value)


def layer_norm_stats(nc, sem, x_res, mean_var, stats, rstd, work, sums_ready=True):
    moments, std_in, std_out = sem("moments"), sem("std_in"), sem("std_out")
    with nc.Block() as block:

        @block.vector
        def _(dve):
            if "vector_first" in work:
                work["vector_first"](dve)
            if not sums_ready:
                for t in range(TILES):
                    dve.bn_stats(stats[:, t, :], x_res[:, t, :]).then_inc(moments, 1)
                dve.wait_ge(moments, TILES)
            for t in range(TILES):
                dve.bn_aggr(mean_var[:, t, :], stats[:, t, :]).then_inc(moments, 1)
            dve.wait_ge(moments, TILES if sums_ready else 2 * TILES)
            dve.tensor_scalar(rstd, mean_var[:, :, 1], LN_EPS, None, ALU.add).then_inc(std_in, 1)
            dve.wait_ge(std_out, 1)
            dve.reciprocal(rstd, rstd)
            if "vector" in work:
                work["vector"](dve)

        @block.scalar
        def _(act):
            if "scalar_first" in work:
                work["scalar_first"](act)
            act.wait_ge(std_in, 1)
            act.activation(rstd, rstd, ACT.Sqrt).then_inc(std_out, 1)
            if "scalar" in work:
                work["scalar"](act)

        for name in ("sync", "gpsimd", "tensor"):
            if name in work:
                {"sync": block.sync, "gpsimd": block.gpsimd, "tensor": block.tensor}[name](work[name])


def attention(nc, kept, causal, x_res, mean_var, rstd, stats, cst, ident, ident_bf, causal_bf, weights, split_w=None,
              later_loads=None, ready=None, first=None):
    scale = float((D if causal else DH) ** -0.5)
    UNITS = HEADS // 2 if causal else 4
    with ExitStack() as ctx:
        tag = "c" if causal else "a"

        def sb(name, shape, dt):
            return ctx.enter_context(nc.sbuf_tensor(f"{tag}_{name}", shape, dt))

        def sem(name):
            return kept.enter_context(nc.semaphore(f"{tag}_{name}"))

        WCOLS = HEADS * P if causal else 2 * GROUPS * 3 * QUAD
        V_COLS = P + HEADS if causal else P
        if causal:
            w_hi, w_lo, wv_hi, wv_lo, wo, bv, bo, bias, u_bias = (
                ready.w_hi, ready.w_lo, ready.wv_hi, ready.wv_lo, ready.wo, ready.bv, ready.bo, ready.bias, ready.u_bias)
            layer_norm_stats(nc, sem, x_res, mean_var, stats, rstd[:, :], {})
        else:
            w_hi, w_lo = sb("w_hi", [P, WCOLS], F32R), sb("w_lo", [P, WCOLS], F32R)
            wv_hi, wv_lo = sb("wv_hi", [P, V_COLS], F32R), sb("wv_lo", [P, V_COLS], F32R)
            wv, wo = sb("wv", [P, P], F32), sb("wo", [P, P], F32)
            bv, bo = sb("bv", [P, P], F32), sb("bo", [P, P], F32)
            bias = sb("bias", [P, HEADS], F32)
            q_st = [sb(f"q_st{p}", [P, GROUPS, SEQ], F32R) for p in range(2)]
            k_st = [sb(f"k_st{p}", [P, HEADS, SEQ], F32R) for p in range(2)]
            loaded, hi_made = sem("loaded"), sem("hi_made")
            with nc.sbuf_tensor("a_wqk", [P, WCOLS], F32) as wqk, nc.sbuf_tensor("to_cast", [P, 2, P], F32) as to_cast:
                first_loads, casts, consts_in = first

                def fixed_rows(pool):
                    for p in range(2):
                        pool.memset(q_st[p][3 * QUAD:P, :, :].bitcast(F32), 0.0)

                def load_all(sp):
                    first_loads(sp, to_cast)
                    for dst, name in ((wv, "wv"), (wo, "wo"), (bv, "bv"), (bo, "bo")):
                        sp.dma_start(dst[:, :], weights[name]).then_inc(loaded, 16)
                    sp.dma_start(wqk[:, :], weights["wqk"]).then_inc(loaded, 16)
                    sp.dma_start(bias[:, 0:2 * GROUPS], weights["bqk"]).then_inc(loaded, 16)
                    gate_w, up_w, big, (gate_in, up_in, down_in), down_w = split_w
                    for w, w_in in ((gate_w, gate_in), (up_w, up_in)):
                        sp.dma_start(w[1][:, :, :].rearrange("p e f -> p (e f)").bitcast(F32), w_in).then_inc(big, 16)
                    sp.dma_start(down_w[:, :, :], down_in).then_inc(big, 16)

                def hi_parts(act):
                    act.wait_ge(consts_in, 16)
                    for p in range(2):
                        act.copy(k_st[p][3 * QUAD:P, :, :],
                                 cst("head")[3 * QUAD:P, :].unsqueeze(2).to_broadcast([QUAD, HEADS, SEQ]))
                    act.wait_ge(loaded, 6 * 16)
                    act.copy(w_hi[:, :], wqk[:, :])
                    act.copy(wv_hi[:, 0:P], wv[:, :]).then_inc(hi_made, 1)

                def lo_parts(dve):
                    dve.wait_ge(hi_made, 1)
                    dve.tensor_tensor(w_lo[:, :], wqk[:, :], w_hi[:, :].bitcast(F32), ALU.subtract)
                    dve.tensor_tensor(wv_lo[:, 0:P], wv[:, :], wv_hi[:, 0:P].bitcast(F32), ALU.subtract)

                layer_norm_stats(nc, sem, x_res, mean_var, stats, rstd[:, :], {
                    "sync": load_all, "vector_first": lambda dve: casts(dve, to_cast), "vector": lo_parts,
                    "scalar_first": hi_parts, "gpsimd": fixed_rows}, sums_ready=False)

        TWO = range(2)
        xn = sb("xn", [P, CH, P], F32)
        x_hi = [sb(f"x_hi{p}", [P, SEQ], F32R) for p in TWO]
        x_lo = [sb(f"x_lo{p}", [P, SEQ], F32R) for p in TWO]
        v_st = ready.v_st if causal else [sb(f"v_st{p}", [P, CH, HEADS, VCOLS], F32) for p in TWO]
        row_max = [sb(f"row_max{p}", [P, HEADS, CH], F32) for p in TWO]
        shift = [sb(f"shift{p}", [P, HEADS, CH], F32) for p in TWO]
        o_all = [ready.o_all0, ready.o_all1] if causal else [sb(f"o_all{p}", [P, GROUPS, SEQ], F32) for p in TWO]
        r_inv = sb("r_inv", [P, HEADS], F32)
        att = sb("att", [P, HEADS, DH], F32)
        att_t = sb("att_t", [P, P], F32)
        ST_COLS = SEQ + P if causal else 2 * SEQ
        probs = ready.probs if causal else sb("probs", [P, 8, ST_COLS], F32)
        if causal:
            t_hi = [sb(f"t_hi{p}", [P, HEADS, SEQ], F32R) for p in TWO]
            t_lo = [sb(f"t_lo{p}", [P, HEADS, SEQ], F32R) for p in TWO]
            SHIFT_ROWS = QUAD + HEADS
            neg_max = sb("neg_max", [SHIFT_ROWS, 2, SEQ], F32R)
            u_row = [sb(f"u_row{p}", [P, CH, HEADS], F32) for p in TWO]
            pick = sb("pick", [SHIFT_ROWS, HEADS // 2], F32R)
            m_row = sb("m_row", [P, HEADS, CH], F32)
        else:
            k_all = sb("k_all", [P, GROUPS, SEQ], F32)

        def bank(name, n=1):
            return ctx.enter_context(nc.psum_tensor(f"{tag}_{name}", [P, 512 * n], F32))

        ps_s = [bank(f"ps_s{i}") for i in TWO]
        ps_st = [bank(f"ps_st{i}") for i in TWO]
        ps_o = bank("ps_o")
        ps_x = bank("ps_x")
        ps_p = [bank(f"ps_p{i}") for i in TWO]

        consts_set = sem("consts_set")
        xn_ready, xt_done, xhi_ready, xlo_ready = sem("xn_ready"), sem("xt_done"), sem("xhi_ready"), sem("xlo_ready")
        v_done, v_ready, bias_added = sem("v_done"), sem("v_ready"), sem("bias_added")
        proj_done, proj_hi, proj_lo = sem("proj_done"), sem("proj_hi"), sem("proj_lo")
        s_done, max_done, shift_ready, shift_t_done, shift_set = (
            sem("s_done"), sem("max_done"), sem("shift_ready"), sem("shift_t_done"), sem("shift_set"))
        st_done, exp_done, o_done, o_kept = sem("st_done"), sem("exp_done"), sem("o_done"), sem("o_kept")
        ot_done, rinv_done, att_done, att_t_done, att_t_kept, out_done, res_done = (
            sem("ot_done"), sem("rinv_done"), sem("att_done"), sem("att_t_done"), sem("att_t_kept"),
            sem("out_done"), sem("res_done"))
        if causal:
            m_done, cut_begun, cut_done, zeroed = sem("m_done"), sem("cut_begun"), sem("cut_done"), sem("zeroed")
        else:
            k_spread, split_hi, split_lo = sem("k_spread"), sem("split_hi"), sem("split_lo")
        probs_ready = cut_done if causal else exp_done
        N_CONST = 7 if causal else 5

        AT = CAUSAL_AT if causal else PLAIN_AT
        STEP = AT["step"]

        def pipeline(pieces, Fori):
            def at_time(b, p, at, newest):
                for name in ("center", "norm", "low", "v", "shift", "keep_shift"):
                    if at == AT[name]:
                        pieces[name](b, p)
                for n in range(UNITS):
                    if at == AT["project"][n]:
                        pieces["project"](b, p, n)
                for h in range(HEADS):
                    if not causal and at == AT["spread_k"][0] + h * AT["spread_k"][1]:
                        pieces["spread_k"](b, p, h)
                    if at == AT["shifted"][h]:
                        pieces["shifted"](b, p, h)
                    if at == AT["scores"][h]:
                        pieces["scores"](b, p, h)
                for n in range(GROUPS * CH):
                    if at == AT["values"][n]:
                        pieces["values"](b, p, n // CH, n % CH)
                for n in range(3 * CH):
                    if at == AT["end"][n]:
                        pieces["end"](b, p, n // 3, n % 3, newest)
                if not causal and at in AT["split"]:
                    pieces["split"](b, AT["split"].index(at))

            def step(i, parity, head, middle, tail):
                newest = i if head else None
                for s in range(STEP):
                    if tail:
                        at_time(i - 2, parity, 2 * STEP + s, newest)
                    if middle:
                        at_time(i - 1, 1 - parity, STEP + s, newest)
                    if head:
                        at_time(i, parity, s, newest)

            step(0, 0, True, False, False)
            step(1, 1, True, True, False)
            with Fori(0, BATCH // 2 - 1) as pair:
                step(2 * pair + 2, 0, True, True, True)
                step(2 * pair + 3, 1, True, True, True)
            step(BATCH, 0, False, True, True)
            step(BATCH + 1, 1, False, False, True)

        def nothing(*_):
            pass

        with nc.Block() as block:

            if later_loads is not None:
                block.sync(later_loads)

            @block.gpsimd
            def _(pool):
                for p in TWO:
                    pool.memset(v_st[p][:, :, :, DH:DH + 1], 1.0).then_inc(consts_set, 1)
                    pool.memset(v_st[p][:, :, :, DH + 1:VCOLS], 0.0).then_inc(consts_set, 1)

                def center(b, p):
                    pool.wait_ge(xn_ready, b + 1)
                    for c in range(CH):
                        pool.tensor_tensor(x_res[:, b * CH + c, :], x_res[:, b * CH + c, :], bo[:, :],
                                           ALU.add).then_inc(bias_added, 1)

                def spread_k(b, p, h):
                    if not isinstance(b, int) or b >= 2:
                        pool.wait_ge(st_done, HEADS * (b - 2) + h + 1)
                    pool.wait_ge(proj_lo, b * UNITS + h // 8 + 1)
                    mask = cst("group")[0:3 * QUAD, h % 4:h % 4 + 1].to_broadcast([3 * QUAD, SEQ])
                    pool.tensor_tensor(k_st[p][0:3 * QUAD, h, :], k_all[0:3 * QUAD, h // 4, :], mask, ALU.mult
                                       ).then_inc(k_spread, 1)

                def split(i, n):
                    pool.wait_ge(split_hi, 2 * i + n + 1)
                    hi, lo = split_w[n]
                    pool.tensor_tensor(lo[:, i, :], lo[:, i, :].bitcast(F32), hi[:, i, :].bitcast(F32),
                                       ALU.subtract).then_inc(split_lo, 1)

                def shifted(b, p, h):
                    if causal:
                        pool.wait_ge(exp_done, HEADS * b + h + 1)
                        pool.sem_inc(cut_begun, 1)
                        slot, at = (h - h % 2) % 8, (0, SEQ)[h % 2]
                        diag = probs[:, slot:slot + 2, at:at + P]
                        pool.affine_select(out=diag, in_=diag, compare_op=ALU.is_ge, fill=0.0, base=0,
                                           pattern=[[0, 2], [1, P]], channel_multiplier=-1).then_inc(cut_done, 1)

                pipeline(dict(center=center, norm=nothing, low=nothing, v=nothing, project=nothing, spread_k=spread_k,
                              scores=nothing, split=split, shifted=shifted, values=nothing, end=nothing,
                              shift=nothing, keep_shift=nothing), pool.Fori)

            @block.scalar
            def _(act):
                def norm(b, p):
                    act.wait_ge(xt_done, b + 1)
                    if causal:
                        behind(act, st_done, HEADS * (b - 1))
                    act.copy(x_hi[p][:, :], ps_p[1][:, 0:SEQ]).then_inc(xhi_ready, 1)

                def project(b, p, u):
                    act.wait_ge(proj_done, b * UNITS + u + 1)
                    if not causal and u < 2:
                        behind(act, k_spread, HEADS * b)
                    for r in range(2):
                        src = ps_p[u % 2][:, r * SEQ:(r + 1) * SEQ]
                        if causal:
                            h = 2 * u + r
                            dst, n, col = t_hi[p][:, h, :], P, h
                        elif u < 2:
                            dst, n, col = k_all[0:3 * QUAD, 2 * u + r, :].bitcast(F32R), 3 * QUAD, GROUPS + 2 * u + r
                        else:
                            dst, n, col = q_st[p][0:3 * QUAD, 2 * (u - 2) + r, :], 3 * QUAD, 2 * (u - 2) + r
                        last = act.activation(dst, src[0:n, :], ACT.Identity, bias=bias[0:n, col:col + 1])
                    last.then_inc(proj_hi, 1)

                def shifted(b, p, h):
                    n = HEADS * b + h
                    act.wait_ge(st_done, n + 1)
                    behind(act, o_done, GROUPS * b + h // 4 - 1)
                    if causal:
                        slot, width = (h - h % 2) % 8, (SEQ, P)[h % 2]
                        at = (0, SEQ)[h % 2]
                        act.activation(probs[:, slot:slot + 2, at:at + width],
                                       ps_st[h % 2][:, 0:2 * width].rearrange("p (n q) -> p n q", q=width),
                                       ACT.Exp, scale=scale).then_inc(exp_done, 1)
                    else:
                        act.activation(probs[:, h % 8, :], ps_st[h % 2][:, 0:ST_COLS], ACT.Exp, scale=scale
                                       ).then_inc(exp_done, 1)

                def keep_shift(b, p):
                    if not causal:
                        act.wait_ge(shift_set, 2 * b + 1)
                        for g in range(2, GROUPS):
                            last = act.copy(q_st[p][3 * QUAD:3 * QUAD + HEADS, g, :], ps_o[0:HEADS, 0:SEQ])
                        last.then_inc(shift_set, 1)

                def split(i, n):
                    hi, lo = split_w[n]
                    act.wait_ge(split_w[2], 3 * 16)
                    act.copy(hi[:, i, :], lo[:, i, :].bitcast(F32)).then_inc(split_hi, 1)

                def values(b, p, g, c):
                    if c < CH - 1:
                        return
                    act.wait_ge(o_done, GROUPS * b + g + 1)
                    act.copy(o_all[p][:, g, :], ps_o[:, 0:SEQ]).then_inc(o_kept, 1)

                def end(b, p, c, part, _):
                    if part == 1:
                        act.wait_ge(att_t_done, CH * b + c + 1)
                        act.copy(att_t[:, :], ps_x[:, 0:P]).then_inc(att_t_kept, 1)

                pipeline(dict(center=nothing, norm=norm, low=nothing, v=nothing, project=project, spread_k=nothing,
                              scores=nothing, split=split, shifted=shifted, values=values, end=end,
                              shift=nothing, keep_shift=keep_shift), act.Fori)

            @block.vector
            def _(dve):
                dve.memset(ps_o[:, :], 0.0).then_inc(consts_set, 1)
                if causal:
                    dve.memset(neg_max[:, :, :].bitcast(F32), 0.0).then_inc(zeroed, 1)
                    dve.memset(pick[:, :].bitcast(F32), 0.0).then_inc(zeroed, 1)
                    dve.wait_ge(zeroed, 2)
                    dve.tensor_copy(pick[0:HEADS, :], ident[0:HEADS, 0:HEADS:2]).then_inc(consts_set, 1)
                    dve.tensor_copy(pick[QUAD:SHIFT_ROWS, :], ident[QUAD:SHIFT_ROWS, QUAD + 1:SHIFT_ROWS:2]
                                    ).then_inc(consts_set, 1)

                def center(b, p):
                    behind(dve, xt_done, b)
                    for c in range(CH):
                        t = b * CH + c
                        mean = mean_var[:, t:t + 1, 0] if isinstance(t, int) else mean_var[:, bass.ds(t, 1), 0]
                        scl = rstd[:, t:t + 1] if isinstance(t, int) else rstd[:, bass.ds(t, 1)]
                        last = dve.tensor_scalar(xn[:, c, :], x_res[:, t, :], mean, scl, ALU.subtract, ALU.mult)
                    last.then_inc(xn_ready, 1)

                def low(b, p):
                    dve.wait_ge(xhi_ready, b + 1)
                    dve.tensor_tensor(x_lo[p][:, :], ps_p[1][:, 0:SEQ], x_hi[p][:, :].bitcast(F32),
                                      ALU.subtract).then_inc(xlo_ready, 1)

                def v(b, p):
                    dve.wait_ge(v_done, b + 1)
                    for c in range(CH):
                        last = dve.tensor_tensor(v_st[p][:, c, :, 0:DH],
                                                 ps_x[:, c * V_COLS:c * V_COLS + P].rearrange("p (h d) -> p h d", d=DH),
                                                 bv[:, :].rearrange("p (h d) -> p h d", d=DH), ALU.add)
                    if causal:
                        for c in range(CH):
                            at = c * V_COLS + P
                            last = dve.tensor_tensor(u_row[p][:, c, :], ps_x[:, at:at + HEADS], u_bias[:, :], ALU.add)
                    last.then_inc(v_ready, 1)

                def project(b, p, u):
                    dve.wait_ge(proj_hi, b * UNITS + u + 1)
                    for r in range(2):
                        src = ps_p[u % 2][:, r * SEQ:(r + 1) * SEQ]
                        if causal:
                            h = 2 * u + r
                            hi, lo, a, z, col = t_hi[p][:, h, :], t_lo[p][:, h, :], 0, P, h
                        elif u < 2:
                            a, z, col = 2 * QUAD, 3 * QUAD, GROUPS + 2 * u + r
                            hi = k_all[a:z, 2 * u + r, :].bitcast(F32R)
                            lo = hi
                        else:
                            a, z, col = QUAD, 2 * QUAD, 2 * (u - 2) + r
                            hi = q_st[p][a:z, 2 * (u - 2) + r, :]
                            lo = hi
                        last = dve.scalar_tensor_tensor(out=lo, in0=src[a:z, :], scalar=bias[a:z, col:col + 1],
                                                        in1=hi.bitcast(F32), op0=ALU.add, op1=ALU.subtract)
                    last.then_inc(proj_lo, 1)

                def scores(b, p, h):
                    dve.wait_ge(s_done, HEADS * b + h + 1)
                    if causal:
                        dve.tensor_reduce(row_max[p][:, h, 0:1], ps_s[h % 2][:, 0:P], AX_X, ALU.max)
                        dve.tensor_reduce(row_max[p][:, h, 1:2], ps_s[h % 2][:, P:P + SEQ], AX_X,
                                          ALU.max).then_inc(max_done, 1)
                    else:
                        dve.tensor_reduce(row_max[p][:, h, :], ps_s[h % 2][:, :].rearrange("p (c k) -> p c k", k=SEQ),
                                          AX_X, ALU.max).then_inc(max_done, 1)

                def shift_(b, p):
                    dve.wait_ge(max_done, HEADS * (b + 1))
                    if causal:
                        u = u_row[p][:, :, :].rearrange("p c h -> p h c")
                        dve.tensor_tensor(m_row[:, :, :], row_max[p][:, :, :], u, ALU.add).then_inc(m_done, 1)
                        dve.wait_ge(m_done, b + 1)
                        dve.tensor_tensor(shift[p][:, :, :], u, m_row[:, :, :], ALU.subtract).then_inc(shift_ready, 1)
                    else:
                        dve.tensor_scalar(shift[p][:, :, :], row_max[p][:, :, :], -1.0, None,
                                          ALU.mult).then_inc(shift_ready, 1)

                def keep_shift(b, p):
                    dve.wait_ge(shift_t_done, b + 1)
                    if causal:
                        behind(dve, st_done, HEADS * b)
                        for n in range(2):
                            last = dve.tensor_copy(neg_max[n * QUAD:n * QUAD + HEADS, n, :], ps_o[0:HEADS, 0:SEQ])
                        last.then_inc(shift_set, 1)
                    else:
                        for g in range(2):
                            last = dve.tensor_copy(q_st[p][3 * QUAD:3 * QUAD + HEADS, g, :], ps_o[0:HEADS, 0:SEQ])
                        last.then_inc(shift_set, 1)

                def end(b, p, c, part, _):
                    n = CH * b + c
                    if part == 0:
                        dve.wait_ge(ot_done, n + 1)
                        o = ps_x[:, :].rearrange("p (h r) -> p h r", r=QUAD)
                        dve.reciprocal(r_inv[:, :], o[:, :, DH]).then_inc(rinv_done, 1)
                        dve.wait_ge(rinv_done, n + 1)
                        dve.tensor_tensor(att[:, :, :], o[:, :, 0:DH],
                                          r_inv[:, :].unsqueeze(2).to_broadcast([P, HEADS, DH]), ALU.mult
                                          ).then_inc(att_done, 1)
                    if part == 2:
                        dve.wait_ge(out_done, n + 1)
                        dve.wait_ge(bias_added, n + 1)
                        dve.tensor_tensor(x_res[:, n, :], ps_x[:, 0:P], x_res[:, n, :], ALU.add).then_inc(res_done, 1)
                        dve.wait_ge(res_done, n + 1)
                        dve.bn_stats(stats[:, n, :], x_res[:, n, :])

                pipeline(dict(center=center, norm=nothing, low=low, v=v, project=project, spread_k=nothing,
                              scores=scores, split=nothing, shifted=nothing, values=nothing, end=end,
                              shift=shift_, keep_shift=keep_shift), dve.Fori)

            @block.tensor
            def _(pe):
                pe.wait_ge(consts_set, N_CONST)

                def three(out, hi_l, lo_l, hi_r, lo_r, first=True, last=True):
                    pe.matmul(out, hi_l, hi_r, start=first, stop=False)
                    pe.matmul(out, hi_l, lo_r, start=False, stop=False)
                    return pe.matmul(out, lo_l, hi_r, start=False, stop=last)

                def norm(b, p):
                    pe.wait_ge(xn_ready, b + 1)
                    behind(pe, proj_lo, UNITS * b)
                    for c in range(CH):
                        last = pe.transpose(ps_p[1][:, c * P:(c + 1) * P], xn[:, c, :], ident)
                    last.then_inc(xt_done, 1)

                def v(b, p):
                    pe.wait_ge(xlo_ready, b + 1)
                    for c in range(CH):
                        cols = slice(c * P, (c + 1) * P)
                        last = three(ps_x[:, c * V_COLS:(c + 1) * V_COLS], x_hi[p][:, cols], x_lo[p][:, cols],
                                     wv_hi[:, :], wv_lo[:, :])
                    last.then_inc(v_done, 1)

                def project(b, p, u):
                    behind(pe, proj_lo, b * UNITS + u - 1)
                    if u == 0:
                        pe.wait_ge(xlo_ready, b + 1)
                    for r in range(2):
                        if causal:
                            cols, n = slice((2 * u + r) * P, (2 * u + r + 1) * P), P
                        else:
                            g = (GROUPS + 2 * u + r) if u < 2 else 2 * (u - 2) + r
                            cols, n = slice(g * 3 * QUAD, (g + 1) * 3 * QUAD), 3 * QUAD
                        last = three(ps_p[u % 2][0:n, r * SEQ:(r + 1) * SEQ], w_hi[:, cols], w_lo[:, cols],
                                     x_hi[p][:, :], x_lo[p][:, :])
                    last.then_inc(proj_done, 1)

                def scores(b, p, h):
                    behind(pe, max_done, HEADS * b + h - 1)
                    out = ps_s[h % 2]
                    if causal:
                        pe.wait_ge(proj_lo, b * UNITS + h // 2 + 1)
                        pe.matmul(out[:, 0:P], t_hi[p][:, h, 0:P], x_hi[p][:, 0:P], start=True, stop=False)
                        pe.matmul(out[:, 0:P], ident_bf, causal_bf, start=False, stop=True)
                        pe.matmul(out[:, P:P + SEQ], t_hi[p][:, h, P:SEQ], x_hi[p][:, :], start=True, stop=False)
                        last = pe.matmul(out[:, SEQ:SEQ + P], ident_bf, causal_bf, start=False, stop=True)
                    else:
                        pe.wait_ge(proj_lo, b * UNITS + 2 + h // 8 + 1)
                        pe.wait_ge(k_spread, HEADS * b + h + 1)
                        for c in range(CH):
                            last = pe.matmul(out[:, c * SEQ:(c + 1) * SEQ],
                                             q_st[p][0:3 * QUAD, h // 4, c * P:(c + 1) * P], k_st[p][0:3 * QUAD, h, :],
                                             start=True, stop=True)
                    last.then_inc(s_done, 1)

                def shift_(b, p):
                    pe.wait_ge(shift_ready, b + 1)
                    behind(pe, o_kept, GROUPS * b)
                    for c in range(CH):
                        last = pe.transpose(ps_o[0:HEADS, c * P:(c + 1) * P], shift[p][:, :, c], ident)
                    last.then_inc(shift_t_done, 1)

                def shifted(b, p, h):
                    n = HEADS * b + h
                    if h == 0:
                        pe.wait_ge(shift_set, b + 1 if causal else 2 * b + 2)
                    behind(pe, exp_done, n - 1)
                    out = ps_st[h % 2]
                    if causal:
                        keys = slice(P * (h % 2), P * (h % 2) + P)
                        pair, width = h - h % 2, (SEQ, P)[h % 2]
                        q = slice(SEQ - width, SEQ)
                        both = out[:, 0:2 * width].rearrange("p (n q) -> p n q", q=width)
                        three(both, x_hi[p][:, keys], x_lo[p][:, keys], t_hi[p][:, pair:pair + 2, q],
                              t_lo[p][:, pair:pair + 2, q], last=False)
                        last = pe.matmul(both, pick[:, pair // 2:pair // 2 + 1].to_broadcast([SHIFT_ROWS, P]),
                                         neg_max[:, :, q], start=False, stop=True)
                    else:
                        for c in range(CH):
                            last = pe.matmul(out[:, c * SEQ:(c + 1) * SEQ], k_st[p][:, h, c * P:(c + 1) * P],
                                             q_st[p][:, h // 4, :], start=True, stop=True)
                    last.then_inc(st_done, 1)

                def values(b, p, g, c):
                    n = GROUPS * b + g
                    if c == 0:
                        pe.wait_ge(probs_ready, 4 * (n + 1))
                        pe.wait_ge(v_ready, b + 1)
                        behind(pe, o_kept, n)
                    for k in range(4):
                        pr = probs[:, 4 * (g % 2) + k, :]
                        rows = slice(k * QUAD, k * QUAD + VCOLS)
                        if causal and c == 1:
                            out, pr = ps_o[rows, P:SEQ], pr[:, SEQ:SEQ + P]
                        else:
                            out, pr = ps_o[rows, 0:SEQ], pr[:, c * SEQ:(c + 1) * SEQ]
                        last = pe.matmul(out, v_st[p][:, c, 4 * g + k, :], pr, start=(c == 0), stop=(c == CH - 1))
                    if c == CH - 1:
                        last.then_inc(o_done, 1)

                def end(b, p, c, part, i):
                    n = CH * b + c
                    if part == 0:
                        pe.wait_ge(o_kept, GROUPS * (b + 1))
                        if c == 1:
                            pe.wait_ge(res_done, n)
                        elif i is not None:
                            pe.wait_ge(v_ready, i + 1)
                        else:
                            behind(pe, res_done, n)
                        for g in range(GROUPS):
                            last = pe.transpose(ps_x[:, g * P:(g + 1) * P], o_all[p][:, g, c * P:(c + 1) * P], ident)
                        last.then_inc(ot_done, 1)
                    elif part == 1:
                        pe.wait_ge(att_done, n + 1)
                        pe.transpose(ps_x[:, 0:P], att[:, :, :].rearrange("p h d -> p (h d)"), ident).then_inc(att_t_done, 1)
                    else:
                        pe.wait_ge(att_t_kept, n + 1)
                        pe.matmul(ps_x[:, 0:P], att_t[:, :], wo[:, :], start=True, stop=True).then_inc(out_done, 1)

                pipeline(dict(center=nothing, norm=norm, low=nothing, v=v, project=project, spread_k=nothing,
                              scores=scores, split=nothing, shifted=shifted, values=values, end=end,
                              shift=shift_, keep_shift=nothing), pe.Fori)


class CausalWeights:

    C, U, UB = TILES * EXPERTS, TILES * EXPERTS + HEADS, TILES * EXPERTS + 2 * HEADS

    def __init__(self, nc, ctx, kept, weights):
        self.nc, self.ctx, self.weights = nc, ctx, weights
        self.probs = self.sb("probs", [P, 8, SEQ + P], F32)
        self.o_all0 = self.sb("o_all0", [P, GROUPS, SEQ], F32)
        flat = self.probs[:, :, :].rearrange("p a b -> p (a b)")
        HALF = HEADS // 2
        self.wqT = flat[:, 0:HEADS * P].rearrange("p (h k) -> p h k", k=P)
        self.wkT = [flat[:, HEADS * P:(HEADS + HALF) * P].rearrange("p (h k) -> p h k", k=P),
                    self.o_all0[:, :, :].rearrange("p g (h k) -> p (g h) k", k=P)]
        self.wv, self.wo, self.bv, self.bo = (self.sb(n, [P, P], F32) for n in ("wv", "wo", "bv", "bo"))
        self.bq, self.bk, self.bqk = (self.sb(n, [P, HEADS], F32) for n in ("bq", "bk", "bqk"))
        self.loaded, self.bqk_made, self.m_made, self.m_kept, self.w_made, self.hi_made = (
            kept.enter_context(nc.semaphore(f"cw_{n}")) for n in ("loaded", "bqk_made", "m_made", "m_kept", "w_made", "hi_made"))

    def sb(self, name, shape, dt):
        return self.ctx.enter_context(self.nc.sbuf_tensor(f"cw_{name}", shape, dt))

    def load(self, sp):
        half = HEADS // 2
        for n in range(2):
            sp.dma_start(self.wkT[n], self.weights["wkT"][:, n * half:(n + 1) * half, :]).then_inc(self.loaded, 16)
        for dst, name in ((self.wqT, "wqT"), (self.bq[:, :], "bq"), (self.bk[:, :], "bk"),
                          (self.wv[:, :], "wv"), (self.wo[:, :], "wo"), (self.bv[:, :], "bv"), (self.bo[:, :], "bo")):
            sp.dma_start(dst, self.weights[name]).then_inc(self.loaded, 16)

    def make_room(self):
        self.w_hi, self.w_lo = (self.sb(n, [P, HEADS * P], F32R) for n in ("w_hi", "w_lo"))
        self.wv_hi, self.wv_lo = (self.sb(n, [P, P + HEADS], F32R) for n in ("wv_hi", "wv_lo"))
        self.bias, self.u_bias = (self.sb(n, [P, HEADS], F32) for n in ("bias", "u_bias"))
        self.o_all1 = self.sb("o_all1", [P, GROUPS, SEQ], F32)
        self.v_st = [self.sb(f"v_st{p}", [P, CH, HEADS, VCOLS], F32) for p in range(2)]
        self.m = [self.o_all1[:, 0:2, :].rearrange("p a b -> p (a b)"), self.o_all1[:, 2:4, :].rearrange("p a b -> p (a b)"),
                  self.v_st[0][:, :, :, :].rearrange("p c h v -> p (c h v)"), self.v_st[1][:, :, :, :].rearrange("p c h v -> p (c h v)")]

    def key_weights(self, h):
        return self.wkT[h // (HEADS // 2)][:, h % (HEADS // 2), :]

    def products(self, pe, q, bank):
        behind(pe, self.m_kept, q - 1)
        for n in range(4):
            last = pe.matmul(bank[:, n * P:(n + 1) * P], self.wqT[:, 4 * q + n, :], self.key_weights(4 * q + n),
                             start=True, stop=True)
        last.then_inc(self.m_made, 1)

    def keep(self, act, q, bank):
        cols = slice(q * 4 * P, (q + 1) * 4 * P)
        act.wait_ge(self.m_made, q + 1)
        act.copy(self.w_hi[:, cols], bank[:, :])
        act.copy(self.m[q], bank[:, :]).then_inc(self.m_kept, 1)

    def low(self, pool):
        pool.wait_ge(self.loaded, 9 * 16)
        pool.tensor_tensor(self.bqk[:, :], self.bq[:, :], self.bk[:, :], ALU.mult).then_inc(self.bqk_made, 1)
        for q in range(HEADS // 4):
            cols = slice(q * 4 * P, (q + 1) * 4 * P)
            pool.wait_ge(self.m_kept, q + 1)
            pool.tensor_tensor(self.w_lo[:, cols], self.m[q], self.w_hi[:, cols].bitcast(F32), ALU.subtract)

    def key_biases(self, pe, bank):
        pe.wait_ge(self.loaded, 9 * 16)
        for h in range(HEADS):
            pe.matmul(bank[:, self.C + h:self.C + h + 1], self.key_weights(h), self.bq[:, h:h + 1], start=True, stop=True)

    def row_biases(self, pe, bank, ones):
        for h in range(HEADS):
            pe.matmul(bank[:, self.U + h:self.U + h + 1], self.wqT[:, h, :], self.bk[:, h:h + 1], start=True, stop=True)
        pe.wait_ge(self.bqk_made, 1)
        pe.matmul(bank[:, self.UB:self.UB + HEADS], ones, self.bqk[:, :], start=True, stop=True).then_inc(self.w_made, 1)

    def keep_biases(self, act, bank):
        act.copy(self.wv_hi[:, 0:P], self.wv[:, :])
        act.wait_ge(self.w_made, 1)
        act.copy(self.bias[:, :], bank[:, self.C:self.C + HEADS])
        act.copy(self.u_bias[:, :], bank[:, self.UB:self.UB + HEADS])
        act.copy(self.wv_hi[:, P:P + HEADS], bank[:, self.U:self.U + HEADS]).then_inc(self.hi_made, 1)

    def low_biases(self, dve, bank):
        dve.wait_ge(self.hi_made, 1)
        dve.tensor_tensor(self.wv_lo[:, P:P + HEADS], bank[:, self.U:self.U + HEADS], self.wv_hi[:, P:P + HEADS].bitcast(F32),
                          ALU.subtract)
        dve.tensor_tensor(self.wv_lo[:, 0:P], self.wv[:, :], self.wv_hi[:, 0:P].bitcast(F32), ALU.subtract)


def experts(nc, kept, layer, x_res, mean_var, rstd, stats, cst, ident, ones_bf, below_bf, gate_w, up_w, down_w, router_w,
            router_b, moe_consts, xn_dram, y_dram, rings, beside=None, out=None, stored=None):
    with ExitStack() as ctx:
        def sb(name, shape, dt):
            return ctx.enter_context(nc.sbuf_tensor(f"m{layer}_{name}", shape, dt))

        def sem(name):
            return kept.enter_context(nc.semaphore(f"m{layer}_{name}"))

        tables = sb("tables", [P, MOE_COLS], F32)
        tables_in = sem("tables_in")

        def load_tables(sp):
            sp.dma_start(tables[:, :], moe_consts).then_inc(tables_in, 16)
            sp.wait_ge(tables_in, 16)

        def table(name):
            return tables[:, MOE_CONST[name][0]:MOE_CONST[name][1]]

        gates = sb("gates", [P, TOPK, TILES], F32)
        turn_experts = sb("turn_experts", [P, SLOT_TILES // TURN], I32)
        src_row = sb("src_row", [P, SLOT_TILES], U32)
        dst_row = sb("dst_row", [P, SLOT_TILES], U32)
        xs = [sb(f"xs{j}", [P, P], F32) for j in range(RING)]
        in_landed, out_landed, got, first_added, weighed, second_added = rings
        BEFORE = 16 * layer * (SLOT_TILES // RING)
        shape = [P, TILES, EXPERTS]

        def gather(pool, t):
            pool.indirect_dma_start(out=xs[t % RING][:, :], out_offset=None, in_=xn_dram[:, :],
                                    in_offset=bass.IndirectOffsetOnAxis(ap=src_row[:, t:t + 1], axis=0)
                                    ).then_inc(in_landed[t % RING], 16)

        with ExitStack() as rctx:
            def rb(name, shape, dt):
                return rctx.enter_context(nc.sbuf_tensor(f"m{layer}_{name}", shape, dt))

            ps_l = rctx.enter_context(nc.psum_tensor(f"m{layer}_ps_l", [P, 512], F32))
            work = {"sync": load_tables}
            if beside is not None:
                work["tensor"] = lambda pe: beside.key_biases(pe, ps_l)
            layer_norm_stats(nc, sem, x_res, mean_var, stats, rstd[:, :], work)

            PAIRS = TOPK * TILES
            xn = rb("xn", [P, TILES, P], F32)
            xt = rb("xt", [P, TILES, P], F32)
            logits = rb("logits", shape, F32)
            left = rb("left", shape, F32)
            chosen = rb("chosen", [P, TOPK] + shape[1:], F32)
            both = rb("both", shape, BF16)
            key = rb("key", shape, F32)
            top = rb("top", [P, TOPK, TILES], F32)
            rank = rb("rank", [P, TOPK, TILES], F32)
            drop = rb("drop", [P, TILES], F32)
            ex = rb("ex", [P, TILES], F32)
            den = rb("den", [P, TILES], F32)
            over = rb("over", [P, EXPERTS, TILES], F32)
            n_tiles = rb("n_tiles", [P, EXPERTS], F32)
            upto = rb("upto", [P, EXPERTS, EXPERTS], F32)
            end_tile = rb("end_tile", [P, EXPERTS], F32)
            first_slot = rb("first_slot", [P, EXPERTS], F32)
            place = rb("place", shape, F32)
            placed = rb("placed", [P, TOPK] + shape[1:], F32)
            slot_f = rb("slot_f", [P, PAIRS], F32)
            slot_i = rb("slot_i", [P, PAIRS], I32)
            in_tile_i = rb("in_tile_i", [P, PAIRS], I32)
            tile_i = rb("tile_i", [P, PAIRS], I32)
            in_tile = rb("in_tile", [P, PAIRS], F32)
            tile_of = rb("tile_of", [P, PAIRS], F32)
            row_is = rb("row_is", [P, PAIRS, P], BF16)
            tile_is = rb("tile_is", [P, PAIRS, SLOT_TILES], F32)
            named = rb("named", [P, PAIRS, 2, SLOT_TILES], BF16)
            found = rb("found", [P, SLOT_TILES], F32)
            second = rb("second", [P, SLOT_TILES], F32)
            padding = rb("padding", [P, SLOT_TILES], F32)
            token = rb("token", [P, SLOT_TILES], F32)
            past = rb("past", [P, SLOT_TILES, EXPERTS], F32)
            tile_expert = rb("tile_expert", [P, 1 + SLOT_TILES], F32)
            digits = rb("digits", [P, SLOT_TILES // TURN, TURN], F32)
            word = rb("word", [P, SLOT_TILES // TURN], F32)
            word_i = rb("word_i", [P, SLOT_TILES // TURN], I32)
            top_digit_i = rb("top_digit_i", [P, SLOT_TILES // TURN], I32)
            ps_t = [rctx.enter_context(nc.psum_tensor(f"m{layer}_ps_t{i}", [P, 512], F32)) for i in range(2)]
            ps_m = [rctx.enter_context(nc.psum_tensor(f"m{layer}_ps_m{i}", [P, 512], F32)) for i in range(2)]
            ps_n = rctx.enter_context(nc.psum_tensor(f"m{layer}_ps_n", [P, 512], F32))
            ps_c = rctx.enter_context(nc.psum_tensor(f"m{layer}_ps_c", [P, 512], F32))
            ps_w = rctx.enter_context(nc.psum_tensor(f"m{layer}_ps_w", [P, 512], F32))
            xn_ready, xt_done, xt_kept, logits_done = sem("xn_ready"), sem("xt_done"), sem("xt_kept"), sem("logits_done")
            link, gap_ready, ex_done = sem("link"), sem("gap_ready"), sem("ex_done")
            both_ready, counted, xn_written = sem("both_ready"), sem("counted"), sem("xn_written")
            tiles_known, row_known, named_lo, named_hi, found_done = (
                sem("tiles_known"), sem("row_known"), sem("named_lo"), sem("named_hi"), sem("found_done"))
            TPB = 4

            with nc.Block() as block:

                @block.sync
                def _(sp):
                    for q in range(TILES // TPB):
                        sp.wait_ge(xn_ready, (q + 1) * TPB)
                        sp.dma_start(xn_dram[q * TPB * P:(q + 1) * TPB * P, :].rearrange("(t p) d -> p t d", p=P),
                                     xn[:, q * TPB:(q + 1) * TPB, :]).then_inc(xn_written, 16)

                @block.vector
                def _(dve):
                    done = [0]

                    def then(instruction):
                        done[0] += 1
                        instruction.then_inc(link, 1)
                        dve.wait_ge(link, done[0])

                    for t in range(TILES):
                        dve.tensor_scalar(xn[:, t, :], x_res[:, t, :], mean_var[:, t, 0:1], rstd[:, t:t + 1],
                                          ALU.subtract, ALU.mult).then_inc(xn_ready, 1)
                    dve.wait_ge(logits_done, 1)
                    wide = lambda a: a.unsqueeze(2).to_broadcast(shape)
                    rb_wide = router_b[:, :].unsqueeze(1).to_broadcast(shape)
                    rank_wide = table("rank").unsqueeze(1).to_broadcast(shape)
                    then(dve.tensor_tensor(logits[:, :, :], ps_l[:, 0:TILES * EXPERTS].rearrange("p (t e) -> p t e", e=EXPERTS),
                                           rb_wide, ALU.add))
                    src = logits
                    for k in range(TOPK):
                        then(dve.tensor_reduce(top[:, k, :], src[:, :, :], AX_X, ALU.max))
                        then(dve.tensor_tensor(key[:, :, :], src[:, :, :], wide(top[:, k, :]), ALU.is_equal))
                        then(dve.tensor_tensor(key[:, :, :], key[:, :, :], rank_wide, ALU.mult))
                        then(dve.tensor_reduce(rank[:, k, :], key[:, :, :], AX_X, ALU.max))
                        then(dve.tensor_tensor(chosen[:, k, :, :], rank_wide, wide(rank[:, k, :]), ALU.is_equal))
                        if k == 0:
                            then(dve.scalar_tensor_tensor(out=left[:, :, :].rearrange("p t e -> p (t e)"),
                                                          in0=chosen[:, 0, :, :].rearrange("p t e -> p (t e)"),
                                                          scalar=-3.0e38, in1=logits[:, :, :].rearrange("p t e -> p (t e)"),
                                                          op0=ALU.mult, op1=ALU.add))
                            src = left
                    dve.tensor_tensor(both[:, :, :], chosen[:, 0, :, :], chosen[:, 1, :, :], ALU.add).then_inc(both_ready, 1)
                    dve.tensor_tensor(drop[:, :], top[:, 1, :], top[:, 0, :], ALU.subtract).then_inc(gap_ready, 1)
                    dve.wait_ge(counted, 1)
                    then(dve.tensor_tensor(over[:, :, :], ps_c[:, 0:EXPERTS].unsqueeze(2).to_broadcast([P, EXPERTS, TILES]),
                                           table("full").unsqueeze(1).to_broadcast([P, EXPERTS, TILES]), ALU.is_gt))
                    then(dve.tensor_reduce(n_tiles[:, :], over[:, :, :], AX_X, ALU.add))
                    then(dve.tensor_tensor(upto[:, :, :], n_tiles[:, :].unsqueeze(1).to_broadcast([P, EXPERTS, EXPERTS]),
                                           table("upto").rearrange("p (a b) -> p a b", b=EXPERTS), ALU.mult))
                    then(dve.tensor_reduce(end_tile[:, :], upto[:, :, :], AX_X, ALU.add))
                    then(dve.tensor_tensor(first_slot[:, :], end_tile[:, :], n_tiles[:, :], ALU.subtract))
                    then(dve.tensor_scalar(first_slot[:, :], first_slot[:, :], float(P), None, ALU.mult))
                    dve.wait_ge(counted, 2)
                    then(dve.tensor_tensor(place[:, :, :], ps_n[:, 0:TILES * EXPERTS].rearrange("p (t e) -> p t e", e=EXPERTS),
                                           first_slot[:, :].unsqueeze(1).to_broadcast(shape), ALU.add))
                    then(dve.tensor_tensor(placed[:, :, :, :], chosen[:, :, :, :],
                                           place[:, :, :].unsqueeze(1).to_broadcast([P, TOPK] + shape[1:]), ALU.mult))
                    then(dve.tensor_reduce(slot_f[:, :], placed[:, :, :, :].rearrange("p k t e -> p (k t) e"), AX_X, ALU.add))
                    then(dve.tensor_copy(slot_i[:, :], slot_f[:, :]))
                    then(dve.tensor_scalar(tile_i[:, :], slot_i[:, :], P.bit_length() - 1, None, ALU.arith_shift_right))
                    then(dve.tensor_scalar(in_tile_i[:, :], slot_i[:, :], P - 1, None, ALU.bitwise_and))
                    then(dve.tensor_copy(tile_of[:, :], tile_i[:, :]))
                    then(dve.tensor_copy(in_tile[:, :], in_tile_i[:, :]))
                    dve.tensor_tensor(tile_is[:, :, :], tile_of[:, :].unsqueeze(2).to_broadcast([P, PAIRS, SLOT_TILES]),
                                      table("tile_no").unsqueeze(1).to_broadcast([P, PAIRS, SLOT_TILES]), ALU.is_equal
                                      ).then_inc(tiles_known, 1)
                    for k in range(TOPK):
                        half = slice(k * TILES, (k + 1) * TILES)
                        dve.tensor_tensor(row_is[:, half, :], in_tile[:, half].unsqueeze(2).to_broadcast([P, TILES, P]),
                                          table("row_no").unsqueeze(1).to_broadcast([P, TILES, P]), ALU.is_equal
                                          ).then_inc(row_known, 1)
                    then(dve.tensor_tensor(past[:, :, :], table("tile_no").unsqueeze(2).to_broadcast([P, SLOT_TILES, EXPERTS]),
                                           end_tile[:, :].unsqueeze(1).to_broadcast([P, SLOT_TILES, EXPERTS]), ALU.is_ge))
                    dve.memset(tile_expert[:, 0:1], 0.0)
                    then(dve.tensor_reduce(tile_expert[:, 1:], past[:, :, :], AX_X, ALU.add))
                    then(dve.tensor_scalar(tile_expert[:, :], tile_expert[:, :], float(EXPERTS - 1), None, ALU.min))
                    then(dve.tensor_tensor(digits[:, :, :], tile_expert[:, 1:].rearrange("p (q n) -> p q n", n=TURN),
                                           table("digit").rearrange("p (q n) -> p q n", n=TURN), ALU.mult))
                    then(dve.tensor_reduce(word[:, :], digits[:, :, :], AX_X, ALU.add))
                    then(dve.tensor_copy(word_i[:, :], word[:, :]))
                    then(dve.tensor_scalar(top_digit_i[:, :], tile_expert[:, 0:SLOT_TILES:TURN], float(EXPERTS ** TURN),
                                           None, ALU.mult))
                    then(dve.tensor_tensor(turn_experts[:, :], word_i[:, :], top_digit_i[:, :], ALU.bitwise_or))
                    dve.wait_ge(ex_done, 1)
                    then(dve.tensor_scalar(den[:, :], ex[:, :], 1.0, None, ALU.add))
                    then(dve.reciprocal(gates[:, 0, :], den[:, :]))
                    then(dve.tensor_tensor(gates[:, 1, :], gates[:, 0, :], ex[:, :], ALU.mult))
                    dve.wait_ge(found_done, 1)
                    hi, lo = ps_w[:, SLOT_TILES:2 * SLOT_TILES], found
                    then(dve.tensor_copy(found[:, :], ps_w[:, 0:SLOT_TILES]))
                    then(dve.scalar_tensor_tensor(out=found[:, :], in0=hi, scalar=float(P), in1=lo[:, :], op0=ALU.mult, op1=ALU.add))
                    dve.tensor_scalar(second[:, :], found[:, :], float(P + TOKENS), float(TOKENS), ALU.is_ge, ALU.mult)
                    then(dve.tensor_scalar(token[:, :], found[:, :], float(P), 0.0, ALU.subtract, ALU.max))
                    dve.tensor_tensor(src_row[:, :], token[:, :], second[:, :], ALU.subtract)
                    then(dve.scalar_tensor_tensor(out=padding[:, :], in0=found[:, :], scalar=0.0, in1=table("pad_row"),
                                                  op0=ALU.is_equal, op1=ALU.mult))
                    then(dve.scalar_tensor_tensor(out=dst_row[:, :], in0=found[:, :], scalar=float(P), in1=padding[:, :],
                                                  op0=ALU.subtract, op1=ALU.add))
                    if beside is not None:
                        beside.low_biases(dve, ps_l)

                @block.scalar
                def _(act):
                    if beside is not None:
                        beside.keep(act, 0, ps_m[0])
                        beside.keep(act, 1, ps_m[1])
                    for q in range(TILES // TPB):
                        act.wait_ge(xt_done, q + 1)
                        act.copy(xt[:, q * TPB:(q + 1) * TPB, :], ps_t[q % 2][:, :].rearrange("p (t k) -> p t k", k=P)
                                 ).then_inc(xt_kept, 1)
                    if beside is not None:
                        beside.keep(act, 2, ps_m[0])
                        beside.keep(act, 3, ps_m[1])
                    act.wait_ge(gap_ready, 1)
                    act.activation(ex[:, :], drop[:, :], ACT.Exp).then_inc(ex_done, 1)
                    act.wait_ge(tiles_known, 1)
                    act.activation(named[:, :, 0, :], tile_is[:, :, :], ACT.Copy, scale=table("part_no")).then_inc(named_lo, 1)
                    if beside is not None:
                        beside.keep_biases(act, ps_l)

                @block.tensor
                def _(pe):
                    if beside is not None:
                        beside.products(pe, 0, ps_m[0])
                        beside.products(pe, 1, ps_m[1])
                    def logits_of(q):
                        pe.wait_ge(xt_kept, q + 1)
                        for t in range(q * TPB, (q + 1) * TPB):
                            last = pe.matmul(ps_l[:, t * EXPERTS:(t + 1) * EXPERTS], xt[:, t, :], router_w[:, :],
                                             start=True, stop=True)
                        return last

                    for q in range(TILES // TPB):
                        pe.wait_ge(xn_ready, (q + 1) * TPB)
                        behind(pe, xt_kept, q - 1)
                        for t in range(TPB):
                            last = pe.transpose(ps_t[q % 2][:, t * P:(t + 1) * P], xn[:, q * TPB + t, :], ident)
                        last.then_inc(xt_done, 1)
                        if q:
                            logits_of(q - 1)
                    last = logits_of(TILES // TPB - 1)
                    last.then_inc(logits_done, 1)
                    if beside is not None:
                        beside.products(pe, 2, ps_m[0])
                        beside.products(pe, 3, ps_m[1])
                    pe.wait_ge(both_ready, 1)
                    for t in range(TILES):
                        last = pe.matmul(ps_c[:, 0:EXPERTS], ones_bf, both[:, t, :], start=(t == 0), stop=(t == TILES - 1))
                    last.then_inc(counted, 1)
                    before = ps_n[:, 0:TILES * EXPERTS].rearrange("p (t e) -> p t e", e=EXPERTS)
                    pe.matmul(before, below_bf, both[:, :, :], start=True, stop=False)
                    for t in range(TILES - 1):
                        n = TILES - 1 - t
                        last = pe.matmul(before[:, t + 1:TILES, :], ones_bf, both[:, t:t + 1, :].to_broadcast([P, n, EXPERTS]),
                                         start=False, stop=(t == TILES - 2))
                    last.then_inc(counted, 1)
                    if beside is not None:
                        beside.row_biases(pe, ps_l, cst("ones"))
                    pe.wait_ge(named_lo, 1)
                    pe.wait_ge(named_hi, 1)
                    for j in range(PAIRS):
                        if j % TILES == 0:
                            pe.wait_ge(row_known, j // TILES + 1)
                        last = pe.matmul(ps_w[:, 0:2 * SLOT_TILES], row_is[:, j, :],
                                         named[:, j, :, :].rearrange("p n a -> p (n a)"),
                                         start=(j == 0), stop=(j == PAIRS - 1))
                    last.then_inc(found_done, 1)

                @block.gpsimd
                def _(pool):
                    if beside is not None:
                        beside.low(pool)
                    pool.wait_ge(tiles_known, 1)
                    pool.tensor_tensor(named[:, :, 1, :], tile_is[:, :, :],
                                       table("pair_no").unsqueeze(2).to_broadcast([P, PAIRS, SLOT_TILES]), ALU.mult
                                       ).then_inc(named_hi, 1)

        with ExitStack() as ectx:
            def eb(name, shape, dt):
                return ectx.enter_context(nc.sbuf_tensor(f"m{layer}_{name}", shape, dt))

            TWO = range(2)
            HALF = FF // 2
            xs_hi = [eb(f"xs_hi{p}", [P, P], F32R) for p in TWO]
            xs_lo = [eb(f"xs_lo{p}", [P, P], F32R) for p in TWO]
            act_g = [eb(f"act_g{p}", [P, FF], F32) for p in TWO]
            hid = [eb(f"hid{p}", [P, FF], F32) for p in TWO]
            hid_t = [eb(f"hid_t{p}", [P, FF], F32) for p in TWO]
            ys = [eb(f"ys{j}", [P, P], F32) for j in range(RING)]
            y = eb("y", [P, TOPK, TILES, P], F32)
            ps = [ectx.enter_context(nc.psum_tensor(f"m{layer}_ps{i}", [P, 512], F32)) for i in range(8)]
            ps_g, ps_u, ps_h, ps_x, ps_y = ps[0:2], ps[2:4], ps[4:6], ps[6], ps[7]
            t_done, hi_ready, lo_ready, gate_done, up_done, silu_done = (
                sem("t_done"), sem("hi_ready"), sem("lo_ready"), sem("gate_done"), sem("up_done"), sem("silu_done"))
            hid_ready, ht_done, front_kept, back_kept, y_done, y_kept = (
                sem("hid_ready"), sem("ht_done"), sem("front_kept"), sem("back_kept"), sem("y_done"), sem("y_kept"))
            TURNS = SLOT_TILES // TURN

            def turns(step, Fori):
                for j in range(TURN):
                    step(0, j)
                with Fori(1, TURNS - 1) as turn:
                    for j in range(TURN):
                        step(turn, j)
                for j in range(TURN):
                    step(TURNS - 1, j)

            def rounds(turn, j):
                return turn * (TURN // RING) + j // RING

            with nc.Block() as block:

                @block.tensor
                def _(pe):
                    expert = {}

                    def load_experts(turn, first):
                        word = pe.value_load(turn_experts[0:1, bass.ds(turn, 1)], min_val=0, max_val=EXPERTS ** (TURN + 1) - 1)
                        for n in range(0 if first else -1, TURN):
                            expert[n] = (word >> (3 * (n % (TURN + 1)))) & (EXPERTS - 1)

                    def to_columns(turn, j):
                        pe.wait_ge(in_landed[j % RING], BEFORE + 16 * rounds(turn, j) + 16)
                        pe.transpose(ps_x[:, 0:P], xs[j % RING][:, :], ident).then_inc(t_done, 1)

                    def product(out, p, w, e, between=None):
                        pe.matmul(out[:, :], xs_hi[p][:, :], w[0][:, e, :], start=True, stop=False)
                        pe.matmul(out[:, :], xs_hi[p][:, :], w[1][:, e, :], start=False, stop=False)
                        if between is not None:
                            between()
                        return pe.matmul(out[:, :], xs_lo[p][:, :], w[0][:, e, :], start=False, stop=True)

                    def back(t, p):
                        pe.wait_ge(hid_ready, t + 1)
                        for f in range(FCH):
                            last = pe.transpose(ps_h[f // 2][:, (f % 2) * P:(f % 2 + 1) * P], hid[p][:, f * P:(f + 1) * P], ident)
                        last.then_inc(ht_done, 1)

                    def down(t, p, e):
                        pe.wait_ge(front_kept, t + 1)
                        pe.wait_ge(back_kept, t + 1)
                        behind(pe, y_kept, t)
                        for f in range(FCH):
                            last = pe.matmul(ps_y[:, 0:P], hid_t[p][:, f * P:(f + 1) * P],
                                             down_w[:, e, f * P:(f + 1) * P], start=(f == 0), stop=(f == FCH - 1))
                        last.then_inc(y_done, 1)

                    def step(turn, j):
                        t, p = TURN * turn + j, j % 2
                        first = isinstance(t, int) and t == 0
                        final = isinstance(t, int) and t == SLOT_TILES - 1
                        if j == 0:
                            load_experts(turn, first)
                        pe.wait_ge(lo_ready, t + 1)
                        product(ps_g[p], p, gate_w, expert[j],
                                None if first else lambda: back(t - 1, 1 - p)).then_inc(gate_done, 1)
                        if not final:
                            to_columns(turn, j + 1)
                        product(ps_u[p], p, up_w, expert[j]).then_inc(up_done, 1)
                        if not first:
                            down(t - 1, 1 - p, expert[j - 1])

                    to_columns(0, 0)
                    turns(step, pe.Fori)
                    back(SLOT_TILES - 1, 1)
                    down(SLOT_TILES - 1, 1, expert[TURN - 1])

                @block.scalar
                def _(act):
                    def high(t, p):
                        act.wait_ge(t_done, t + 1)
                        act.copy(xs_hi[p][:, :], ps_x[:, 0:P]).then_inc(hi_ready, 1)

                    def front(t, p):
                        act.wait_ge(ht_done, t + 1)
                        act.copy(hid_t[p][:, 0:HALF], ps_h[0][:, 0:HALF]).then_inc(front_kept, 1)

                    def step(turn, j):
                        t, p = TURN * turn + j, j % 2
                        if not (isinstance(t, int) and t == 0):
                            front(t - 1, 1 - p)
                        act.wait_ge(gate_done, t + 1)
                        act.activation(act_g[p][:, :], ps_g[p][:, :], ACT.Silu).then_inc(silu_done, 1)
                        if not (isinstance(t, int) and t == SLOT_TILES - 1):
                            high(t + 1, 1 - p)

                    high(0, 0)
                    turns(step, act.Fori)
                    front(SLOT_TILES - 1, 1)
                    for t in range(TILES):
                        if t % 4 == 0:
                            act.wait_ge(got[t // 4], 16 * TOPK * (layer + 1))
                        last = act.activation(y[:, 1, t, :], y[:, 1, t, :], ACT.Copy, scale=gates[:, 1, t:t + 1])
                        if t % 4 == 3:
                            last.then_inc(weighed, 1)

                @block.vector
                def _(dve):
                    def low(t, p):
                        dve.wait_ge(hi_ready, t + 1)
                        dve.tensor_tensor(xs_lo[p][:, :], ps_x[:, 0:P], xs_hi[p][:, :].bitcast(F32),
                                          ALU.subtract).then_inc(lo_ready, 1)

                    def rest(t, p):
                        dve.wait_ge(ht_done, t + 1)
                        dve.tensor_copy(hid_t[p][:, HALF:FF], ps_h[1][:, 0:HALF]).then_inc(back_kept, 1)

                    def keep(turn, j, t):
                        dve.wait_ge(y_done, t + 1)
                        if not (isinstance(turn, int) and rounds(turn, j) == 0):
                            dve.wait_ge(out_landed[j % RING], BEFORE + 16 * rounds(turn, j))
                        dve.tensor_copy(ys[(j - 1) % RING][:, :], ps_y[:, 0:P]).then_inc(y_kept, 1)

                    def step(turn, j):
                        t, p = TURN * turn + j, j % 2
                        first = isinstance(t, int) and t == 0
                        if not first:
                            rest(t - 1, 1 - p)
                        if not (isinstance(t, int) and t == SLOT_TILES - 1):
                            low(t + 1, 1 - p)
                        dve.wait_ge(silu_done, t + 1)
                        dve.wait_ge(up_done, t + 1)
                        dve.tensor_tensor(hid[p][:, :], ps_u[p][:, :], act_g[p][:, :], ALU.mult).then_inc(hid_ready, 1)
                        if not first:
                            keep(turn, j, t - 1)

                    low(0, 0)
                    turns(step, dve.Fori)
                    rest(SLOT_TILES - 1, 1)
                    keep(TURNS, 0, SLOT_TILES - 1)
                    for t in range(TILES):
                        if t % 4 == 0:
                            dve.wait_ge(got[t // 4], 16 * TOPK * (layer + 1))
                        dve.scalar_tensor_tensor(out=x_res[:, t, :], in0=y[:, 0, t, :], scalar=gates[:, 0, t:t + 1],
                                                 in1=x_res[:, t, :], op0=ALU.mult, op1=ALU.add).then_inc(first_added, 1)
                        if t % 4 == 3:
                            q = t // 4
                            four = slice(q * 4, (q + 1) * 4)
                            dve.wait_ge(first_added, layer * TILES + t + 1)
                            dve.wait_ge(weighed, layer * (TILES // 4) + q + 1)
                            dve.tensor_tensor(x_res[:, four, :], x_res[:, four, :], y[:, 1, four, :], ALU.add
                                              ).then_inc(second_added, 1)
                            if out is None:
                                dve.wait_ge(second_added, layer * (TILES // 4) + q + 1)
                                for u in range(q * 4, (q + 1) * 4):
                                    dve.bn_stats(stats[:, u, :], x_res[:, u, :])

                @block.gpsimd
                def _(pool):
                    pool.wait_ge(xn_written, 16 * (TILES // 4))
                    for t in range(RING):
                        gather(pool, t)
                    for t in range(SLOT_TILES + 2):
                        if t + RING < SLOT_TILES:
                            pool.wait_ge(t_done, t + 1)
                            gather(pool, t + RING)
                        if t >= 2:
                            pool.wait_ge(y_kept, t - 1)
                            pool.indirect_dma_start(
                                out=y_dram[:, :], out_offset=bass.IndirectOffsetOnAxis(ap=dst_row[:, t - 2:t - 1], axis=0),
                                in_=ys[(t - 2) % RING][:, :], in_offset=None).then_inc(out_landed[(t - 2) % RING], 16)

                @block.sync
                def _(sp):
                    for j in range(RING):
                        sp.wait_ge(out_landed[j], BEFORE + 16 * (SLOT_TILES // RING))
                    for q in range(TILES // 4):
                        for k in range(TOPK):
                            rows = y_dram[k * TOKENS + q * 4 * P:k * TOKENS + (q + 1) * 4 * P, :]
                            sp.dma_start(y[:, k, q * 4:(q + 1) * 4, :], rows.rearrange("(t p) d -> p t d", p=P)
                                         ).then_inc(got[q], 16)
                    if out is not None:
                        for q in range(TILES // 4):
                            sp.wait_ge(second_added, layer * (TILES // 4) + q + 1)
                            sp.dma_start(out[q * 4 * P:(q + 1) * 4 * P, :].rearrange("(t p) d -> p t d", p=P),
                                         x_res[:, q * 4:(q + 1) * 4, :]).then_inc(stored, 16)
                        sp.wait_ge(stored, 16 * (TILES // 4))


def hybrid_kernel(nc, ins, out):
    with ExitStack() as ctx:
        def sb(name, shape, dt):
            return ctx.enter_context(nc.sbuf_tensor(name, shape, dt))

        def sem(name):
            return ctx.enter_context(nc.semaphore(name))

        x_res = sb("x_res", [P, TILES, P], F32)
        consts = sb("consts", [P, CONST_COLS], F32)
        mean_var = sb("mean_var", [P, TILES, 2], F32)
        stats = sb("stats", [P, TILES, 6], F32)
        rstd = sb("rstd", [P, TILES], F32)
        ones_bf, below_bf, ident_bf, causal_bf = (sb(n, [P, P], BF16) for n in ("ones_bf", "below_bf", "ident_bf", "causal_bf"))
        gate_w = [sb(f"gate_{n}", [P, EXPERTS, FF], F32R) for n in ("hi", "lo")]
        up_w = [sb(f"up_{n}", [P, EXPERTS, FF], F32R) for n in ("hi", "lo")]
        down_w = sb("down_w", [P, EXPERTS, FF], F32)
        router_w = sb("router_w", [P, EXPERTS], F32)
        router_b = sb("router_b", [P, EXPERTS], F32)
        xn_dram = nc.dram_tensor("xn_dram", (TOKENS, D), F32, kind="Internal").ap()
        y_dram = nc.dram_tensor("y_dram", (TOPK * TOKENS + SLOT_TILES * P, D), F32, kind="Internal").ap()

        def cst(name):
            return consts[:, CONST[name][0]:CONST[name][1]]

        ident = cst("ident")

        small, big, consts_in = sem("small"), sem("big"), sem("consts_in")

        def first_loads(sp, to_cast):
            sp.dma_start(consts[:, :], ins["consts"]).then_inc(consts_in, 16)
            for dst, src in ((x_res[:, :, :], ins["x"].rearrange("(t p) d -> p t d", p=P)),
                             (to_cast[:, :, :], ins["cast"]), (router_w[:, :], ins["router_w"]),
                             (router_b[:, :], ins["router_b"])):
                sp.dma_start(dst, src).then_inc(small, 16)

        def casts(dve, to_cast):
            dve.wait_ge(consts_in, 16)
            dve.wait_ge(small, SMALL_LOADS * 16)
            for dst, src in ((ones_bf, cst("ones")), (ident_bf, ident), (below_bf, to_cast[:, 0, :]), (causal_bf, to_cast[:, 1, :])):
                dve.tensor_copy(dst[:, :], src)

        rings = ([sem(f"in_landed{j}") for j in range(RING)], [sem(f"out_landed{j}") for j in range(RING)],
                 [sem(f"got{q}") for q in range(TILES // 4)], sem("first_added"), sem("weighed"), sem("second_added"))
        moe = (x_res, mean_var, rstd, stats, cst, ident, ones_bf[:, :], below_bf[:, :], gate_w, up_w, down_w, router_w,
               router_b, ins["moe_consts"], xn_dram, y_dram, rings)
        attn = (x_res, mean_var, rstd, stats, cst, ident, ident_bf[:, :], causal_bf[:, :])
        with ExitStack() as causal_ctx:
            ready = CausalWeights(nc, causal_ctx, ctx, {k[2:]: v for k, v in ins.items() if k.startswith("c_")})
            attention(nc, ctx, False, *attn, {k[2:]: v for k, v in ins.items() if k.startswith("a_")},
                      (gate_w, up_w, big, (ins["gate_w"], ins["up_w"], ins["down_w"]), down_w), ready.load,
                      first=(first_loads, casts, consts_in))
            ready.make_room()
            experts(nc, ctx, 0, *moe, ready)
            attention(nc, ctx, True, *attn, None, ready=ready)
        experts(nc, ctx, 1, *moe, out=out, stored=sem("stored"))


def constants():
    import numpy as np
    c, m = np.zeros((P, CONST_COLS), np.float32), np.zeros((P, MOE_COLS), np.float32)

    def put(array, where, name, value):
        array[:, where[name][0]:where[name][1]] = value

    i = np.arange(P)
    put(c, CONST, "ident", np.eye(P))
    put(c, CONST, "ones", 1.0)
    put(c, CONST, "head", i[:, None] - 3 * QUAD == np.arange(HEADS)[None, :])
    put(c, CONST, "group", (i[:, None] % QUAD) // DH == np.arange(GROUPS)[None, :])
    put(m, MOE_CONST, "rank", EXPERTS - np.arange(EXPERTS))
    put(m, MOE_CONST, "full", P * np.arange(TILES))
    e = np.arange(EXPERTS)
    put(m, MOE_CONST, "upto", (e[None, :] <= e[:, None]).astype(np.float32).reshape(1, -1))
    put(m, MOE_CONST, "tile_no", np.arange(SLOT_TILES))
    put(m, MOE_CONST, "row_no", i)
    put(m, MOE_CONST, "digit", np.tile(EXPERTS ** np.arange(TURN), SLOT_TILES // TURN))
    put(m, MOE_CONST, "part_no", i[:, None])
    put(m, MOE_CONST, "pair_no", 1 + np.arange(TOPK * TILES))
    put(m, MOE_CONST, "pad_row", P + TOPK * TOKENS + P * np.arange(SLOT_TILES)[None, :] + i[:, None])
    below = i[:, None] < i[None, :]
    causal = np.where(i[None, :] <= i[:, None], 0.0, MASKED)
    return c, m, np.stack([below, causal], 1).astype(np.float32)


def kernel(**inputs):
    import numpy as np
    import concourse.bacc as bacc
    from concourse.bass_utils import run_bass_kernel_spmd

    a = {k: np.asarray(v) for k, v in inputs.items()}
    wide = lambda v: np.ascontiguousarray(np.broadcast_to(v[None, :], (P, v.shape[0])))
    qkv, qkv_b = a["L0_attn_a_qkv_weight"], a["L0_attn_a_qkv_bias"]

    def groups(w):
        w = w.reshape(GROUPS, 1, QUAD, -1)
        return np.broadcast_to(w, (GROUPS, 3, QUAD, w.shape[-1])).reshape(GROUPS * 3 * QUAD, -1)

    bqk = np.zeros((P, 2 * GROUPS), np.float32)
    bqk[0:3 * QUAD] = np.concatenate([groups(qkv_b[0:D, None]), groups(qkv_b[D:2 * D, None])]).reshape(2 * GROUPS, 3 * QUAD).T
    kqv, kqv_b = a["L0_attn_b_Wkqv"], a["L0_attn_b_bkqv"]
    consts, moe_consts, cast = constants()
    arrays = {
        "consts": consts, "cast": cast, "moe_consts": moe_consts,
        "x": a["L0_attn_a_input_tensor"].reshape(TILES * P, D),
        "router_w": a["L0_ffn_router_w"].T,
        "router_b": wide(a["L0_ffn_router_b"]),
        "gate_w": a["L0_ffn_gate_w"].transpose(2, 0, 1).reshape(P, -1),
        "up_w": a["L0_ffn_up_w"].transpose(2, 0, 1).reshape(P, -1),
        "down_w": a["L0_ffn_down_w"].transpose(2, 0, 1).reshape(FCH, P, EXPERTS, P).transpose(1, 2, 0, 3).reshape(P, EXPERTS, FF),
        "a_wqk": np.concatenate([groups(qkv[0:D]), groups(qkv[D:2 * D])]).T,
        "a_bqk": bqk,
        "a_wv": qkv[2 * D:].T, "a_bv": wide(qkv_b[2 * D:]),
        "a_wo": a["L0_attn_a_out_weight"].T, "a_bo": wide(a["L0_attn_a_out_bias"]),
        "c_wkT": kqv[:, :, 0:D].transpose(2, 0, 1), "c_wqT": kqv[:, :, D:2 * D].transpose(2, 0, 1),
        "c_bk": kqv_b[:, 0:D].T, "c_bq": kqv_b[:, D:2 * D].T,
        "c_wv": kqv[:, :, 2 * D:].transpose(1, 0, 2).reshape(D, HEADS * DH), "c_bv": wide(kqv_b[:, 2 * D:].reshape(-1)),
        "c_wo": a["L0_attn_b_Wp"], "c_bo": wide(a["L0_attn_b_bp"]),
    }
    nc = bacc.Bacc("TRN2", target_bir_lowering=False, num_devices=1)
    arrays = {k: np.ascontiguousarray(v) for k, v in arrays.items()}
    ins = {k: nc.dram_tensor(f"in_{k}", v.shape, mybir.dt.from_np(v.dtype), kind="ExternalInput").ap()
           for k, v in arrays.items()}
    out = nc.dram_tensor("out_x", (TILES * P, D), F32, kind="ExternalOutput").ap()
    hybrid_kernel(nc, ins, out)
    r = run_bass_kernel_spmd(nc, [{f"in_{k}": v for k, v in arrays.items()}], core_ids=[0])
    return np.asarray(r.results[0]["out_x"]).reshape(BATCH, SEQ, D)
```
